# Optimizing a Trainium2 kernel written in Bass

```python
import numpy as np
import jax
import jax.numpy as jnp

def _softmax(x, axis=-1):
    return jax.nn.softmax(x, axis=axis)

def _gelu(x):
    return jax.nn.gelu(x, approximate=True)

def _silu(x):
    return jax.nn.silu(x)

def _sigmoid(x):
    return jax.nn.sigmoid(x)

def _layernorm(x, axis=-1, eps=1e-05):
    m = jnp.mean(x, axis=axis, keepdims=True)
    v = jnp.var(x, axis=axis, keepdims=True)
    return (x - m) / jnp.sqrt(v + eps)

def _scatter_add(tgt, idx, src, axis=0):
    return tgt.at[idx].add(src)

def _segment_sum(src, seg, n):
    return jax.ops.segment_sum(src, seg, n)
kernel_name = 'mk_gnn_resnorm_d2_gnn_r8_f2879c'

def setup_inputs(seed: int=0):
    np.random.seed(seed)
    _w = jnp.asarray

    def _rec_inputs():
        import jax
        import jax.numpy as jnp
        _gk = jax.random.key(seed)
        x = -0.0003713 + 1 * jax.random.normal(jax.random.fold_in(_gk, 1), (12500, 128), jnp.float32)
        _s = jax.random.randint(jax.random.fold_in(_gk, 2), (200000,), 0, 12500, jnp.int32)
        _d = jax.random.randint(jax.random.fold_in(_gk, 3), (200000,), 0, 12500, jnp.int32)
        _loop = jnp.arange(12500, dtype=jnp.int32)
        src = jnp.concatenate([_s, _d, _loop])
        dst = jnp.concatenate([_d, _s, _loop])
        _o = jnp.argsort(dst, stable=True)
        src = src[_o]
        dst = dst[_o]
        edge_attr_32 = 0.000189758 + 1.00013 * jax.random.normal(jax.random.fold_in(_gk, 11), (412500, 32), jnp.float32)
        return (x, src, dst, edge_attr_32)
    x, src, dst, edge_attr_32 = _rec_inputs()

    def _L0_gnn_setup():
        import jax, jax.numpy as jnp
        import numpy as np
        N_NODES = 12500
        N_EDGES = 200000
        IN_DIM = 128
        OUT_DIM = 128
        EDGE_DIM = 32
        EPS = 1e-05

        def _layernorm(h, gamma, beta):
            mu = jnp.mean(h, axis=-1, keepdims=True)
            var = jnp.var(h, axis=-1, keepdims=True)
            return (h - mu) * jax.lax.rsqrt(var + EPS) * gamma + beta
        key = jax.random.key(seed)
        ks = jax.random.split(key, 10)
        hid = OUT_DIM * 2
        x = jax.random.normal(ks[0], (N_NODES, IN_DIM), dtype=jnp.float32)
        edge_index = jax.random.randint(ks[1], (2, N_EDGES), 0, N_NODES, dtype=jnp.int64)
        edge_attr = jax.random.normal(ks[2], (N_EDGES, EDGE_DIM), dtype=jnp.float32)
        W1 = jax.random.normal(ks[3], (IN_DIM + EDGE_DIM, hid), dtype=jnp.float32) / np.sqrt(IN_DIM + EDGE_DIM)
        b1 = jnp.zeros((hid,), jnp.float32)
        g1 = jnp.ones((hid,), jnp.float32)
        be1 = jnp.zeros((hid,), jnp.float32)
        W2 = jax.random.normal(ks[4], (hid, OUT_DIM), dtype=jnp.float32) / np.sqrt(hid)
        b2 = jnp.zeros((OUT_DIM,), jnp.float32)
        Wu = jax.random.normal(ks[5], (IN_DIM + OUT_DIM, OUT_DIM), dtype=jnp.float32) / np.sqrt(IN_DIM + OUT_DIM)
        bu = jnp.zeros((OUT_DIM,), jnp.float32)
        gu = jnp.ones((OUT_DIM,), jnp.float32)
        beu = jnp.zeros((OUT_DIM,), jnp.float32)
        return {'x': x, 'edge_index': edge_index, 'edge_attr': edge_attr, 'W1': W1, 'b1': b1, 'g1': g1, 'be1': be1, 'W2': W2, 'b2': b2, 'Wu': Wu, 'bu': bu, 'gu': gu, 'beu': beu}
    _L0_gnn_all = _L0_gnn_setup()
    _L0_gnn_in = {k: v for k, v in _L0_gnn_all.items() if k in ('W1', 'b1', 'g1', 'be1', 'W2', 'b2', 'Wu', 'bu', 'gu', 'beu')}
    del _L0_gnn_all

    def _L1_gnn_setup():
        import jax, jax.numpy as jnp
        import numpy as np
        EPS = 1e-05

        def _gcn_norm(edge_index, num_nodes):
            src = jnp.concatenate([edge_index[0], jnp.arange(num_nodes)])
            dst = jnp.concatenate([edge_index[1], jnp.arange(num_nodes)])
            deg = jax.ops.segment_sum(jnp.ones_like(dst, dtype=jnp.float32), dst, num_segments=num_nodes)
            dinv = jnp.where(deg > 0, jax.lax.rsqrt(deg), 0.0)
            norm = dinv[src] * dinv[dst]
            return (src, dst, norm)

        def _gcn_conv(x, src, dst, norm, W, b, num_nodes):
            h = x @ W
            msg = h[src] * norm[:, None]
            out = jax.ops.segment_sum(msg, dst, num_segments=num_nodes)
            return out + b

        def _batchnorm(x, gamma, beta):
            m = jnp.mean(x, axis=0)
            v = jnp.var(x, axis=0)
            return (x - m) * jax.lax.rsqrt(v + EPS) * gamma + beta
        key = jax.random.key(seed)
        ks = jax.random.split(key, 4)
        N, E, D = (6250, 100000, 128)
        x = jax.random.normal(ks[0], (N, D), dtype=jnp.float32)
        edge_index = jax.random.randint(ks[1], (2, E), 0, N, dtype=jnp.int64)
        scale = 1.0 / np.sqrt(D)
        W0 = jax.random.normal(ks[2], (D, D), dtype=jnp.float32) * scale
        W1 = jax.random.normal(ks[3], (D, D), dtype=jnp.float32) * scale
        zeros = jnp.zeros((D,), jnp.float32)
        ones = jnp.ones((D,), jnp.float32)
        return {'x': x, 'edge_index': edge_index, 'W0': W0, 'b0': zeros, 'g0': ones, 'be0': zeros, 'W1': W1, 'b1': zeros, 'g1': ones, 'be1': zeros}
    _L1_gnn_all = _L1_gnn_setup()
    _L1_gnn_in = {k: v for k, v in _L1_gnn_all.items() if k in ('W0', 'b0', 'g0', 'be0', 'W1', 'b1', 'g1', 'be1')}
    del _L1_gnn_all
    return {'x': x, 'src': src, 'dst': dst, 'edge_attr_32': edge_attr_32, 'L0_gnn_W1': _L0_gnn_in['W1'], 'L0_gnn_b1': _L0_gnn_in['b1'], 'L0_gnn_g1': _L0_gnn_in['g1'], 'L0_gnn_be1': _L0_gnn_in['be1'], 'L0_gnn_W2': _L0_gnn_in['W2'], 'L0_gnn_b2': _L0_gnn_in['b2'], 'L0_gnn_Wu': _L0_gnn_in['Wu'], 'L0_gnn_bu': _L0_gnn_in['bu'], 'L0_gnn_gu': _L0_gnn_in['gu'], 'L0_gnn_beu': _L0_gnn_in['beu'], 'L1_gnn_W0': _L1_gnn_in['W0'], 'L1_gnn_b0': _L1_gnn_in['b0'], 'L1_gnn_g0': _L1_gnn_in['g0'], 'L1_gnn_be0': _L1_gnn_in['be0'], 'L1_gnn_W1': _L1_gnn_in['W1'], 'L1_gnn_b1': _L1_gnn_in['b1'], 'L1_gnn_g1': _L1_gnn_in['g1'], 'L1_gnn_be1': _L1_gnn_in['be1']}

def reference(x, src, dst, edge_attr_32, L0_gnn_W1, L0_gnn_b1, L0_gnn_g1, L0_gnn_be1, L0_gnn_W2, L0_gnn_b2, L0_gnn_Wu, L0_gnn_bu, L0_gnn_gu, L0_gnn_beu, L1_gnn_W0, L1_gnn_b0, L1_gnn_g0, L1_gnn_be0, L1_gnn_W1, L1_gnn_b1, L1_gnn_g1, L1_gnn_be1):
    import jax
    import jax.numpy as jnp

    def _L0_gnn_ref(x, edge_index, edge_attr, W1, b1, g1, be1, W2, b2, Wu, bu, gu, beu):
        import jax, jax.numpy as jnp
        import numpy as np
        N_NODES = 12500
        N_EDGES = 200000
        IN_DIM = 128
        OUT_DIM = 128
        EDGE_DIM = 32
        EPS = 1e-05

        def _layernorm(h, gamma, beta):
            mu = jnp.mean(h, axis=-1, keepdims=True)
            var = jnp.var(h, axis=-1, keepdims=True)
            return (h - mu) * jax.lax.rsqrt(var + EPS) * gamma + beta
        row, col = (edge_index[0], edge_index[1])
        msg_in = jnp.concatenate([x[row], edge_attr], axis=-1)
        h = msg_in @ W1 + b1
        h = jax.nn.gelu(_layernorm(h, g1, be1), approximate=False)
        msg = h @ W2 + b2
        agg = jax.ops.segment_sum(msg, col, num_segments=x.shape[0])
        u = jnp.concatenate([x, agg], axis=-1) @ Wu + bu
        u = jax.nn.gelu(_layernorm(u, gu, beu), approximate=False)
        return u + x

    def _L1_gnn_ref(x, edge_index, W0, b0, g0, be0, W1, b1, g1, be1):
        import jax, jax.numpy as jnp
        import numpy as np
        EPS = 1e-05

        def _gcn_norm(edge_index, num_nodes):
            src = jnp.concatenate([edge_index[0], jnp.arange(num_nodes)])
            dst = jnp.concatenate([edge_index[1], jnp.arange(num_nodes)])
            deg = jax.ops.segment_sum(jnp.ones_like(dst, dtype=jnp.float32), dst, num_segments=num_nodes)
            dinv = jnp.where(deg > 0, jax.lax.rsqrt(deg), 0.0)
            norm = dinv[src] * dinv[dst]
            return (src, dst, norm)

        def _gcn_conv(x, src, dst, norm, W, b, num_nodes):
            h = x @ W
            msg = h[src] * norm[:, None]
            out = jax.ops.segment_sum(msg, dst, num_segments=num_nodes)
            return out + b

        def _batchnorm(x, gamma, beta):
            m = jnp.mean(x, axis=0)
            v = jnp.var(x, axis=0)
            return (x - m) * jax.lax.rsqrt(v + EPS) * gamma + beta
        N = x.shape[0]
        src, dst, norm = _gcn_norm(edge_index, N)
        residual = x
        h = x
        for W, b, g, be in ((W0, b0, g0, be0), (W1, b1, g1, be1)):
            h = _gcn_conv(h, src, dst, norm, W, b, N)
            h = _batchnorm(h, g, be)
            h = jax.nn.relu(h)
        return h + residual
    edge_index = jnp.stack([src, dst])
    x = _layernorm(x + _L0_gnn_ref(x, edge_index, edge_attr_32, L0_gnn_W1, L0_gnn_b1, L0_gnn_g1, L0_gnn_be1, L0_gnn_W2, L0_gnn_b2, L0_gnn_Wu, L0_gnn_bu, L0_gnn_gu, L0_gnn_beu), axis=-1)
    x = _layernorm(x + _L1_gnn_ref(x, edge_index, L1_gnn_W0, L1_gnn_b0, L1_gnn_g0, L1_gnn_be0, L1_gnn_W1, L1_gnn_b1, L1_gnn_g1, L1_gnn_be1), axis=-1)
    return x

_drawn_inputs = setup_inputs


def setup_inputs(seed=0):
    import zlib

    import numpy as np

    out = dict(_drawn_inputs(seed))
    spreads = {'L0_gnn_b1': (0.0, 0.1),
     'L0_gnn_g1': (1.0, 0.2),
     'L0_gnn_be1': (0.0, 0.1),
     'L0_gnn_b2': (0.0, 0.1),
     'L0_gnn_bu': (0.0, 0.8),
     'L0_gnn_gu': (1.0, 0.2),
     'L0_gnn_beu': (0.0, 0.27),
     'L1_gnn_b0': (0.0, 2.0),
     'L1_gnn_g0': (1.0, 0.2),
     'L1_gnn_be0': (0.0, 0.303),
     'L1_gnn_b1': (0.0, 2.0),
     'L1_gnn_g1': (1.0, 0.2),
     'L1_gnn_be1': (0.0, 0.1)}
    factors = {}
    for name, (base, spread) in spreads.items():
        noise = np.random.default_rng([zlib.crc32(name.encode()), seed]).standard_normal(out[name].shape)
        drawn = base * np.exp(spread * noise) if base else spread * noise
        out[name] = jnp.asarray(drawn.astype(out[name].dtype))
    for name, factor in factors.items():
        out[name] = (out[name] * factor).astype(out[name].dtype)
    return out
```

```python
import concourse.bass as bass
from concourse import mybir
from contextlib import ExitStack

F32 = mybir.dt.float32
I32 = mybir.dt.int32
ALU = mybir.AluOpType
ACT = mybir.ActivationFunctionType
AX = mybir.AxisListType

P = 128
TG = 8
GE = TG * P
WIN = 64
WIN_SHIFT = 6
RING = 4
CHUNK = 2
NC_CH = TG // CHUNK
D = 128
ED = 32
H = 256
TV = H + ED
TR = 320
HC = H + 1
QK = P // ED
EPS = 1e-5
NB = 7


def wait_for(engine, sem, count):
    if isinstance(count, int) and count <= 0:
        return
    engine.wait_ge(sem, count)


def carry(engine, sem):
    engine.sem_inc(sem, 1)


def ring_steps(engine, n, step):
    for k in range(RING):
        step(k, 0, k)
    with engine.Fori(1, n // RING) as i:
        for k in range(RING):
            step(i * RING + k, i, k)


def pair_steps(engine, n, step):
    for k in range(2):
        step(k, 0, k)
    with engine.Fori(1, n // 2) as i:
        for k in range(2):
            step(i * 2 + k, i, k)


class Shape:
    def __init__(self, n_nodes, n_groups):
        self.N = n_nodes
        self.NT = -(-n_nodes // P)
        self.NP = self.NT * P
        self.G = n_groups
        self.GP = n_groups // RING
        self.ACC = self.NP + WIN
        self.BN = max(d for d in range(1, 513) if n_nodes % d == 0)


def semaphores(nc, m, prefix, names):
    for n in names:
        if f"{prefix}_{n}" not in m["sems"]:
            m["sems"][f"{prefix}_{n}"] = nc.alloc_semaphore(name=f"{prefix}_{n}")
    return [m["sems"][f"{prefix}_{n}"] for n in names]


def clear(nc, sems):
    for s in sems:
        nc.sync.sem_clear(s)
    nc.all_engine_barrier()


def clear_all(nc, m, sems):
    nc.gpsimd.drain()
    gathered = [s for slot in m["gathered"] for s in slot]
    nums = [s.num for s in gathered]
    assert nums == list(range(nums[0], nums[-1] + 1))
    nc.gpsimd.dma_reset(range(nums[0], nums[-1] + 1))
    nc.all_engine_barrier()
    clear(nc, [*sems, *gathered])


def prepare(nc, sh, a, m):
    with ExitStack() as ctx:
        def sb(name, shape, dt=F32):
            return ctx.enter_context(nc.sbuf_tensor(name, shape, dt))

        w1x = sb("w1x", [P, H])
        w1e = sb("w1e", [P, H])
        b2b = sb("b2b", [P, D])
        w2 = sb("w2", [P, 2, D])
        mean = sb("prep_mean", [P, 3])
        wt = sb("prep_transposed", [P, 9, P])
        dst_rows = sb("dst_rows", [sh.GP, RING, GE], I32)
        dst_cols = sb("dst_cols", [P, sh.G, TG], I32)
        low = sb("group_low", [sh.GP, RING], I32)
        high = sb("group_high", [sh.GP, RING], I32)
        span = sb("group_span", [sh.GP, RING], I32)
        shifted = sb("group_shifted", [sh.GP, RING], I32)
        need = sb("group_rounds", [sh.GP, RING], I32)
        low_b = sb("low_b", [P, sh.G], I32)
        need_row = sb("need_row", [1, sh.G], I32)
        iota_i = sb("iota_i", [P, WIN], I32)
        zeros = sb("zeros", [P, 4 * HC])
        turned = ctx.enter_context(nc.psum_tensor("prep_turned", [P, 12, P], F32))
        prods = ctx.enter_context(nc.psum_tensor("prep_prods", [P, 512], F32))
        (loaded_w, loaded_dst, zero_set, zeroed, cleared, made, centred, turned_ok, copied, prods_ok, folded,
         range_ok, chain, range_out, range_in) = semaphores(nc, m, "prep", [
            "loaded_w", "loaded_dst", "zero_set", "zeroed", "cleared", "made", "centred", "turned", "copied", "prods",
            "folded", "range", "chain", "range_out", "range_in"])
        block = ctx.enter_context(nc.Block())
        n_w = 1 + QK + 7 + 2

        @block.sync
        def _(sp):
            sp.dma_start(dst_rows[:, :, :], a["dst_rows"]).then_inc(loaded_dst, 16)
            sp.dma_start(dst_cols[:, :, :], a["dst_cols"]).then_inc(loaded_dst, 16)
            sp.dma_start(w1x[:, :], a["W1"][0:D, :]).then_inc(loaded_w, 16)
            for q in range(QK):
                sp.dma_start(w1e[q * ED:(q + 1) * ED, :], a["W1"][D:D + ED, :]).then_inc(loaded_w, 16)
            for dst, src in ((m["b1b"], a["b1"]), (m["g1b"], a["g1"]), (m["be1b"], a["be1"]), (b2b, a["b2"]),
                             (m["bub"], a["bu"]), (m["gub"], a["gu"]), (m["beub"], a["beu"])):
                sp.dma_start(dst[:, :], src.partition_broadcast(P)).then_inc(loaded_w, 16)
            sp.dma_start(w2[:, :, :], a["W2"].rearrange("(j p) d -> p j d", p=P)).then_inc(loaded_w, 16)
            sp.dma_start(m["wu"][:, :, :], a["Wu"].rearrange("(j p) d -> p j d", p=P)).then_inc(loaded_w, 16)
            for j in range(2):
                sp.dma_start(m["wc"][:, j, :], a["Wc"][j]).then_inc(m["loaded_conv"], 16)
                for r in range(3):
                    sp.dma_start(m["colc"][:, j, r:r + 1], a["colc"][j][r].rearrange("(p o) -> p o", o=1)).then_inc(
                        m["loaded_conv"], 16)
            sp.wait_ge(range_ok, 2)
            sp.dma_start(m["low_dram"].rearrange("(p j) -> p j", j=RING), low[:, :]).then_inc(range_out, 16)
            sp.dma_start(m["need_dram"].rearrange("(p j) -> p j", j=RING), need[:, :]).then_inc(range_out, 16)
            sp.wait_ge(range_out, 32)
            sp.dma_start(m["low_first"][:, :], m["low_dram"].rearrange("(o g) -> o g", o=1)).then_inc(range_in, 16)
            sp.dma_start(need_row[:, :], m["need_dram"].rearrange("(o g) -> o g", o=1)).then_inc(range_in, 16)
            sp.dma_start(low_b[:, :], m["low_dram"].partition_broadcast(P)).then_inc(range_in, 16)
            sp.wait_ge(zero_set, 1)
            for acc in m["acc"][0]:
                rows = sh.NP // P
                for r in range(0, rows, 4):
                    k = min(4, rows - r)
                    sp.dma_start(acc[r * P:(r + k) * P, :].rearrange("(p k) c -> p (k c)", p=P),
                                 zeros[:, 0:k * HC]).then_inc(zeroed, 16)
                sp.dma_start(acc[sh.NP:sh.ACC, :], zeros[0:WIN, 0:HC]).then_inc(zeroed, 16)
            sp.wait_ge(zeroed, 2 * 16 * (-(-(sh.NP // P) // 4) + 1))

        @block.gpsimd
        def _(pool):
            nc.gpsimd.memset(zeros[:, :], 0.0).then_inc(zero_set, 1)
            nc.gpsimd.memset(m["ident"][:, :], 0.0).then_inc(cleared, 1)
            pool.wait_ge(cleared, 1)
            nc.gpsimd.affine_select(out=m["ident"][:, :], in_=m["ident"][:, :], compare_op=ALU.not_equal, fill=1.0,
                                    base=0, pattern=[[-1, P]], channel_multiplier=1).then_inc(made, 1)
            nc.gpsimd.iota(iota_i[:, :], pattern=[[1, WIN]], base=0, channel_multiplier=0).then_inc(made, 1)
            nc.gpsimd.memset(m["wm"][:, :, :], 0.0).then_inc(made, 1)
            nc.gpsimd.memset(m["expo"][:, :], -0.5).then_inc(made, 1)

        @block.vector
        def _(dve):
            count = [0]

            def link(ins):
                count[0] += 1
                ins.then_inc(chain, 1)
                dve.wait_ge(chain, count[0])

            dve.wait_ge(loaded_dst, 32)
            nc.vector.tensor_reduce(high[:, :], dst_rows[:, :, :], AX.X, ALU.max).then_inc(chain, 1)
            count[0] += 1
            nc.vector.tensor_reduce(low[:, :], dst_rows[:, :, :], AX.X, ALU.min).then_inc(range_ok, 1)
            dve.wait_ge(range_ok, 1)
            dve.wait_ge(chain, count[0])
            link(nc.vector.tensor_tensor(span[:, :], high[:, :], low[:, :], ALU.subtract))
            link(nc.vector.tensor_scalar(shifted[:, :], span[:, :], WIN_SHIFT, None, ALU.logical_shift_right))
            nc.vector.tensor_scalar(need[:, :], shifted[:, :], 1, None, ALU.add).then_inc(range_ok, 1)
            dve.wait_ge(made, 4)
            link(nc.vector.tensor_copy(m["iota"][:, :], iota_i[:, :]))
            dve.wait_ge(loaded_w, 16 * n_w)
            for j, t in enumerate((w1x, w1e, m["b1b"])):
                link(nc.vector.tensor_reduce(mean[:, j:j + 1], t[:, :], AX.X, ALU.add))
            link(nc.vector.tensor_scalar(mean[:, :], mean[:, :], -1.0 / H, None, ALU.mult))
            for j, (t, o) in enumerate(((w1x, m["w1c"]), (w1e, w1e), (m["b1b"], m["b1b"]))):
                nc.vector.tensor_scalar(o[:, :], t[:, :], mean[:, j:j + 1], None, ALU.add).then_inc(centred, 1)
            dve.wait_ge(turned_ok, 1)
            for r in range(3):
                nc.vector.tensor_copy(wt[:, 3 * r:3 * r + 3, :], turned[:, 4 * r:4 * r + 3, :]).then_inc(copied, 1)
            dve.wait_ge(centred, 3)
            link(nc.vector.tensor_tensor(m["wtab"][:, 0:H], m["w1c"][:, :], m["g1b"][:, :], ALU.mult))
            link(nc.vector.tensor_tensor(m["btab"][:, 0:H], m["b1b"][:, :], m["g1b"][:, :], ALU.mult))
            for q in range(QK):
                r = slice(q * ED, (q + 1) * ED)
                link(nc.vector.tensor_tensor(m["wm"][r, q, 0:H], w1e[r, :], m["g1b"][r, :], ALU.mult))
            dve.wait_ge(prods_ok, 1)
            nc.vector.tensor_scalar(m["wtab"][:, H:TV], prods[:, 0:ED], 2.0 / H, None, ALU.mult).then_inc(folded, 1)
            nc.vector.tensor_scalar(m["btab"][:, H:TV], prods[:, ED:2 * ED], 2.0 / H, None, ALU.mult).then_inc(folded, 1)
            for q in range(QK):
                r = slice(q * ED, (q + 1) * ED)
                nc.vector.tensor_scalar(m["wm"][r, q, H:TV], prods[r, 2 * ED:3 * ED], 1.0 / H, None,
                                        ALU.mult).then_inc(folded, 1)
            nc.vector.tensor_copy(m["w2u"][:, :, :], prods[:, D:4 * D].rearrange("p (j d) -> p j d", j=3)).then_inc(
                folded, 1)
            dve.wait_ge(range_in, 48)
            link(nc.vector.tensor_reduce(m["rounds"][:, :], need_row[:, :], AX.X, ALU.max))
            link(nc.vector.tensor_tensor(m["place_first"][:, :, :], dst_cols[:, :, :],
                                         low_b[:, :, None].broadcast_to([P, sh.G, TG]), ALU.subtract))

        @block.tensor
        def _(pe):
            pe.wait_ge(centred, 3)
            pe.wait_ge(made, 4)
            parts = [m["w1c"][:, 0:P], m["w1c"][:, P:H], w1e[:, 0:P], w1e[:, P:H], m["b1b"][:, 0:P], m["b1b"][:, P:H],
                     w2[:, 0, :], w2[:, 1, :], b2b[:, :]]
            for n, t in enumerate(parts):
                last = nc.tensor.matmul(turned[:, 4 * (n // 3) + n % 3, :], t, m["ident"][:, :], start=True, stop=True)
            last.then_inc(turned_ok, 1)
            pe.wait_ge(copied, 3)
            for n, left in ((0, 0), (1, 4), (2, 2)):
                for j in range(2):
                    nc.tensor.matmul(prods[:, n * ED:(n + 1) * ED], wt[:, left + j, :], wt[:, 2 + j, 0:ED],
                                     start=(j == 0), stop=(j == 1))
            for n in range(3):
                last = nc.tensor.matmul(prods[:, (n + 1) * D:(n + 2) * D], wt[:, 6 + n, :], m["wu"][:, 1, :],
                                        start=True, stop=True)
            last.then_inc(prods_ok, 1)


def node_table(nc, sh, a, m):
    with ExitStack() as ctx:
        def sb(name, shape, dt=F32):
            return ctx.enter_context(nc.sbuf_tensor(name, shape, dt))

        xt = sb("tab_xt", [D, 2, P])
        row = sb("tab_row", [P, 2, TR])
        pc = sb("tab_pc", [P, 2, H])
        ps_row = [ctx.enter_context(nc.psum_tensor(f"tab_ps_row{k}", [P, 512], F32)) for k in range(2)]
        ps_pc = [ctx.enter_context(nc.psum_tensor(f"tab_ps_pc{k}", [P, 512], F32)) for k in range(2)]
        x_in0, x_in1, multiplied, biased, squared, out0, out1, padded = semaphores(nc, m, "tab", [
            "x_in0", "x_in1", "multiplied", "biased", "squared", "row_out0", "row_out1", "padded"])
        x_in, row_out = [x_in0, x_in1], [out0, out1]
        block = ctx.enter_context(nc.Block())

        @block.sync
        def _(sp):
            def step(c, i, k):
                wait_for(sp, multiplied, c - 1)
                carry(sp, m["went"][2])
                sp.dma_start(xt[:, k, :], a["xt"][:, bass.ds(c * P, P)]).then_inc(x_in[k], 16)
            pair_steps(sp, sh.NT, step)

        @block.gpsimd
        def _(pool):
            nc.gpsimd.memset(row[:, :, TV + 1:TR], 0.0).then_inc(padded, 1)

        @block.tensor
        def _(pe):
            def step(c, i, k):
                pe.wait_ge(x_in[k], i * 16 + 16)
                wait_for(pe, biased, c - 1)
                nc.tensor.matmul(ps_row[k][:, 0:TV], xt[:, k, :], m["wtab"][:, :], start=True, stop=True)
                nc.tensor.matmul(ps_pc[k][:, 0:H], xt[:, k, :], m["w1c"][:, :], start=True, stop=True).then_inc(
                    multiplied, 1)
            pair_steps(pe, sh.NT, step)

        @block.vector
        def _(dve):
            def step(c, i, k):
                dve.wait_ge(multiplied, c + 1)
                wait_for(dve, row_out[k], i * 16)
                wait_for(dve, squared, c - 1)
                nc.vector.tensor_tensor(row[:, k, 0:TV], ps_row[k][:, 0:TV], m["btab"][:, :], ALU.add)
                nc.vector.tensor_tensor(pc[:, k, :], ps_pc[k][:, 0:H], m["b1b"][:, :], ALU.add).then_inc(biased, 1)
            pair_steps(dve, sh.NT, step)

        @block.scalar
        def _(act):
            act.wait_ge(padded, 1)

            def step(c, i, k):
                act.wait_ge(biased, c + 1)
                nc.scalar.activation(pc[:, k, :], pc[:, k, :], ACT.Square, scale=H ** -0.5,
                                     accum_out=row[:, k, TV:TV + 1]).then_inc(squared, 1)
                act.wait_ge(squared, c + 1)
                act.dma_start(m["table"][bass.ds(c * P, P), :], row[:, k, :]).then_inc(row_out[k], 16)
            pair_steps(act, sh.NT, step)
            for k in range(2):
                act.wait_ge(row_out[k], 16 * (sh.NT // 2))


def window_add(nc, ctx, sh, m, name, acc, width, summed, ps_sum, act_went):
    held = ctx.enter_context(nc.sbuf_tensor(f"{name}_window", [WIN, 2, width], F32))
    in0, in1, out0, out1, added = semaphores(nc, m, "win", ["win_in0", "win_in1", "win_out0", "win_out1", "win_added"])
    win_in, win_out = [in0, in1], [out0, out1]

    def store(act, s, k):
        act.wait_ge(added, s + 1)
        carry(act, act_went)
        low = nc.scalar.value_load(m["low"][0:1, bass.ds(s, 1)], min_val=0, max_val=sh.NP)
        act.dma_start(acc[k % 2][bass.ds(low, WIN), :], held[:, k % 2, :]).then_inc(win_out[k % 2], 16)

    def load(act, s, i, k):
        wait_for(act, win_out[k % 2], i * 32 + 16 * (k // 2))
        carry(act, act_went)
        low = nc.scalar.value_load(m["low"][0:1, bass.ds(s, 1)], min_val=0, max_val=sh.NP)
        act.dma_start(held[:, k % 2, :], acc[k % 2][bass.ds(low, WIN), :]).then_inc(win_in[k % 2], 16)

    def add(dve, s, i, k):
        dve.wait_ge(summed, s + 1)
        dve.wait_ge(win_in[k % 2], i * 32 + 16 * (k // 2) + 16)
        nc.vector.tensor_tensor(held[:, k % 2, :], held[:, k % 2, :], ps_sum[k % 2][0:WIN, 0:width],
                                ALU.add).then_inc(added, 1)

    def stored(act):
        for p in range(2):
            act.wait_ge(win_out[p], 16 * (sh.G // 2))

    return store, load, add, stored, added, [in0, in1, out0, out1, added]


def earlier(s, i, k, lag):
    return s - lag, (i if k >= lag else i - 1), (k - lag) % RING


def message_pass(nc, sh, a, m):
    with ExitStack() as ctx:
        def sb(name, shape, dt=F32):
            return ctx.enter_context(nc.sbuf_tensor(name, shape, dt))

        idx = sb("msg_idx", [P, RING * TG], I32)
        ea_t = sb("msg_ea_t", [P, RING, CHUNK, P])
        ea_n = sb("msg_ea_n", [P, RING, TG, ED])
        rows = sb("msg_rows", [P, RING, TG, TR])
        prod = sb("msg_prod", [P, TG, ED])
        dot = sb("msg_dot", [P, 2, TG])
        var = sb("msg_var", [P, 2, TG])
        rstd = sb("msg_rstd", [P, 2, TG])
        hid = sb("msg_hid", [P, 2, TG, HC])
        onehot = sb("msg_onehot", [P, 2, TG, WIN])
        ps_e = ctx.enter_context(nc.psum_tensor("msg_ps_e", [P, 2, CHUNK, 512], F32))
        ps_sum = [ctx.enter_context(nc.psum_tensor(f"msg_ps_sum{k}", [P, 512], F32)) for k in range(2)]
        edges_in = semaphores(nc, m, "msg", [f"edges_in{k}" for k in range(RING)])
        pool_went, act_went, sp_went = m["went"]
        gathered = m["gathered"]
        (ea_done, joined, stat, var_ok, rstd_ok, scaled, activated, placed, summed, ones_set) = own = semaphores(
            nc, m, "msg", ["ea_done", "joined", "stat", "var_ok", "rstd_ok", "scaled", "activated", "placed", "summed",
                             "ones_set"])
        store, load, add, stored, added, win_sems = window_add(nc, ctx, sh, m, "msg", m["acc"][0], HC, summed, ps_sum,
                                                               act_went)
        block = ctx.enter_context(nc.Block())

        @block.sync
        def _(sp):
            def step(s, i, k):
                wait_for(sp, var_ok, s - (RING - 1))
                carry(sp, m["went"][2])
                sp.dma_start(idx[:, k * TG:(k + 1) * TG],
                             a["src"][bass.ds(s * P, P), :]).then_inc(edges_in[k], 16)
                sp.dma_start(ea_t[:, k, :, :], a["ea_t"][bass.ds(s * P, P), :].rearrange("p (c e) -> p c e", c=CHUNK)
                             ).then_inc(edges_in[k], 16)
                sp.dma_start(ea_n[:, k, :, :], a["ea_n"][bass.ds(s * P, P), :].rearrange("p (t d) -> p t d", t=TG)
                             ).then_inc(edges_in[k], 16)
            ring_steps(sp, sh.G, step)

        @block.gpsimd
        def _(pool):
            nc.gpsimd.memset(hid[:, :, :, H:HC], 1.0).then_inc(ones_set, 1)

            def root(s, k):
                pool.wait_ge(var_ok, s + 1)
                wait_for(pool, scaled, s * NC_CH - NC_CH)
                nc.gpsimd.tensor_tensor(rstd[:, k % 2, :], var[:, k % 2, :], m["expo"][:, 0:TG],
                                        ALU.pow).then_inc(rstd_ok, 1)

            def step(s, i, k):
                pool.wait_ge(edges_in[k], i * 48 + 48)
                wait_for(pool, scaled, s * NC_CH - NC_CH * (RING - 1))
                carry(pool, pool_went)
                for t in range(TG):
                    nc.gpsimd.indirect_dma_start(
                        rows[:, k, t, :], None, m["table"],
                        bass.IndirectOffsetOnAxis(idx[:, k * TG + t:k * TG + t + 1], axis=0)).then_inc(gathered[k][t], 16)
                if not isinstance(s, int) or s >= 1:
                    root(s - 1, k - 1)
            ring_steps(pool, sh.G, step)
            root(sh.G - 1, RING - 1)

        @block.tensor
        def _(pe):
            def edge_part(s, i, k, chunks):
                for c in chunks:
                    wait_for(pe, joined, s * NC_CH + (c - 1))
                    for j in range(CHUNK):
                        t = c * CHUNK + j
                        last = nc.tensor.matmul(ps_e[:, c % 2, j, 0:TV], ea_t[:, k, t // QK, :], m["wm"][:, t % QK, :],
                                                start=True, stop=True)
                    last.then_inc(ea_done, 1)

            def segment_sum(s, k):
                pe.wait_ge(placed, s + 1)
                wait_for(pe, added, s - 1)
                for c in range(NC_CH):
                    pe.wait_ge(activated, s * NC_CH + (c + 1))
                    for t in range(c * CHUNK, (c + 1) * CHUNK):
                        last = nc.tensor.matmul(ps_sum[k % 2][0:WIN, 0:HC], onehot[:, k % 2, t, :], hid[:, k % 2, t, :],
                                                start=(t == 0), stop=(t == TG - 1))
                last.then_inc(summed, 1)

            def step(s, i, k):
                pe.wait_ge(edges_in[k], i * 48 + 48)
                edge_part(s, i, k, (0, 1))
                if not isinstance(s, int) or s >= 2:
                    segment_sum(s - 2, k - 2)
                edge_part(s, i, k, (2, 3))
            ring_steps(pe, sh.G, step)
            segment_sum(sh.G - 2, 0)
            segment_sum(sh.G - 1, 1)

        @block.vector
        def _(dve):
            def join(s, i, k):
                for c in range(NC_CH):
                    for t in range(c * CHUNK, (c + 1) * CHUNK):
                        dve.wait_ge(gathered[k][t], i * 16 + 16)
                    dve.wait_ge(ea_done, s * NC_CH + (c + 1))
                    r = rows[:, k, c * CHUNK:(c + 1) * CHUNK, 0:TV]
                    nc.vector.tensor_tensor(r, r, ps_e[:, c % 2, :, 0:TV], ALU.add).then_inc(joined, 1)

            def variance(s, i, k):
                dve.wait_ge(edges_in[k], i * 48 + 48)
                dve.wait_ge(joined, s * NC_CH + NC_CH)
                nc.vector.tensor_tensor(prod[:, :, :], rows[:, k, :, H:TV], ea_n[:, k, :, :], ALU.mult).then_inc(stat, 1)
                dve.wait_ge(stat, s * 3 + 1)
                nc.vector.tensor_reduce(dot[:, 0, :], prod[:, :, :], AX.X, ALU.add).then_inc(stat, 1)
                dve.wait_ge(stat, s * 3 + 2)
                nc.vector.tensor_tensor(dot[:, 1, :], dot[:, 0, :], rows[:, k, :, TV], ALU.add).then_inc(stat, 1)
                dve.wait_ge(stat, s * 3 + 3)
                wait_for(dve, rstd_ok, s - 1)
                nc.vector.tensor_scalar(var[:, k % 2, :], dot[:, 1, :], EPS, EPS, ALU.add, ALU.max).then_inc(var_ok, 1)

            def place(s, k):
                wait_for(dve, summed, s - 1)
                nc.vector.tensor_tensor(onehot[:, k % 2, :, :], m["iota"][:, None, :].broadcast_to([P, TG, WIN]),
                                        m["place"][:, bass.ds(s * TG, TG)][:, :, None].broadcast_to([P, TG, WIN]),
                                        ALU.is_equal).then_inc(placed, 1)

            def scale(s, k):
                dve.wait_ge(rstd_ok, s + 1)
                wait_for(dve, summed, s - 1)
                for t in range(TG):
                    last = nc.vector.scalar_tensor_tensor(
                        out=hid[:, k % 2, t, 0:H], in0=rows[:, k % RING, t, 0:H], scalar=rstd[:, k % 2, t:t + 1],
                        in1=m["be1b"][:, :], op0=ALU.mult, op1=ALU.add)
                    if t % CHUNK == CHUNK - 1:
                        last.then_inc(scaled, 1)

            def step(s, i, k):
                join(s, i, k)
                variance(s, i, k)
                if not isinstance(s, int) or s >= 2:
                    add(dve, *earlier(s, i, k, 2))
                place(s, k)
                if not isinstance(s, int) or s >= 1:
                    scale(s - 1, (k - 1) % RING)
            ring_steps(dve, sh.G, step)
            n = sh.G // RING
            add(dve, sh.G - 2, n - 1, 2)
            scale(sh.G - 1, 3)
            add(dve, sh.G - 1, n - 1, 3)

        @block.scalar
        def _(act):
            def gelu(s, k):
                for c in range(NC_CH):
                    act.wait_ge(scaled, s * NC_CH + (c + 1))
                    h = hid[:, k % 2, c * CHUNK:(c + 1) * CHUNK, 0:H]
                    nc.scalar.activation(h, h, ACT.Gelu).then_inc(activated, 1)

            act.wait_ge(ones_set, 1)

            def step(s, i, k):
                if not isinstance(s, int) or s >= 2:
                    store(act, s - 2, k)
                if not isinstance(s, int) or s >= 1:
                    gelu(s - 1, (k - 1) % 2)
                load(act, s, i, k)
            ring_steps(act, sh.G, step)
            store(act, sh.G - 2, 0)
            gelu(sh.G - 1, 1)
            store(act, sh.G - 1, 1)
            stored(act)
    return [*edges_in, *own, *win_sems]


def conv_pass(nc, sh, a, m, layer):
    name = f"conv{layer}"
    with ExitStack() as ctx:
        idx = ctx.enter_context(nc.sbuf_tensor(f"{name}_idx", [P, RING * TG], I32))
        rows = ctx.enter_context(nc.sbuf_tensor(f"{name}_rows", [P, RING, TG, D], F32))
        onehot = ctx.enter_context(nc.sbuf_tensor(f"{name}_onehot", [P, 2, TG, WIN], F32))
        ps_sum = [ctx.enter_context(nc.psum_tensor(f"{name}_ps_sum{k}", [P, 512], F32)) for k in range(2)]
        idx_in = semaphores(nc, m, "conv", [f"idx_in{k}" for k in range(RING)])
        pool_went, act_went, sp_went = m["went"]
        gathered = m["gathered"]
        placed, summed = own = semaphores(nc, m, "conv", ["placed", "summed"])
        store, load, add, stored, added, win_sems = window_add(nc, ctx, sh, m, name, m["acc"][1 + layer], D, summed,
                                                               ps_sum, act_went)
        block = ctx.enter_context(nc.Block())

        @block.sync
        def _(sp):
            def step(s, i, k):
                for t in range(TG):
                    wait_for(sp, gathered[k][t], i * 16)
                carry(sp, m["went"][2])
                sp.dma_start(idx[:, k * TG:(k + 1) * TG], a["src"][bass.ds(s * P, P), :]).then_inc(idx_in[k], 16)
            ring_steps(sp, sh.G, step)

        @block.gpsimd
        def _(pool):
            def step(s, i, k):
                pool.wait_ge(idx_in[k], i * 16 + 16)
                wait_for(pool, summed, s - (RING - 1))
                carry(pool, pool_went)
                for t in range(TG):
                    nc.gpsimd.indirect_dma_start(
                        rows[:, k, t, :], None, m["conv_table"][layer],
                        bass.IndirectOffsetOnAxis(idx[:, k * TG + t:k * TG + t + 1], axis=0)).then_inc(gathered[k][t], 16)
            ring_steps(pool, sh.G, step)

        @block.tensor
        def _(pe):
            def step(s, i, k):
                pe.wait_ge(placed, s + 1)
                wait_for(pe, added, s - 1)
                for t in range(TG):
                    pe.wait_ge(gathered[k][t], i * 16 + 16)
                    last = nc.tensor.matmul(ps_sum[k % 2][0:WIN, 0:D], onehot[:, k % 2, t, :], rows[:, k, t, :],
                                            start=(t == 0), stop=(t == TG - 1))
                last.then_inc(summed, 1)
            ring_steps(pe, sh.G, step)

        @block.vector
        def _(dve):
            def step(s, i, k):
                if not isinstance(s, int) or s >= 2:
                    add(dve, *earlier(s, i, k, 2))
                wait_for(dve, summed, s - 1)
                nc.vector.tensor_tensor(onehot[:, k % 2, :, :], m["iota"][:, None, :].broadcast_to([P, TG, WIN]),
                                        m["place"][:, bass.ds(s * TG, TG)][:, :, None].broadcast_to([P, TG, WIN]),
                                        ALU.is_equal).then_inc(placed, 1)
            ring_steps(dve, sh.G, step)
            n = sh.G // RING
            add(dve, sh.G - 2, n - 1, 2)
            add(dve, sh.G - 1, n - 1, 3)

        @block.scalar
        def _(act):
            def step(s, i, k):
                if not isinstance(s, int) or s >= 2:
                    store(act, s - 2, k)
                load(act, s, i, k)
            ring_steps(act, sh.G, step)
            store(act, sh.G - 2, 0)
            store(act, sh.G - 1, 1)
            stored(act)
    return [*idx_in, *own, *win_sems]


def rounds_of(nc, sh, m, one_round):
    reset, moved = semaphores(nc, m, "rounds", ["reset", "moved"])
    with nc.Block() as block:
        @block.vector
        def _(dve):
            nc.vector.tensor_copy(m["place"][:, :], m["place_first"][:, :, :].rearrange("p g t -> p (g t)")).then_inc(
                reset, 1)
            nc.vector.tensor_copy(m["low"][:, :], m["low_first"][:, :]).then_inc(reset, 1)
            dve.wait_ge(reset, 2)
    rounds = nc.values_load(m["rounds"][0:1, 0:1], min_val=1, max_val=sh.NP // WIN + 1,
                            skip_runtime_bounds_check_because="a group's dst lie in the nodes, so the spans do")
    with nc.Fori(0, rounds):
        used = one_round()
        with nc.Block() as block:
            @block.vector
            def _(dve):
                nc.vector.tensor_scalar(m["place"][:, :], m["place"][:, :], -float(WIN), None, ALU.add).then_inc(
                    moved, 1)
                nc.vector.tensor_scalar(m["low"][:, :], m["low"][:, :], WIN, sh.NP, ALU.add, ALU.min).then_inc(
                    moved, 1)
                dve.wait_ge(moved, 2)
        clear_all(nc, m, [*used, moved])
    clear(nc, [reset])


def halves_to_mean_rstd(nc, dve, link, st, mv, t1):
    link(nc.vector.tensor_tensor(mv[:, 0, :], st[:, :, 1], st[:, :, 4], ALU.add))
    link(nc.vector.tensor_scalar(mv[:, 0, :], mv[:, 0, :], 0.5, None, ALU.mult))
    link(nc.vector.tensor_tensor(t1[:, :], st[:, :, 1], mv[:, 0, :], ALU.subtract))
    link(nc.vector.tensor_tensor(t1[:, :], t1[:, :], t1[:, :], ALU.mult))
    link(nc.vector.tensor_tensor(mv[:, 1, :], st[:, :, 2], st[:, :, 5], ALU.add))
    link(nc.vector.tensor_scalar(mv[:, 1, :], mv[:, 1, :], 1.0 / D, EPS, ALU.mult, ALU.add))
    link(nc.vector.tensor_tensor(mv[:, 1, :], mv[:, 1, :], t1[:, :], ALU.add))


def node_update(nc, sh, a, m):
    NT = sh.NT
    with ExitStack() as ctx:
        def sb(name, shape, dt=F32):
            return ctx.enter_context(nc.sbuf_tensor(name, shape, dt))

        u = sb("upd_u", [P, NT, D])
        st = sb("upd_st", [P, NT, 6])
        mv = sb("upd_mv", [P, 2, NT])
        rs = sb("upd_rs", [P, NT])
        t1 = sb("upd_t1", [P, NT])
        with ExitStack() as c2:
            def sb2(name, shape, dt=F32):
                return c2.enter_context(nc.sbuf_tensor(name, shape, dt))

            ab = sb2("upd_ab", [P, 2, 2, HC])
            xt = sb2("upd_xt", [D, 2, P])
            s_rows = sb2("upd_rows", [P, 2, HC])
            s_cols = sb2("upd_cols", [P, 2, 2, P])
            bias = sb2("upd_bias", [P, 2, D])
            ps_t = [c2.enter_context(nc.psum_tensor(f"upd_ps_t{k}", [P, 512], F32)) for k in range(2)]
            ps_u = [c2.enter_context(nc.psum_tensor(f"upd_ps_u{k}", [P, 512], F32)) for k in range(2)]
            in0, in1, added, turned, copied, multiplied, based, made_u, stats_ok = semaphores(nc, m, "upd", [
                "in0", "in1", "added", "turned", "copied", "multiplied", "based", "made_u", "stats"])
            loaded = [in0, in1]
            with nc.Block() as block:
                @block.sync
                def _(sp):
                    sp.dma_start(m["x2"][:, :, :], a["x_rows"]).then_inc(m["loaded_x"], 16)

                    def step(c, i, k):
                        wait_for(sp, added, c - 1)
                        wait_for(sp, multiplied, c - 1)
                        carry(sp, m["went"][2])
                        for p in range(2):
                            sp.dma_start(ab[:, k, p, :], m["acc"][0][p][bass.ds(c * P, P), :]).then_inc(loaded[k], 16)
                        sp.dma_start(xt[:, k, :], a["xt"][:, bass.ds(c * P, P)]).then_inc(loaded[k], 16)
                    pair_steps(sp, NT, step)

                @block.vector
                def _(dve):
                    def sums(c, i, k):
                        dve.wait_ge(loaded[k], i * 48 + 48)
                        wait_for(dve, turned, c - 1)
                        nc.vector.tensor_tensor(s_rows[:, k, :], ab[:, k, 0, :], ab[:, k, 1, :], ALU.add).then_inc(
                            added, 1)
                        dve.wait_ge(added, c + 1)
                        nc.vector.tensor_copy(m["deg"][:, bass.ds(c, 1)], s_rows[:, k, H:HC])
                        nc.vector.scalar_tensor_tensor(out=bias[:, k, :], in0=m["w2u"][:, 2, :],
                                                       scalar=s_rows[:, k, H:HC], in1=m["bub"][:, :], op0=ALU.mult,
                                                       op1=ALU.add).then_inc(based, 1)

                    def collect(c, k):
                        dve.wait_ge(multiplied, c + 1)
                        dve.wait_ge(based, c + 1)
                        uc = u[:, bass.ds(c, 1), :].rearrange("p o d -> p (o d)")
                        nc.vector.tensor_tensor(uc, ps_u[k % 2][:, 0:D], bias[:, k % 2, :], ALU.add).then_inc(made_u, 1)
                        dve.wait_ge(made_u, c + 1)
                        nc.vector.bn_stats(st[:, bass.ds(c, 1), :].rearrange("p o d -> p (o d)"), uc).then_inc(
                            stats_ok, 1)

                    def step(c, i, k):
                        sums(c, i, k)
                        if not isinstance(c, int) or c >= 1:
                            collect(c - 1, k - 1)
                    pair_steps(dve, NT, step)
                    collect(NT - 1, 1)
                    dve.wait_ge(stats_ok, NT)

                @block.tensor
                def _(pe):
                    def turn(c, k):
                        pe.wait_ge(added, c + 1)
                        wait_for(pe, copied, c - 1)
                        for j in range(2):
                            last = nc.tensor.matmul(ps_t[k][:, j * P:(j + 1) * P], s_rows[:, k, j * P:(j + 1) * P],
                                                    m["ident"][:, :], start=True, stop=True)
                        last.then_inc(turned, 1)

                    def multiply(c, k):
                        pe.wait_ge(copied, c + 1)
                        wait_for(pe, made_u, c - 1)
                        nc.tensor.matmul(ps_u[k][:, 0:D], xt[:, k, :], m["wu"][:, 0, :], start=True, stop=False)
                        for j in range(2):
                            last = nc.tensor.matmul(ps_u[k][:, 0:D], s_cols[:, k, j, :], m["w2u"][:, j, :],
                                                    start=False, stop=(j == 1))
                        last.then_inc(multiplied, 1)

                    def step(c, i, k):
                        turn(c, k)
                        if not isinstance(c, int) or c >= 1:
                            multiply(c - 1, 1 - k)
                    pair_steps(pe, NT, step)
                    multiply(NT - 1, 1)

                @block.scalar
                def _(act):
                    def step(c, i, k):
                        act.wait_ge(turned, c + 1)
                        wait_for(act, multiplied, c - 1)
                        nc.scalar.activation(s_cols[:, k, :, :].rearrange("p j d -> p (j d)"), ps_t[k][:, 0:H],
                                             ACT.Copy).then_inc(copied, 1)
                    pair_steps(act, NT, step)

        n_b = NT // NB
        chain, var_ok, rstd_ok, shifted, gelu_ok, summed_ok = semaphores(nc, m, "ln", [
            "chain", "var_ok", "rstd_ok", "shifted", "gelu", "summed"])
        with nc.Block() as block:
            @block.gpsimd
            def _(pool):
                pool.wait_ge(var_ok, 2)
                nc.gpsimd.tensor_tensor(rs[:, :], mv[:, 1, :], m["expo"][:, 0:NT], ALU.pow).then_inc(rstd_ok, 1)
                nc.gpsimd.tensor_tensor(m["dinv"][:, :], t1[:, :], m["expo"][:, 0:NT], ALU.pow).then_inc(rstd_ok, 1)
                pool.wait_ge(var_ok, 3)
                nc.gpsimd.tensor_tensor(rs[:, :], mv[:, 1, :], m["expo"][:, 0:NT], ALU.pow).then_inc(rstd_ok, 1)

            @block.scalar
            def _(act):
                for b in range(n_b):
                    act.wait_ge(shifted, b + 1)
                    t = u[:, b * NB:(b + 1) * NB, :]
                    nc.scalar.activation(t, t, ACT.Gelu).then_inc(gelu_ok, 1)

            @block.vector
            def _(dve):
                count = [0]

                def link(ins):
                    count[0] += 1
                    ins.then_inc(chain, 1)
                    dve.wait_ge(chain, count[0])

                halves_to_mean_rstd(nc, dve, link, st, mv, t1)
                nc.vector.tensor_copy(mv[:, 0, :], mv[:, 0, :]).then_inc(var_ok, 1)
                nc.vector.tensor_scalar(t1[:, :], m["deg"][:, :], 1.0, None, ALU.add).then_inc(var_ok, 1)
                dve.wait_ge(rstd_ok, 2)

                def spread(v):
                    return v[:, :, None].broadcast_to([P, NB, D])

                def across(v):
                    return v[:, None, :].broadcast_to([P, NB, D])

                for b in range(n_b):
                    r = slice(b * NB, (b + 1) * NB)
                    t = u[:, r, :]
                    link(nc.vector.tensor_tensor(t, t, spread(mv[:, 0, r]), ALU.subtract))
                    link(nc.vector.tensor_tensor(t, t, spread(rs[:, r]), ALU.mult))
                    link(nc.vector.tensor_tensor(t, t, across(m["gub"]), ALU.mult))
                    nc.vector.tensor_tensor(t, t, across(m["beub"]), ALU.add).then_inc(shifted, 1)
                dve.wait_ge(m["loaded_x"], 16)
                for b in range(n_b):
                    r = slice(b * NB, (b + 1) * NB)
                    dve.wait_ge(gelu_ok, b + 1)
                    link(nc.vector.scalar_tensor_tensor(
                        out=u[:, r, :].rearrange("p t d -> p (t d)"), in0=m["x2"][:, r, :].rearrange("p t d -> p (t d)"),
                        scalar=2.0, in1=u[:, r, :].rearrange("p t d -> p (t d)"), op0=ALU.mult, op1=ALU.add))
                    for c in range(b * NB, (b + 1) * NB):
                        last = nc.vector.bn_stats(st[:, c, :], u[:, c, :])
                    link(last)
                halves_to_mean_rstd(nc, dve, link, st, mv, t1)
                nc.vector.tensor_copy(mv[:, 0, :], mv[:, 0, :]).then_inc(var_ok, 1)
                dve.wait_ge(rstd_ok, 3)
                for b in range(n_b):
                    r = slice(b * NB, (b + 1) * NB)
                    t = u[:, r, :]
                    link(nc.vector.tensor_tensor(t, t, spread(mv[:, 0, r]), ALU.subtract))
                    link(nc.vector.tensor_tensor(m["x2"][:, r, :], t, spread(rs[:, r]), ALU.mult))
    clear(nc, conv_table(nc, sh, a, m, 0))


def conv_table(nc, sh, a, m, layer):
    NT = sh.NT
    name = f"ctab{layer}"
    with ExitStack() as ctx:
        def sb(n, shape, dt=F32):
            return ctx.enter_context(nc.sbuf_tensor(f"{name}_{n}", shape, dt))

        xr = sb("xr", [P, 2, D])
        hs = sb("hs", [P, 2, D])
        out = sb("out", [P, 2, D])
        ps_t = [ctx.enter_context(nc.psum_tensor(f"{name}_ps_t{k}", [P, 512], F32)) for k in range(2)]
        ps_h = [ctx.enter_context(nc.psum_tensor(f"{name}_ps_h{k}", [P, 512], F32)) for k in range(2)]
        picked, turned, columns, multiplied, scaled, out0, out1 = own = semaphores(nc, m, "ctab", [
            "picked", "turned", "columns", "multiplied", "scaled", "out0", "out1"])
        row_out = [out0, out1]
        block = ctx.enter_context(nc.Block())

        @block.scalar
        def _(act):
            def pick(c, i, k):
                wait_for(act, turned, c - 1)
                nc.scalar.activation(xr[:, k, :], m["x2"][:, bass.ds(c, 1), :].rearrange("p o d -> p (o d)"),
                                     ACT.Copy).then_inc(picked, 1)

            def columns_of(c, k):
                wait_for(act, multiplied, c - 1)
                if layer == 0:
                    act.wait_ge(turned, c + 1)
                    nc.scalar.activation(hs[:, k % 2, :], ps_t[k % 2][:, 0:D], ACT.Copy).then_inc(columns, 1)
                else:
                    nc.scalar.activation(hs[:, k % 2, :], m["cols"][:, bass.ds(c * P, P)], ACT.Relu,
                                         bias=m["shift"][:, 0:1], scale=m["gain"][:, 0:1]).then_inc(columns, 1)

            def step(c, i, k):
                if layer == 0:
                    pick(c, i, k)
                    if not isinstance(c, int) or c >= 1:
                        columns_of(c - 1, k - 1)
                else:
                    columns_of(c, k)
            pair_steps(act, NT, step)
            if layer == 0:
                columns_of(NT - 1, 1)

        @block.tensor
        def _(pe):
            def turn(c, k):
                pe.wait_ge(picked, c + 1)
                wait_for(pe, columns, c - 1)
                nc.tensor.matmul(ps_t[k][:, 0:D], xr[:, k, :], m["ident"][:, :], start=True, stop=True).then_inc(
                    turned, 1)

            def multiply(c, k):
                pe.wait_ge(columns, c + 1)
                wait_for(pe, scaled, c - 1)
                nc.tensor.matmul(ps_h[k % 2][:, 0:D], hs[:, k % 2, :], m["wc"][:, layer, :], start=True,
                                 stop=True).then_inc(multiplied, 1)

            def step(c, i, k):
                if layer == 0:
                    turn(c, k)
                    if not isinstance(c, int) or c >= 1:
                        multiply(c - 1, k - 1)
                else:
                    multiply(c, k)
            pe.wait_ge(m["loaded_conv"], 16 * 8)
            pair_steps(pe, NT, step)
            if layer == 0:
                multiply(NT - 1, 1)

        @block.vector
        def _(dve):
            def step(c, i, k):
                dve.wait_ge(multiplied, c + 1)
                wait_for(dve, row_out[k], i * 16)
                nc.vector.tensor_scalar(out[:, k, :], ps_h[k][:, 0:D], m["dinv"][:, bass.ds(c, 1)], None,
                                        ALU.mult).then_inc(scaled, 1)
            pair_steps(dve, NT, step)

        @block.sync
        def _(sp):
            def step(c, i, k):
                sp.wait_ge(scaled, c + 1)
                carry(sp, m["went"][2])
                sp.dma_start(m["conv_table"][layer][bass.ds(c * P, P), :], out[:, k, :]).then_inc(row_out[k], 16)
            pair_steps(sp, NT, step)
            for k in range(2):
                sp.wait_ge(row_out[k], 16 * (NT // 2))
    return own


def batch_norm(nc, sh, a, m, layer):
    NT = sh.NT
    name = f"bn{layer}"
    with ExitStack() as ctx:
        def sb(n, shape, dt=F32):
            return ctx.enter_context(nc.sbuf_tensor(f"{name}_{n}", shape, dt))

        ab = sb("ab", [P, 2, 3, D])
        diag = sb("diag", [P, 2, P])
        n_s = sh.N // sh.BN
        st = sb("st", [P, n_s, 6])
        mv = sb("mv", [P, 2])
        rs = sb("rs", [P, 2])
        ps_c = [ctx.enter_context(nc.psum_tensor(f"{name}_ps_c{k}", [P, 512], F32)) for k in range(2)]
        in0, in1, diag_ok, turned, filled, chain, var_ok, rstd_ok = own = semaphores(nc, m, "bn", [
            "in0", "in1", "diag", "turned", "filled", "chain", "var_ok", "rstd_ok"])
        loaded = [in0, in1]
        block = ctx.enter_context(nc.Block())

        @block.sync
        def _(sp):
            def step(c, i, k):
                wait_for(sp, turned, c - 1)
                carry(sp, m["went"][2])
                for p, part in enumerate((*m["acc"][1 + layer], m["conv_table"][layer])):
                    sp.dma_start(ab[:, k, p, :], part[bass.ds(c * P, P), :]).then_inc(loaded[k], 16)
            pair_steps(sp, NT, step)

        @block.tensor
        def _(pe):
            def step(c, i, k):
                pe.wait_ge(loaded[k], i * 48 + 48)
                pe.wait_ge(diag_ok, c + 1)
                wait_for(pe, filled, c - 1)
                for p in range(3):
                    last = nc.tensor.matmul(ps_c[k][:, 0:P], ab[:, k, p, :], diag[:, k, :], start=(p == 0),
                                            stop=(p == 2))
                last.then_inc(turned, 1)
            pair_steps(pe, NT, step)

        @block.scalar
        def _(act):
            def step(c, i, k):
                act.wait_ge(turned, c + 1)
                nc.scalar.activation(m["cols"][:, bass.ds(c * P, P)], ps_c[k][:, 0:P], ACT.Identity,
                                     bias=m["colc"][:, layer, 0:1]).then_inc(filled, 1)
            act.wait_ge(m["loaded_conv"], 16 * 8)
            pair_steps(act, NT, step)

        @block.gpsimd
        def _(pool):
            pool.wait_ge(var_ok, 1)
            nc.gpsimd.tensor_tensor(rs[:, 0:1], mv[:, 1:2], m["expo"][:, 0:1], ALU.pow).then_inc(rstd_ok, 1)

        @block.vector
        def _(dve):
            def step(c, i, k):
                wait_for(dve, turned, c - 1)
                nc.vector.tensor_scalar(diag[:, k, :], m["ident"][:, :], m["dinv"][:, bass.ds(c, 1)], None,
                                        ALU.mult).then_inc(diag_ok, 1)
            pair_steps(dve, NT, step)
            count = [0]

            def link(ins):
                count[0] += 1
                ins.then_inc(chain, 1)
                dve.wait_ge(chain, count[0])

            dve.wait_ge(filled, NT)
            for j in range(n_s):
                last = nc.vector.bn_stats(st[:, j, :], m["cols"][:, j * sh.BN:(j + 1) * sh.BN])
            link(last)
            link(nc.vector.bn_aggr(mv[:, :], st[:, :, :].rearrange("p j s -> p (j s)")))
            nc.vector.tensor_scalar(mv[:, 1:2], mv[:, 1:2], EPS, None, ALU.add).then_inc(var_ok, 1)
            dve.wait_ge(rstd_ok, 1)
            link(nc.vector.tensor_tensor(m["gain"][:, :], rs[:, 0:1], m["colc"][:, layer, 1:2], ALU.mult))
            link(nc.vector.tensor_tensor(rs[:, 1:2], mv[:, 0:1], m["gain"][:, :], ALU.mult))
            link(nc.vector.tensor_tensor(m["shift"][:, :], m["colc"][:, layer, 2:3], rs[:, 1:2], ALU.subtract))
    return own


def last_norm(nc, sh, a, m, out):
    NT = sh.NT
    full = sh.N // P
    rest = sh.N - full * P
    with ExitStack() as ctx:
        def sb(n, shape, dt=F32):
            return ctx.enter_context(nc.sbuf_tensor(f"fin_{n}", shape, dt))

        hs = sb("hs", [P, 2, P])
        st = sb("st", [P, NT, 6])
        mv = sb("mv", [P, 2, NT])
        rs = sb("rs", [P, NT])
        t1 = sb("t1", [P, NT])
        ps_y = [ctx.enter_context(nc.psum_tensor(f"fin_ps_y{k}", [P, 512], F32)) for k in range(2)]
        clipped, turned, joined, stats_ok, chain, var_ok, rstd_ok, normed, out_ok = semaphores(nc, m, "fin", [
            "clipped", "turned", "joined", "stats", "chain", "var_ok", "rstd_ok", "normed", "out"])
        block = ctx.enter_context(nc.Block())
        n_b = NT // NB

        @block.scalar
        def _(act):
            def step(c, i, k):
                wait_for(act, turned, c - 1)
                nc.scalar.activation(hs[:, k, :], m["cols"][:, bass.ds(c * P, P)], ACT.Relu,
                                     bias=m["shift"][:, 0:1], scale=m["gain"][:, 0:1]).then_inc(clipped, 1)
            pair_steps(act, NT, step)

        @block.tensor
        def _(pe):
            def step(c, i, k):
                pe.wait_ge(clipped, c + 1)
                wait_for(pe, joined, c - 1)
                nc.tensor.matmul(ps_y[k][:, 0:D], hs[:, k, :], m["ident"][:, :], start=True, stop=True).then_inc(
                    turned, 1)
            pair_steps(pe, NT, step)

        @block.gpsimd
        def _(pool):
            pool.wait_ge(var_ok, 1)
            nc.gpsimd.tensor_tensor(rs[:, :], mv[:, 1, :], m["expo"][:, 0:NT], ALU.pow).then_inc(rstd_ok, 1)

        @block.vector
        def _(dve):
            def step(c, i, k):
                dve.wait_ge(turned, c + 1)
                xc = m["x2"][:, bass.ds(c, 1), :].rearrange("p o d -> p (o d)")
                nc.vector.scalar_tensor_tensor(out=xc, in0=xc, scalar=2.0, in1=ps_y[k][:, 0:D], op0=ALU.mult,
                                               op1=ALU.add).then_inc(joined, 1)
                dve.wait_ge(joined, c + 1)
                nc.vector.bn_stats(st[:, bass.ds(c, 1), :].rearrange("p o d -> p (o d)"), xc).then_inc(stats_ok, 1)
            pair_steps(dve, NT, step)
            dve.wait_ge(stats_ok, NT)
            count = [0]

            def link(ins):
                count[0] += 1
                ins.then_inc(chain, 1)
                dve.wait_ge(chain, count[0])

            halves_to_mean_rstd(nc, dve, link, st, mv, t1)
            nc.vector.tensor_copy(mv[:, 0, :], mv[:, 0, :]).then_inc(var_ok, 1)
            dve.wait_ge(rstd_ok, 1)
            for b in range(n_b):
                r = slice(b * NB, (b + 1) * NB)
                t = m["x2"][:, r, :]
                link(nc.vector.tensor_tensor(t, t, mv[:, 0, r][:, :, None].broadcast_to([P, NB, D]), ALU.subtract))
                nc.vector.tensor_tensor(t, t, rs[:, r][:, :, None].broadcast_to([P, NB, D]), ALU.mult).then_inc(
                    normed, 1)

        @block.sync
        def _(sp):
            stores = 0
            for b in range(n_b):
                sp.wait_ge(normed, b + 1)
                first, last = b * NB, min((b + 1) * NB, full)
                if last > first:
                    sp.dma_start(out[first * P:last * P, :].rearrange("(c p) d -> p c d", p=P),
                                 m["x2"][:, first:last, :]).then_inc(out_ok, 16)
                    stores += 1
            if rest:
                sp.dma_start(out[full * P:sh.N, :], m["x2"][0:rest, full, :]).then_inc(out_ok, 16)
                stores += 1
            sp.wait_ge(out_ok, 16 * stores)


def build(nc, a, out, n_nodes, n_groups):
    sh = Shape(n_nodes, n_groups)
    NT = sh.NT
    with ExitStack() as ctx:
        def sb(name, shape, dt=F32):
            return ctx.enter_context(nc.sbuf_tensor(name, shape, dt))

        def dram(name, shape, dt=F32):
            return nc.dram_tensor(name, shape, dt, kind="Internal").ap()

        m = {
            "sems": {}, "ident": sb("ident", [P, P]), "iota": sb("iota", [P, WIN]), "expo": sb("expo", [P, max(NT, TG)]),
            "w1c": sb("w1c", [P, H]), "wtab": sb("wtab", [P, TV]), "btab": sb("btab", [P, TV]),
            "wm": sb("wm", [P, QK, TV]), "w2u": sb("w2u", [P, 3, D]), "wu": sb("wu", [P, 2, D]),
            "wc": sb("wc", [P, 2, D]), "colc": sb("colc", [P, 2, 3]),
            "b1b": sb("b1b", [P, H]), "g1b": sb("g1b", [P, H]), "be1b": sb("be1b", [P, H]),
            "bub": sb("bub", [P, D]), "gub": sb("gub", [P, D]), "beub": sb("beub", [P, D]),
            "place_first": sb("place_first", [P, sh.G, TG]), "place": sb("place", [P, sh.G * TG]),
            "low_first": sb("low_first", [1, sh.G], I32), "low": sb("low", [1, sh.G], I32),
            "rounds": sb("rounds", [1, 1], I32), "deg": sb("deg", [P, NT]), "dinv": sb("dinv", [P, NT]),
            "gain": sb("gain", [P, 1]), "shift": sb("shift", [P, 1]),
            "low_dram": dram("low_dram", [sh.G], I32), "need_dram": dram("need_dram", [sh.G], I32),
            "table": dram("table", [sh.NP, TR]),
            "conv_table": [dram(f"conv_table{j}", [sh.NP, D]) for j in range(2)],
            "acc": [[dram(f"acc{j}_{p}", [sh.ACC, HC if j == 0 else D]) for p in range(2)] for j in range(3)],
        }
        gathered = semaphores(nc, m, "all", [f"gathered{n}" for n in range(RING * TG)])
        m["went"] = semaphores(nc, m, "all", ["pool_went", "act_went", "sp_went"])
        m["gathered"] = [gathered[k * TG:(k + 1) * TG] for k in range(RING)]
        m["loaded_conv"], m["loaded_x"], zero_made, conv_zeroed = semaphores(nc, m, "all", [
            "loaded_conv", "loaded_x", "zero_made", "conv_zeroed"])
        prepare(nc, sh, a, m)
        node_table(nc, sh, a, m)
        rounds_of(nc, sh, m, lambda: message_pass(nc, sh, a, m))
        m["x2"] = sb("x2", [P, NT, D])
        with ExitStack() as zctx:
            zeros = zctx.enter_context(nc.sbuf_tensor("conv_zeros", [P, NB * D], F32))
            with nc.Block() as block:
                @block.gpsimd
                def _(pool):
                    nc.gpsimd.memset(zeros[:, :], 0.0).then_inc(zero_made, 1)

                @block.sync
                def _(sp):
                    sp.wait_ge(zero_made, 1)
                    for acc in (*m["acc"][1], *m["acc"][2]):
                        for b in range(NT // NB):
                            sp.dma_start(acc[b * NB * P:(b + 1) * NB * P, :].rearrange("(p k) c -> p (k c)", p=P),
                                         zeros[:, :]).then_inc(conv_zeroed, 16)
                        sp.dma_start(acc[sh.NP:sh.ACC, :], zeros[0:WIN, 0:D]).then_inc(conv_zeroed, 16)
            node_update(nc, sh, a, m)
            with nc.Block() as block:
                @block.sync
                def _(sp):
                    sp.wait_ge(conv_zeroed, 4 * 16 * (NT // NB + 1))
        m["cols"] = sb("cols", [P, sh.NP])
        rounds_of(nc, sh, m, lambda: conv_pass(nc, sh, a, m, 0))
        clear(nc, batch_norm(nc, sh, a, m, 0))
        conv_table(nc, sh, a, m, 1)
        rounds_of(nc, sh, m, lambda: conv_pass(nc, sh, a, m, 1))
        batch_norm(nc, sh, a, m, 1)
        last_norm(nc, sh, a, m, out)


def lay_out(x, src, dst, edge_attr):
    import numpy as np
    n, e = x.shape[0], src.shape[0]
    nt = -(-n // P)
    g = RING * -(-e // (GE * RING))
    pad = g * GE - e
    src = np.concatenate([src, np.zeros(pad, src.dtype)])
    dst = np.concatenate([dst, np.full(pad, n, dst.dtype)])
    ea = np.concatenate([edge_attr, np.zeros((pad, ED), edge_attr.dtype)])
    xp = np.concatenate([x, np.zeros((nt * P - n, D), x.dtype)])
    c = np.ascontiguousarray
    return g, {
        "in_src": c(src.reshape(g * P, TG)),
        "in_dst_rows": c(dst.reshape(g // RING, RING, GE)),
        "in_dst_cols": c(dst.reshape(g, P, TG).transpose(1, 0, 2)),
        "in_ea_n": c(ea.reshape(g * P, TG * ED)),
        "in_ea_t": c(ea.reshape(g, P, TG // QK, QK, ED).transpose(0, 3, 4, 2, 1).reshape(g * P, TG // QK * P)),
        "in_xt": c(xp.T),
        "in_x_rows": c(xp.reshape(nt, P, D).transpose(1, 0, 2)),
    }


_WEIGHTS = ["L0_gnn_W1", "L0_gnn_b1", "L0_gnn_g1", "L0_gnn_be1", "L0_gnn_W2", "L0_gnn_b2", "L0_gnn_Wu", "L0_gnn_bu",
            "L0_gnn_gu", "L0_gnn_beu", "L1_gnn_W0", "L1_gnn_b0", "L1_gnn_g0", "L1_gnn_be0", "L1_gnn_W1", "L1_gnn_b1",
            "L1_gnn_g1", "L1_gnn_be1"]


def kernel(x, src, dst, edge_attr_32, **weights):
    import numpy as np
    import concourse.bacc as bacc
    from concourse.bass_utils import run_bass_kernel_spmd

    g, arrays = lay_out(np.asarray(x), np.asarray(src), np.asarray(dst), np.asarray(edge_attr_32))
    for w in _WEIGHTS:
        arrays[f"in_{w}"] = np.ascontiguousarray(np.asarray(weights[w]))
    nc = bacc.Bacc("TRN2", target_bir_lowering=False, num_devices=1)
    t = {n: nc.dram_tensor(n, v.shape, mybir.dt.from_np(v.dtype), kind="ExternalInput").ap()
         for n, v in arrays.items()}
    a = {k: t[f"in_{k}"] for k in ("src", "dst_rows", "dst_cols", "ea_n", "ea_t", "xt", "x_rows")}
    a.update({k: t[f"in_L0_gnn_{k}"] for k in ("W1", "b1", "g1", "be1", "W2", "b2", "Wu", "bu", "gu", "beu")})
    a["Wc"] = [t["in_L1_gnn_W0"], t["in_L1_gnn_W1"]]
    a["colc"] = [[t[f"in_L1_gnn_{r}{j}"] for r in ("b", "g", "be")] for j in range(2)]
    out = nc.dram_tensor("out", [x.shape[0], D], F32, kind="ExternalOutput").ap()
    build(nc, a, out, x.shape[0], g)
    r = run_bass_kernel_spmd(nc, [arrays], core_ids=[0])
    return r.results[0]["out"]
```

```python
import concourse.bass as bass
from concourse import mybir
from contextlib import ExitStack

F32 = mybir.dt.float32
I32 = mybir.dt.int32
ALU = mybir.AluOpType
ACT = mybir.ActivationFunctionType
AX = mybir.AxisListType

P = 128
TG = 8
GE = TG * P
WIN = 64
WIN_SHIFT = 6
RING = 4
CHUNK = 2
NC_CH = TG // CHUNK
D = 128
ED = 32
H = 256
TV = H + ED
TR = 320
HC = H + 1
QK = P // ED
EPS = 1e-5
NEWTON = 2 + 3 * 3
NB = 7


def wait_for(engine, sem, count):
    if isinstance(count, int) and count <= 0:
        return
    engine.wait_ge(sem, count)


def carry(engine, sem):
    engine.sem_inc(sem, 1)


def ring_steps(engine, n, step):
    for k in range(RING):
        step(k, 0, k)
    with engine.Fori(1, n // RING) as i:
        for k in range(RING):
            step(i * RING + k, i, k)


def pair_steps(engine, n, step):
    for k in range(2):
        step(k, 0, k)
    with engine.Fori(1, n // 2) as i:
        for k in range(2):
            step(i * 2 + k, i, k)


def tile_steps(engine, n, step):
    for j in range(2 * NB):
        step(j, 0, j)
    with engine.Fori(1, n // (2 * NB)) as i:
        for j in range(2 * NB):
            step(i * (2 * NB) + j, i, j)


class Shape:
    def __init__(self, n_nodes, n_groups):
        self.N = n_nodes
        self.NT = -(-n_nodes // P)
        self.NP = self.NT * P
        self.G = n_groups
        self.GP = n_groups // RING
        self.ACC = self.NP + WIN
        self.BN = max(d for d in range(1, 513) if n_nodes % d == 0)


def semaphores(nc, m, prefix, names):
    for n in names:
        if f"{prefix}_{n}" not in m["sems"]:
            m["sems"][f"{prefix}_{n}"] = nc.alloc_semaphore(name=f"{prefix}_{n}")
    return [m["sems"][f"{prefix}_{n}"] for n in names]


def clear(nc, sems):
    for s in sems:
        nc.sync.sem_clear(s)
    nc.all_engine_barrier()


def clear_all(nc, m, sems):
    nc.gpsimd.drain()
    gathered = [s for slot in m["gathered"] for s in slot]
    nums = [s.num for s in gathered]
    assert nums == list(range(nums[0], nums[-1] + 1))
    nc.gpsimd.dma_reset(range(nums[0], nums[-1] + 1))
    nc.all_engine_barrier()
    clear(nc, [*sems, *gathered])


def prepare(nc, sh, a, m):
    with ExitStack() as ctx:
        def sb(name, shape, dt=F32):
            return ctx.enter_context(nc.sbuf_tensor(name, shape, dt))

        w1x = sb("w1x", [P, H])
        w1e = sb("w1e", [P, H])
        b2b = sb("b2b", [P, D])
        w2 = sb("w2", [P, 2, D])
        mean = sb("prep_mean", [P, 3])
        wt = sb("prep_transposed", [P, 9, P])
        dst_rows = sb("dst_rows", [sh.GP, RING, GE], I32)
        dst_cols = sb("dst_cols", [P, sh.G, TG], I32)
        low = sb("group_low", [sh.GP, RING], I32)
        high = sb("group_high", [sh.GP, RING], I32)
        span = sb("group_span", [sh.GP, RING], I32)
        shifted = sb("group_shifted", [sh.GP, RING], I32)
        need = sb("group_rounds", [sh.GP, RING], I32)
        low_b = sb("low_b", [P, sh.G], I32)
        need_row = sb("need_row", [1, sh.G], I32)
        iota_i = sb("iota_i", [P, WIN], I32)
        zeros, zeroed = m["zeros"], m["acc_zeroed"]
        turned = ctx.enter_context(nc.psum_tensor("prep_turned", [P, 12, P], F32))
        prods = ctx.enter_context(nc.psum_tensor("prep_prods", [P, 512], F32))
        (loaded_w, loaded_dst, zero_set, cleared, made, centred, turned_ok, copied, prods_ok, folded,
         range_ok, chain, range_out, range_in) = semaphores(nc, m, "prep", [
            "loaded_w", "loaded_dst", "zero_set", "cleared", "made", "centred", "turned", "copied", "prods",
            "folded", "range", "chain", "range_out", "range_in"])
        block = ctx.enter_context(nc.Block())
        n_w = 1 + QK + 7 + 2

        @block.sync
        def _(sp):
            sp.dma_start(dst_rows[:, :, :], a["dst_rows"]).then_inc(loaded_dst, 16)
            sp.dma_start(dst_cols[:, :, :], a["dst_cols"]).then_inc(loaded_dst, 16)
            sp.dma_start(w1x[:, :], a["W1"][0:D, :]).then_inc(loaded_w, 16)
            for q in range(QK):
                sp.dma_start(w1e[q * ED:(q + 1) * ED, :], a["W1"][D:D + ED, :]).then_inc(loaded_w, 16)
            for dst, src in ((m["b1b"], a["b1"]), (m["g1b"], a["g1"]), (m["be1b"], a["be1"]), (b2b, a["b2"]),
                             (m["bub"], a["bu"]), (m["gub"], a["gu"]), (m["beub"], a["beu"])):
                sp.dma_start(dst[:, :], src.partition_broadcast(P)).then_inc(loaded_w, 16)
            sp.dma_start(w2[:, :, :], a["W2"].rearrange("(j p) d -> p j d", p=P)).then_inc(loaded_w, 16)
            sp.dma_start(m["wu"][:, :, :], a["Wu"].rearrange("(j p) d -> p j d", p=P)).then_inc(loaded_w, 16)
            for j in range(2):
                sp.dma_start(m["wc"][:, j, :], a["Wc"][j]).then_inc(m["loaded_conv"], 16)
                for r in range(3):
                    sp.dma_start(m["colc"][:, j, r:r + 1], a["colc"][j][r].rearrange("(p o) -> p o", o=1)).then_inc(
                        m["loaded_conv"], 16)
            sp.wait_ge(range_ok, 2)
            sp.dma_start(m["low_dram"].rearrange("(p j) -> p j", j=RING), low[:, :]).then_inc(range_out, 16)
            sp.dma_start(m["need_dram"].rearrange("(p j) -> p j", j=RING), need[:, :]).then_inc(range_out, 16)
            sp.wait_ge(range_out, 32)
            sp.dma_start(m["low_first"][:, :], m["low_dram"].rearrange("(o g) -> o g", o=1)).then_inc(range_in, 16)
            sp.dma_start(need_row[:, :], m["need_dram"].rearrange("(o g) -> o g", o=1)).then_inc(range_in, 16)
            sp.dma_start(low_b[:, :], m["low_dram"].partition_broadcast(P)).then_inc(range_in, 16)
            sp.wait_ge(zero_set, 1)
            for acc in m["acc"][0]:
                rows = sh.NT
                for r in range(0, rows, 4):
                    k = min(4, rows - r)
                    sp.dma_start(acc[r * P:(r + k) * P, :].rearrange("(p k) c -> p (k c)", p=P),
                                 zeros[:, 0:k * HC]).then_inc(zeroed, 16)
                sp.dma_start(acc[sh.NP:sh.ACC, :], zeros[0:WIN, 0:HC]).then_inc(zeroed, 16)
                m["acc_zeroed_count"] += 16 * (-(-rows // 4) + 1)

        @block.gpsimd
        def _(pool):
            nc.gpsimd.memset(zeros[:, :], 0.0).then_inc(zero_set, 1)
            nc.gpsimd.memset(m["ident"][:, :], 0.0).then_inc(cleared, 1)
            pool.wait_ge(cleared, 1)
            nc.gpsimd.affine_select(out=m["ident"][:, :], in_=m["ident"][:, :], compare_op=ALU.not_equal, fill=1.0,
                                    base=0, pattern=[[-1, P]], channel_multiplier=1).then_inc(made, 1)
            nc.gpsimd.iota(iota_i[:, :], pattern=[[1, WIN]], base=0, channel_multiplier=0).then_inc(made, 1)
            nc.gpsimd.memset(m["wm"][:, :, :], 0.0).then_inc(made, 1)
            nc.gpsimd.memset(m["expo"][:, :], -0.5).then_inc(made, 1)

        @block.vector
        def _(dve):
            count = [0]

            def link(ins):
                count[0] += 1
                ins.then_inc(chain, 1)
                dve.wait_ge(chain, count[0])

            dve.wait_ge(loaded_dst, 32)
            nc.vector.tensor_reduce(high[:, :], dst_rows[:, :, :], AX.X, ALU.max).then_inc(chain, 1)
            count[0] += 1
            nc.vector.tensor_reduce(low[:, :], dst_rows[:, :, :], AX.X, ALU.min).then_inc(range_ok, 1)
            dve.wait_ge(range_ok, 1)
            dve.wait_ge(chain, count[0])
            link(nc.vector.tensor_tensor(span[:, :], high[:, :], low[:, :], ALU.subtract))
            link(nc.vector.tensor_scalar(shifted[:, :], span[:, :], WIN_SHIFT, None, ALU.logical_shift_right))
            nc.vector.tensor_scalar(need[:, :], shifted[:, :], 1, None, ALU.add).then_inc(range_ok, 1)
            dve.wait_ge(made, 4)
            link(nc.vector.tensor_copy(m["iota"][:, :], iota_i[:, :]))
            dve.wait_ge(loaded_w, 16 * n_w)
            for j, t in enumerate((w1x, w1e, m["b1b"])):
                link(nc.vector.tensor_reduce(mean[:, j:j + 1], t[:, :], AX.X, ALU.add))
            link(nc.vector.tensor_scalar(mean[:, :], mean[:, :], -1.0 / H, None, ALU.mult))
            for j, (t, o) in enumerate(((w1x, m["w1c"]), (w1e, w1e), (m["b1b"], m["b1b"]))):
                nc.vector.tensor_scalar(o[:, :], t[:, :], mean[:, j:j + 1], None, ALU.add).then_inc(centred, 1)
            dve.wait_ge(turned_ok, 1)
            for r in range(3):
                nc.vector.tensor_copy(wt[:, 3 * r:3 * r + 3, :], turned[:, 4 * r:4 * r + 3, :]).then_inc(copied, 1)
            dve.wait_ge(centred, 3)
            link(nc.vector.tensor_tensor(m["wtab"][:, 0:H], m["w1c"][:, :], m["g1b"][:, :], ALU.mult))
            link(nc.vector.tensor_tensor(m["btab"][:, 0:H], m["b1b"][:, :], m["g1b"][:, :], ALU.mult))
            for q in range(QK):
                r = slice(q * ED, (q + 1) * ED)
                link(nc.vector.tensor_tensor(m["wm"][r, q, 0:H], w1e[r, :], m["g1b"][r, :], ALU.mult))
            dve.wait_ge(prods_ok, 1)
            nc.vector.tensor_scalar(m["wtab"][:, H:TV], prods[:, 0:ED], 2.0 / H, None, ALU.mult).then_inc(folded, 1)
            nc.vector.tensor_scalar(m["btab"][:, H:TV], prods[:, ED:2 * ED], 2.0 / H, None, ALU.mult).then_inc(folded, 1)
            for q in range(QK):
                r = slice(q * ED, (q + 1) * ED)
                nc.vector.tensor_scalar(m["wm"][r, q, H:TV], prods[r, 2 * ED:3 * ED], 1.0 / H, None,
                                        ALU.mult).then_inc(folded, 1)
            nc.vector.tensor_copy(m["w2u"][:, :, :], prods[:, D:4 * D].rearrange("p (j d) -> p j d", j=3)).then_inc(
                folded, 1)
            dve.wait_ge(range_in, 48)
            link(nc.vector.tensor_reduce(m["rounds"][:, :], need_row[:, :], AX.X, ALU.max))
            link(nc.vector.tensor_tensor(m["place_first"][:, :, :], dst_cols[:, :, :],
                                         low_b[:, :, None].broadcast_to([P, sh.G, TG]), ALU.subtract))

        @block.tensor
        def _(pe):
            pe.wait_ge(centred, 3)
            pe.wait_ge(made, 4)
            parts = [m["w1c"][:, 0:P], m["w1c"][:, P:H], w1e[:, 0:P], w1e[:, P:H], m["b1b"][:, 0:P], m["b1b"][:, P:H],
                     w2[:, 0, :], w2[:, 1, :], b2b[:, :]]
            for n, t in enumerate(parts):
                last = nc.tensor.matmul(turned[:, 4 * (n // 3) + n % 3, :], t, m["ident"][:, :], start=True, stop=True)
            last.then_inc(turned_ok, 1)
            pe.wait_ge(copied, 3)
            for n, left in ((0, 0), (1, 4), (2, 2)):
                for j in range(2):
                    nc.tensor.matmul(prods[:, n * ED:(n + 1) * ED], wt[:, left + j, :], wt[:, 2 + j, 0:ED],
                                     start=(j == 0), stop=(j == 1))
            for n in range(3):
                last = nc.tensor.matmul(prods[:, (n + 1) * D:(n + 2) * D], wt[:, 6 + n, :], m["wu"][:, 1, :],
                                        start=True, stop=True)
            last.then_inc(prods_ok, 1)


def node_table(nc, sh, a, m):
    with ExitStack() as ctx:
        def sb(name, shape, dt=F32):
            return ctx.enter_context(nc.sbuf_tensor(name, shape, dt))

        xt = sb("tab_xt", [D, 2, NB, P])
        row = sb("tab_row", [P, 2, NB, TR])
        pc = sb("tab_pc", [P, 2, H])
        ps_row = [ctx.enter_context(nc.psum_tensor(f"tab_ps_row{k}", [P, 512], F32)) for k in range(2)]
        ps_pc = [ctx.enter_context(nc.psum_tensor(f"tab_ps_pc{k}", [P, 512], F32)) for k in range(2)]
        x_in0, x_in1, multiplied, biased, squared, out0, out1, padded = semaphores(nc, m, "tab", [
            "x_in0", "x_in1", "multiplied", "biased", "squared", "row_out0", "row_out1", "padded"])
        x_in, row_out = [x_in0, x_in1], [out0, out1]
        block = ctx.enter_context(nc.Block())

        @block.sync
        def _(sp):
            def step(b, i, h):
                wait_for(sp, multiplied, b * NB - NB)
                carry(sp, m["went"][2])
                sp.dma_start(xt[:, h, :, :], a["xt"][:, bass.ds(b * (NB * P), NB * P)].rearrange(
                    "p (c n) -> p c n", n=P)).then_inc(x_in[h], 16)
            pair_steps(sp, sh.NT // NB, step)
            sp.wait_ge(m["acc_zeroed"], m["acc_zeroed_count"])

        @block.gpsimd
        def _(pool):
            nc.gpsimd.memset(row[:, :, :, TV + 1:TR], 0.0).then_inc(padded, 1)

        @block.tensor
        def _(pe):
            def step(c, i, j):
                h, k = j // NB, j % 2
                if j % NB == 0:
                    pe.wait_ge(x_in[h], i * 16 + 16)
                wait_for(pe, biased, c - 1)
                x = xt[:, h, j % NB, :]
                nc.tensor.matmul(ps_row[k][:, 0:TV], x, m["wtab"][:, :], start=True, stop=True)
                nc.tensor.matmul(ps_pc[k][:, 0:H], x, m["w1c"][:, :], start=True, stop=True).then_inc(multiplied, 1)
            tile_steps(pe, sh.NT, step)

        @block.vector
        def _(dve):
            def step(c, i, j):
                h, k = j // NB, j % 2
                dve.wait_ge(multiplied, c + 1)
                if j % NB == 0:
                    wait_for(dve, row_out[h], i * 16)
                wait_for(dve, squared, c - 1)
                nc.vector.tensor_tensor(row[:, h, j % NB, 0:TV], ps_row[k][:, 0:TV], m["btab"][:, :], ALU.add)
                nc.vector.tensor_tensor(pc[:, k, :], ps_pc[k][:, 0:H], m["b1b"][:, :], ALU.add).then_inc(biased, 1)
            tile_steps(dve, sh.NT, step)

        @block.scalar
        def _(act):
            act.wait_ge(padded, 1)

            def step(c, i, j):
                h, k = j // NB, j % 2
                act.wait_ge(biased, c + 1)
                nc.scalar.activation(pc[:, k, :], pc[:, k, :], ACT.Square, scale=H ** -0.5,
                                     accum_out=row[:, h, j % NB, TV:TV + 1]).then_inc(squared, 1)
                if j % NB == NB - 1:
                    act.wait_ge(squared, c + 1)
                    act.dma_start(m["table"][bass.ds((c - (NB - 1)) * P, NB * P), :].rearrange(
                        "(c p) r -> p c r", p=P), row[:, h, :, :]).then_inc(row_out[h], 16)
            tile_steps(act, sh.NT, step)
            for h in range(2):
                act.wait_ge(row_out[h], 16 * (sh.NT // (2 * NB)))


def window_add(nc, ctx, sh, m, name, acc, width, summed, ps_sum, act_went):
    held = ctx.enter_context(nc.sbuf_tensor(f"{name}_window", [WIN, 2, width], F32))
    in0, in1, out0, out1, added = semaphores(nc, m, "win", ["win_in0", "win_in1", "win_out0", "win_out1", "win_added"])
    win_in, win_out = [in0, in1], [out0, out1]

    def store(act, s, k):
        act.wait_ge(added, s + 1)
        carry(act, act_went)
        low = nc.scalar.value_load(m["low"][0:1, bass.ds(s, 1)], min_val=0, max_val=sh.NP)
        act.dma_start(acc[k % 2][bass.ds(low, WIN), :], held[:, k % 2, :]).then_inc(win_out[k % 2], 16)

    def start(act):
        for w in win_out:
            act.sem_inc(w, 16)

    def load(act, s, i, k):
        act.wait_ge(win_out[k % 2], i * 32 + 16 * (k // 2) + 16)
        carry(act, act_went)
        low = nc.scalar.value_load(m["low"][0:1, bass.ds(s, 1)], min_val=0, max_val=sh.NP)
        act.dma_start(held[:, k % 2, :], acc[k % 2][bass.ds(low, WIN), :]).then_inc(win_in[k % 2], 16)

    def add(dve, s, i, k):
        dve.wait_ge(summed, s + 1)
        dve.wait_ge(win_in[k % 2], i * 32 + 16 * (k // 2) + 16)
        nc.vector.tensor_tensor(held[:, k % 2, :], held[:, k % 2, :], ps_sum[k % 2][0:WIN, 0:width],
                                ALU.add).then_inc(added, 1)

    def stored(act):
        for p in range(2):
            act.wait_ge(win_out[p], 16 * (sh.G // 2) + 16)

    return start, store, load, add, stored, added, [in0, in1, out0, out1, added]


def earlier(s, i, k, lag):
    return s - lag, (i if k >= lag else i - 1), (k - lag) % RING


def message_pass(nc, sh, a, m):
    with ExitStack() as ctx:
        def sb(name, shape, dt=F32):
            return ctx.enter_context(nc.sbuf_tensor(name, shape, dt))

        idx = sb("msg_idx", [P, RING * TG], I32)
        ea_t = sb("msg_ea_t", [P, RING, CHUNK, P])
        ea_n = sb("msg_ea_n", [P, RING, TG, ED])
        rows = sb("msg_rows", [P, RING, TG, TR])
        prod = sb("msg_prod", [P, TG, ED])
        dot = sb("msg_dot", [P, 2, TG])
        var = sb("msg_var", [P, 2, TG])
        half = sb("msg_half", [P, 2, TG])
        guess = sb("msg_guess", [P, 2, TG], I32)
        shifted = sb("msg_shifted", [P, 2, TG], I32)
        root = sb("msg_root", [P, 2, 2, TG])
        work = sb("msg_work", [P, 2, TG])
        rstd = sb("msg_rstd", [P, 2, TG])
        hid = sb("msg_hid", [P, 2, TG, HC])
        onehot = sb("msg_onehot", [P, 2, TG, WIN])
        ps_e = ctx.enter_context(nc.psum_tensor("msg_ps_e", [P, 2, CHUNK, 512], F32))
        ps_sum = [ctx.enter_context(nc.psum_tensor(f"msg_ps_sum{k}", [P, 512], F32)) for k in range(2)]
        edges_in = semaphores(nc, m, "msg", [f"edges_in{k}" for k in range(RING)])
        pool_went, act_went, sp_went = m["went"]
        gathered = m["gathered"]
        (ea_done, joined, stat, var_ok, newton, scaled, activated, placed, summed, ones_set) = own = semaphores(
            nc, m, "msg", ["ea_done", "joined", "stat", "var_ok", "newton", "scaled", "activated", "placed", "summed",
                             "ones_set"])
        start, store, load, add, stored, added, win_sems = window_add(nc, ctx, sh, m, "msg", m["acc"][0], HC, summed, ps_sum,
                                                               act_went)
        block = ctx.enter_context(nc.Block())

        @block.sync
        def _(sp):
            def step(s, i, k):
                wait_for(sp, var_ok, s - (RING - 1))
                carry(sp, m["went"][2])
                sp.dma_start(idx[:, k * TG:(k + 1) * TG],
                             a["src"][bass.ds(s * P, P), :]).then_inc(edges_in[k], 16)
                sp.dma_start(ea_t[:, k, :, :], a["ea_t"][bass.ds(s * P, P), :].rearrange("p (c e) -> p c e", c=CHUNK)
                             ).then_inc(edges_in[k], 16)
                sp.dma_start(ea_n[:, k, :, :], a["ea_n"][bass.ds(s * P, P), :].rearrange("p (t d) -> p t d", t=TG)
                             ).then_inc(edges_in[k], 16)
            ring_steps(sp, sh.G, step)

        @block.gpsimd
        def _(pool):
            nc.gpsimd.memset(hid[:, :, :, H:HC], 1.0).then_inc(ones_set, 1)

            def step(s, i, k):
                pool.wait_ge(edges_in[k], i * 48 + 48)
                wait_for(pool, scaled, s * NC_CH - NC_CH * (RING - 1))
                carry(pool, pool_went)
                for t in range(TG):
                    nc.gpsimd.indirect_dma_start(
                        rows[:, k, t, :], None, m["table"],
                        bass.IndirectOffsetOnAxis(idx[:, k * TG + t:k * TG + t + 1], axis=0)).then_inc(gathered[k][t], 16)
            ring_steps(pool, sh.G, step)

        @block.tensor
        def _(pe):
            def edge_part(s, i, k):
                pe.wait_ge(edges_in[k], i * 48 + 48)
                for c in range(NC_CH):
                    wait_for(pe, joined, s * NC_CH + (c - 1))
                    for j in range(CHUNK):
                        t = c * CHUNK + j
                        last = nc.tensor.matmul(ps_e[:, c % 2, j, 0:TV], ea_t[:, k, t // QK, :], m["wm"][:, t % QK, :],
                                                start=True, stop=True)
                    last.then_inc(ea_done, 1)

            def segment_sum(s, k):
                pe.wait_ge(placed, s + 1)
                wait_for(pe, added, s - 1)
                for c in range(NC_CH):
                    pe.wait_ge(activated, s * NC_CH + (c + 1))
                    for t in range(c * CHUNK, (c + 1) * CHUNK):
                        last = nc.tensor.matmul(ps_sum[k][0:WIN, 0:HC], onehot[:, k, t, :], hid[:, k, t, :],
                                                start=(t == 0), stop=(t == TG - 1))
                last.then_inc(summed, 1)

            def step(s, i, k):
                edge_part(s, i, k)
                if not isinstance(s, int) or s >= 3:
                    segment_sum(s - 3, (k - 3) % 2)
            ring_steps(pe, sh.G, step)
            segment_sum(sh.G - 3, 1)
            segment_sum(sh.G - 2, 0)
            segment_sum(sh.G - 1, 1)

        @block.vector
        def _(dve):
            def join(s, i, k, c):
                for t in range(c * CHUNK, (c + 1) * CHUNK):
                    dve.wait_ge(gathered[k][t], i * 16 + 16)
                dve.wait_ge(ea_done, s * NC_CH + (c + 1))
                r = rows[:, k, c * CHUNK:(c + 1) * CHUNK, 0:TV]
                nc.vector.tensor_tensor(r, r, ps_e[:, c % 2, :, 0:TV], ALU.add).then_inc(joined, 1)

            def var_products(s, i, k):
                dve.wait_ge(edges_in[k], i * 48 + 48)
                dve.wait_ge(joined, s * NC_CH + NC_CH)
                nc.vector.tensor_tensor(prod[:, :, :], rows[:, k, :, H:TV], ea_n[:, k, :, :], ALU.mult).then_inc(stat, 1)

            def var_dot(s):
                dve.wait_ge(stat, s * 3 + 1)
                nc.vector.tensor_reduce(dot[:, 0, :], prod[:, :, :], AX.X, ALU.add).then_inc(stat, 1)

            def var_row(s, k):
                dve.wait_ge(stat, s * 3 + 2)
                nc.vector.tensor_tensor(dot[:, 1, :], dot[:, 0, :], rows[:, k, :, TV], ALU.add).then_inc(stat, 1)

            def var_eps(s, k):
                dve.wait_ge(stat, s * 3 + 3)
                nc.vector.tensor_scalar(var[:, k % 2, :], dot[:, 1, :], EPS, EPS, ALU.add, ALU.max).then_inc(var_ok, 1)

            def root_shift(pair):
                dve.wait_ge(var_ok, pair * 2 + 2)
                nc.vector.tensor_scalar(half[:, :, :], var[:, :, :], -0.5, None, ALU.mult)
                nc.vector.tensor_scalar(shifted[:, :, :], var[:, :, :].bitcast(I32), 1, None,
                                        ALU.logical_shift_right).then_inc(newton, 1)

            def root_guess(pair):
                dve.wait_ge(newton, pair * NEWTON + 1)
                nc.vector.tensor_scalar(guess[:, :, :], shifted[:, :, :], -1.0, float(0x5f3759df), ALU.mult,
                                        ALU.add).then_inc(newton, 1)

            roots = [guess[:, :, :].bitcast(F32), root[:, 0, :, :], root[:, 1, :, :], rstd[:, :, :]]

            def root_square(pair, r):
                dve.wait_ge(newton, pair * NEWTON + (2 + 3 * r))
                nc.vector.tensor_tensor(work[:, :, :], roots[r], roots[r], ALU.mult).then_inc(newton, 1)

            def root_times(pair, r):
                dve.wait_ge(newton, pair * NEWTON + (3 + 3 * r))
                nc.vector.tensor_tensor(work[:, :, :], work[:, :, :], half[:, :, :], ALU.mult).then_inc(newton, 1)

            def root_step(pair, r):
                dve.wait_ge(newton, pair * NEWTON + (4 + 3 * r))
                if r == 2:
                    wait_for(dve, scaled, pair * 2 * NC_CH)
                nc.vector.scalar_tensor_tensor(out=roots[r + 1], in0=work[:, :, :], scalar=1.5, in1=roots[r],
                                               op0=ALU.add, op1=ALU.mult).then_inc(newton, 1)

            def place(s, k):
                wait_for(dve, summed, s - 1)
                nc.vector.tensor_tensor(onehot[:, k % 2, :, :], m["iota"][:, None, :].broadcast_to([P, TG, WIN]),
                                        m["place"][:, bass.ds(s * TG, TG)][:, :, None].broadcast_to([P, TG, WIN]),
                                        ALU.is_equal).then_inc(placed, 1)

            def scale(s, k, pair, t):
                if t == 0:
                    dve.wait_ge(newton, pair * NEWTON + NEWTON)
                    wait_for(dve, summed, s - 1)
                ins = nc.vector.scalar_tensor_tensor(
                    out=hid[:, k % 2, t, 0:H], in0=rows[:, k, t, 0:H], scalar=rstd[:, k % 2, t:t + 1],
                    in1=m["be1b"][:, :], op0=ALU.mult, op1=ALU.add)
                if t % CHUNK == CHUNK - 1:
                    ins.then_inc(scaled, 1)

            def even_step(s, i, k):
                pair = i * 2 + k // 2 - 1
                join(s, i, k, 0)
                root_shift(pair)
                join(s, i, k, 1)
                root_guess(pair)
                if not isinstance(s, int):
                    add(dve, *earlier(s, i, k, 4))
                root_square(pair, 0)
                place(s - 2, k)
                root_times(pair, 0)
                join(s, i, k, 2)
                root_step(pair, 0)
                join(s, i, k, 3)
                root_square(pair, 1)
                var_products(s, i, k)
                root_times(pair, 1)
                var_dot(s)
                root_step(pair, 1)
                var_row(s, k)
                root_square(pair, 2)
                var_eps(s, k)
                root_times(pair, 2)
                root_step(pair, 2)
                for t in range(TG):
                    scale(s - 2, (k - 2) % RING, pair, t)

            def odd_step(s, i, k):
                pair = i * 2 + k // 2 - 1
                kl = (k - 2) % RING
                join(s, i, k, 0)
                scale(s - 2, kl, pair, 0)
                join(s, i, k, 1)
                scale(s - 2, kl, pair, 1)
                if not isinstance(s, int):
                    add(dve, *earlier(s, i, k, 4))
                place(s - 2, k)
                scale(s - 2, kl, pair, 2)
                join(s, i, k, 2)
                scale(s - 2, kl, pair, 3)
                join(s, i, k, 3)
                scale(s - 2, kl, pair, 4)
                var_products(s, i, k)
                scale(s - 2, kl, pair, 5)
                var_dot(s)
                scale(s - 2, kl, pair, 6)
                var_row(s, k)
                scale(s - 2, kl, pair, 7)
                var_eps(s, k)

            def step(s, i, k):
                if isinstance(s, int) and s < 2:
                    for c in range(NC_CH):
                        join(s, i, k, c)
                    var_products(s, i, k)
                    var_dot(s)
                    var_row(s, k)
                    var_eps(s, k)
                elif k % 2 == 0:
                    even_step(s, i, k)
                else:
                    odd_step(s, i, k)
            ring_steps(dve, sh.G, step)
            n, last_pair = sh.G // RING, sh.G // 2 - 1
            add(dve, sh.G - 4, n - 1, 0)
            add(dve, sh.G - 3, n - 1, 1)
            root_shift(last_pair)
            root_guess(last_pair)
            for r in range(3):
                root_square(last_pair, r)
                root_times(last_pair, r)
                root_step(last_pair, r)
            for g in (sh.G - 2, sh.G - 1):
                place(g, g % RING)
                for t in range(TG):
                    scale(g, g % RING, last_pair, t)
            add(dve, sh.G - 2, n - 1, 2)
            add(dve, sh.G - 1, n - 1, 3)

        @block.scalar
        def _(act):
            def gelu(s, k):
                for c in range(NC_CH):
                    act.wait_ge(scaled, s * NC_CH + (c + 1))
                    h = hid[:, k % 2, c * CHUNK:(c + 1) * CHUNK, 0:H]
                    nc.scalar.activation(h, h, ACT.Gelu).then_inc(activated, 1)

            start(act)
            act.wait_ge(ones_set, 1)

            def step(s, i, k):
                if not isinstance(s, int):
                    store(act, s - 4, k)
                if not isinstance(s, int) or s >= 3:
                    load(act, *earlier(s, i, k, 3))
                if not isinstance(s, int) or s >= 2:
                    gelu(s - 2, k % 2)
            ring_steps(act, sh.G, step)
            n = sh.G // RING
            store(act, sh.G - 4, 0)
            load(act, sh.G - 3, n - 1, 1)
            store(act, sh.G - 3, 1)
            load(act, sh.G - 2, n - 1, 2)
            load(act, sh.G - 1, n - 1, 3)
            gelu(sh.G - 2, 0)
            gelu(sh.G - 1, 1)
            store(act, sh.G - 2, 0)
            store(act, sh.G - 1, 1)
            stored(act)
    return [*edges_in, *own, *win_sems]


def conv_pass(nc, sh, a, m, layer):
    name = f"conv{layer}"
    with ExitStack() as ctx:
        idx = ctx.enter_context(nc.sbuf_tensor(f"{name}_idx", [P, RING * TG], I32))
        rows = ctx.enter_context(nc.sbuf_tensor(f"{name}_rows", [P, RING, TG, D], F32))
        onehot = ctx.enter_context(nc.sbuf_tensor(f"{name}_onehot", [P, 2, TG, WIN], F32))
        ps_sum = [ctx.enter_context(nc.psum_tensor(f"{name}_ps_sum{k}", [P, 512], F32)) for k in range(2)]
        idx_in = semaphores(nc, m, "conv", [f"idx_in{k}" for k in range(RING)])
        pool_went, act_went, sp_went = m["went"]
        gathered = m["gathered"]
        placed, summed = own = semaphores(nc, m, "conv", ["placed", "summed"])
        start, store, load, add, stored, added, win_sems = window_add(nc, ctx, sh, m, name, m["acc"][1 + layer], D, summed,
                                                               ps_sum, act_went)
        block = ctx.enter_context(nc.Block())

        @block.sync
        def _(sp):
            def step(s, i, k):
                for t in range(TG):
                    wait_for(sp, gathered[k][t], i * 16)
                carry(sp, m["went"][2])
                sp.dma_start(idx[:, k * TG:(k + 1) * TG], a["src"][bass.ds(s * P, P), :]).then_inc(idx_in[k], 16)
            ring_steps(sp, sh.G, step)

        @block.gpsimd
        def _(pool):
            def step(s, i, k):
                pool.wait_ge(idx_in[k], i * 16 + 16)
                wait_for(pool, summed, s - (RING - 1))
                carry(pool, pool_went)
                for t in range(TG):
                    nc.gpsimd.indirect_dma_start(
                        rows[:, k, t, :], None, m["conv_table"][layer],
                        bass.IndirectOffsetOnAxis(idx[:, k * TG + t:k * TG + t + 1], axis=0)).then_inc(gathered[k][t], 16)
            ring_steps(pool, sh.G, step)

        @block.tensor
        def _(pe):
            def step(s, i, k):
                pe.wait_ge(placed, s + 1)
                wait_for(pe, added, s - 1)
                for t in range(TG):
                    pe.wait_ge(gathered[k][t], i * 16 + 16)
                    last = nc.tensor.matmul(ps_sum[k % 2][0:WIN, 0:D], onehot[:, k % 2, t, :], rows[:, k, t, :],
                                            start=(t == 0), stop=(t == TG - 1))
                last.then_inc(summed, 1)
            ring_steps(pe, sh.G, step)

        @block.vector
        def _(dve):
            def step(s, i, k):
                if not isinstance(s, int) or s >= 2:
                    add(dve, *earlier(s, i, k, 2))
                wait_for(dve, summed, s - 1)
                nc.vector.tensor_tensor(onehot[:, k % 2, :, :], m["iota"][:, None, :].broadcast_to([P, TG, WIN]),
                                        m["place"][:, bass.ds(s * TG, TG)][:, :, None].broadcast_to([P, TG, WIN]),
                                        ALU.is_equal).then_inc(placed, 1)
            ring_steps(dve, sh.G, step)
            n = sh.G // RING
            add(dve, sh.G - 2, n - 1, 2)
            add(dve, sh.G - 1, n - 1, 3)

        @block.scalar
        def _(act):
            start(act)

            def step(s, i, k):
                if not isinstance(s, int) or s >= 2:
                    store(act, s - 2, k)
                load(act, s, i, k)
            ring_steps(act, sh.G, step)
            store(act, sh.G - 2, 0)
            store(act, sh.G - 1, 1)
            stored(act)
    return [*idx_in, *own, *win_sems]


def rounds_of(nc, sh, m, one_round):
    reset, moved = semaphores(nc, m, "rounds", ["reset", "moved"])
    with nc.Block() as block:
        @block.vector
        def _(dve):
            nc.vector.tensor_copy(m["place"][:, :], m["place_first"][:, :, :].rearrange("p g t -> p (g t)")).then_inc(
                reset, 1)
            nc.vector.tensor_copy(m["low"][:, :], m["low_first"][:, :]).then_inc(reset, 1)
            dve.wait_ge(reset, 2)
    rounds = nc.values_load(m["rounds"][0:1, 0:1], min_val=1, max_val=sh.NP // WIN + 1,
                            skip_runtime_bounds_check_because="a group's dst lie in the nodes, so the spans do")
    with nc.Fori(0, rounds):
        used = one_round()
        with nc.Block() as block:
            @block.vector
            def _(dve):
                nc.vector.tensor_scalar(m["place"][:, :], m["place"][:, :], -float(WIN), None, ALU.add).then_inc(
                    moved, 1)
                nc.vector.tensor_scalar(m["low"][:, :], m["low"][:, :], WIN, sh.NP, ALU.add, ALU.min).then_inc(
                    moved, 1)
                dve.wait_ge(moved, 2)
        clear_all(nc, m, [*used, moved])
    clear(nc, [reset])


def halves_to_mean_rstd(nc, dve, link, st, mv, t1):
    link(nc.vector.tensor_tensor(mv[:, 0, :], st[:, :, 1], st[:, :, 4], ALU.add))
    link(nc.vector.tensor_scalar(mv[:, 0, :], mv[:, 0, :], 0.5, None, ALU.mult))
    link(nc.vector.tensor_tensor(t1[:, :], st[:, :, 1], mv[:, 0, :], ALU.subtract))
    link(nc.vector.tensor_tensor(t1[:, :], t1[:, :], t1[:, :], ALU.mult))
    link(nc.vector.tensor_tensor(mv[:, 1, :], st[:, :, 2], st[:, :, 5], ALU.add))
    link(nc.vector.tensor_scalar(mv[:, 1, :], mv[:, 1, :], 1.0 / D, EPS, ALU.mult, ALU.add))
    link(nc.vector.tensor_tensor(mv[:, 1, :], mv[:, 1, :], t1[:, :], ALU.add))


def minus_mean_rstd(nc, mv, rs):
    return nc.vector.scalar_tensor_tensor(out=mv[:, 0, :], in0=mv[:, 0, :], scalar=-1.0, in1=rs[:, :], op0=ALU.mult,
                                          op1=ALU.mult)


def node_update(nc, sh, a, m):
    NT = sh.NT
    u, st, mv, rs, t1 = m["u"], m["u_st"], m["u_mv"], m["u_rs"], m["u_t1"]
    with ExitStack() as c2:
        def sb2(name, shape, dt=F32):
            return c2.enter_context(nc.sbuf_tensor(name, shape, dt))

        ab = [sb2(f"upd_ab{p}", [P, 2, NB, HC]) for p in range(2)]
        xt = sb2("upd_xt", [D, 2, NB, P])
        s_cols = sb2("upd_cols", [P, 2, 2, P])
        bias = sb2("upd_bias", [P, 2 * NB, D])
        ps_t = [c2.enter_context(nc.psum_tensor(f"upd_ps_t{k}", [P, 512], F32)) for k in range(2)]
        ps_u = [c2.enter_context(nc.psum_tensor(f"upd_ps_u{k}", [P, 512], F32)) for k in range(2)]
        in0, in1, added, turned, copied, multiplied, based, made_u, stats_ok = semaphores(nc, m, "upd", [
            "in0", "in1", "added", "turned", "copied", "multiplied", "based", "made_u", "stats"])
        loaded = [in0, in1]
        block = c2.enter_context(nc.Block())

        @block.sync
        def _(sp):
            sp.dma_start(m["x2"][:, :, :], a["x_rows"]).then_inc(m["loaded_x"], 16)

            def step(b, i, h):
                wait_for(sp, made_u, b * NB - NB)
                carry(sp, m["went"][2])
                for p in range(2):
                    sp.dma_start(ab[p][:, h, :, :], m["acc"][0][p][bass.ds(b * (NB * P), NB * P), :].rearrange(
                        "(c p) r -> p c r", p=P)).then_inc(loaded[h], 16)
                sp.dma_start(xt[:, h, :, :], a["xt"][:, bass.ds(b * (NB * P), NB * P)].rearrange(
                    "p (c n) -> p c n", n=P)).then_inc(loaded[h], 16)
            pair_steps(sp, NT // NB, step)

        @block.vector
        def _(dve):
            def sums(b, i, h):
                dve.wait_ge(loaded[h], i * 48 + 48)
                nc.vector.tensor_tensor(ab[0][:, h, :, :], ab[0][:, h, :, :], ab[1][:, h, :, :], ALU.add).then_inc(
                    added, 1)
                dve.wait_ge(added, b + 1)
                nc.vector.tensor_copy(m["deg"][:, bass.ds(b * NB, NB)], ab[0][:, h, :, H])

            def base(c, j):
                nc.vector.scalar_tensor_tensor(out=bias[:, j, :], in0=m["w2u"][:, 2, :],
                                               scalar=ab[0][:, j // NB, j % NB, H:HC], in1=m["bub"][:, :],
                                               op0=ALU.mult, op1=ALU.add).then_inc(based, 1)

            def collect(c, j):
                dve.wait_ge(multiplied, c + 1)
                dve.wait_ge(based, c + 1)
                uc = u[:, bass.ds(c, 1), :].rearrange("p o d -> p (o d)")
                nc.vector.tensor_tensor(uc, ps_u[j % 2][:, 0:D], bias[:, j, :], ALU.add).then_inc(made_u, 1)

            def spread(c):
                dve.wait_ge(made_u, c + 1)
                uc = u[:, bass.ds(c, 1), :].rearrange("p o d -> p (o d)")
                nc.vector.bn_stats(st[:, bass.ds(c, 1), :].rearrange("p o d -> p (o d)"), uc).then_inc(stats_ok, 1)

            def step(c, i, j):
                if j % NB == 0:
                    sums(i * 2 + j // NB, i, j // NB)
                base(c, j)
                if not isinstance(c, int) or c >= 2:
                    spread(c - 2)
                if not isinstance(c, int) or c >= 1:
                    collect(c - 1, (j - 1) % (2 * NB))
            tile_steps(dve, NT, step)
            spread(NT - 2)
            collect(NT - 1, 2 * NB - 1)
            spread(NT - 1)
            dve.wait_ge(stats_ok, NT)

        @block.tensor
        def _(pe):
            def turn(b, c, j):
                if j % NB == 0:
                    pe.wait_ge(added, b + 1)
                wait_for(pe, copied, c - 1)
                for r in range(2):
                    last = nc.tensor.transpose(ps_t[j % 2][:, r * P:(r + 1) * P],
                                               ab[0][:, j // NB, j % NB, r * P:(r + 1) * P], m["ident"][:, :])
                last.then_inc(turned, 1)

            def multiply(c, j):
                pe.wait_ge(copied, c + 1)
                wait_for(pe, made_u, c - 1)
                k = j % 2
                nc.tensor.matmul(ps_u[k][:, 0:D], xt[:, j // NB, j % NB, :], m["wu"][:, 0, :], start=True, stop=False)
                for r in range(2):
                    last = nc.tensor.matmul(ps_u[k][:, 0:D], s_cols[:, k, r, :], m["w2u"][:, r, :],
                                            start=False, stop=(r == 1))
                last.then_inc(multiplied, 1)

            def step(c, i, j):
                turn(i * 2 + j // NB, c, j)
                if not isinstance(c, int) or c >= 1:
                    multiply(c - 1, (j - 1) % (2 * NB))
            tile_steps(pe, NT, step)
            multiply(NT - 1, 2 * NB - 1)

        @block.scalar
        def _(act):
            def step(c, i, j):
                act.wait_ge(turned, c + 1)
                wait_for(act, multiplied, c - 1)
                nc.scalar.activation(s_cols[:, j % 2, :, :].rearrange("p r d -> p (r d)"), ps_t[j % 2][:, 0:H],
                                     ACT.Copy).then_inc(copied, 1)
            tile_steps(act, NT, step)

    n_b = NT // NB
    chain, var_ok, rstd_ok, ready, normed, shifted, gelu_ok = semaphores(nc, m, "ln", [
        "chain", "var_ok", "rstd_ok", "ready", "normed", "shifted", "gelu"])
    with nc.Block() as block:
        @block.gpsimd
        def _(pool):
            pool.wait_ge(var_ok, 2)
            nc.gpsimd.tensor_tensor(rs[:, :], mv[:, 1, :], m["expo"][:, 0:NT], ALU.pow).then_inc(rstd_ok, 1)
            nc.gpsimd.tensor_tensor(m["dinv"][:, :], t1[:, :], m["expo"][:, 0:NT], ALU.pow).then_inc(rstd_ok, 1)
            pool.wait_ge(var_ok, 3)
            nc.gpsimd.tensor_tensor(rs[:, :], mv[:, 1, :], m["expo"][:, 0:NT], ALU.pow).then_inc(rstd_ok, 1)

        @block.scalar
        def _(act):
            def normalise(b):
                for c in range(b * NB, (b + 1) * NB):
                    last = nc.scalar.activation(u[:, c, :], u[:, c, :], ACT.Identity, bias=mv[:, 0, c:c + 1],
                                                scale=rs[:, c:c + 1])
                last.then_inc(normed, 1)

            def gelu(b):
                act.wait_ge(shifted, b + 1)
                t = u[:, b * NB:(b + 1) * NB, :]
                nc.scalar.activation(t, t, ACT.Gelu).then_inc(gelu_ok, 1)

            act.wait_ge(ready, 1)
            for b in range(n_b):
                normalise(b)
                if b >= 1:
                    gelu(b - 1)
            gelu(n_b - 1)

        @block.vector
        def _(dve):
            count = [0]

            def link(ins):
                count[0] += 1
                ins.then_inc(chain, 1)
                dve.wait_ge(chain, count[0])

            halves_to_mean_rstd(nc, dve, link, st, mv, t1)
            nc.vector.tensor_copy(mv[:, 0, :], mv[:, 0, :]).then_inc(var_ok, 1)
            nc.vector.tensor_scalar(t1[:, :], m["deg"][:, :], 1.0, None, ALU.add).then_inc(var_ok, 1)
            dve.wait_ge(rstd_ok, 1)
            minus_mean_rstd(nc, mv, rs).then_inc(ready, 1)

            def across(v):
                return v[:, None, :].broadcast_to([P, NB, D])

            def flat(t):
                return t.rearrange("p t d -> p (t d)")

            def affine(b):
                dve.wait_ge(normed, b + 1)
                t = u[:, b * NB:(b + 1) * NB, :]
                link(nc.vector.tensor_tensor(t, t, across(m["gub"]), ALU.mult))
                nc.vector.tensor_tensor(t, t, across(m["beub"]), ALU.add).then_inc(shifted, 1)

            def plus_2x(b):
                dve.wait_ge(gelu_ok, b + 1)
                r = slice(b * NB, (b + 1) * NB)
                link(nc.vector.scalar_tensor_tensor(out=flat(u[:, r, :]), in0=flat(m["x2"][:, r, :]), scalar=2.0,
                                                    in1=flat(u[:, r, :]), op0=ALU.mult, op1=ALU.add))
                for c in range(b * NB, (b + 1) * NB):
                    last = nc.vector.bn_stats(st[:, c, :], u[:, c, :])
                if b == n_b - 1:
                    link(last)

            dve.wait_ge(m["loaded_x"], 16)
            for b in range(n_b):
                affine(b)
                if b >= 2:
                    plus_2x(b - 2)
            plus_2x(n_b - 2)
            plus_2x(n_b - 1)
            dve.wait_ge(rstd_ok, 2)
            halves_to_mean_rstd(nc, dve, link, st, mv, t1)
            nc.vector.tensor_copy(mv[:, 0, :], mv[:, 0, :]).then_inc(var_ok, 1)
            dve.wait_ge(rstd_ok, 3)
            link(minus_mean_rstd(nc, mv, rs))


def conv_table(nc, sh, a, m, layer):
    NT = sh.NT
    name = f"ctab{layer}"
    with ExitStack() as ctx:
        def sb(n, shape, dt=F32):
            return ctx.enter_context(nc.sbuf_tensor(f"{name}_{n}", shape, dt))

        xr = sb("xr", [P, 2, NB, D])
        hs = sb("hs", [P, 2, D])
        out = sb("out", [P, 2, NB, D])
        ps_t = [ctx.enter_context(nc.psum_tensor(f"{name}_ps_t{k}", [P, 512], F32)) for k in range(2)]
        ps_h = [ctx.enter_context(nc.psum_tensor(f"{name}_ps_h{k}", [P, 512], F32)) for k in range(2)]
        normed, kept, turned, columns, multiplied, scaled, out0, out1 = own = semaphores(nc, m, "ctab", [
            "normed", "kept", "turned", "columns", "multiplied", "scaled", "out0", "out1"])
        row_out = [out0, out1]
        block = ctx.enter_context(nc.Block())

        @block.scalar
        def _(act):
            def normalise(c, i, j):
                wait_for(act, turned, c - (2 * NB - 1))
                if j % NB == 0:
                    wait_for(act, kept, i * 2 + (j // NB - 1))
                nc.scalar.activation(xr[:, j // NB, j % NB, :], m["u"][:, bass.ds(c, 1), :].rearrange("p o d -> p (o d)"),
                                     ACT.Identity, bias=m["u_mv"][:, 0, bass.ds(c, 1)],
                                     scale=m["u_rs"][:, bass.ds(c, 1)]).then_inc(normed, 1)

            def columns_of(c, k):
                wait_for(act, multiplied, c - 1)
                if layer == 0:
                    act.wait_ge(turned, c + 1)
                    nc.scalar.activation(hs[:, k, :], ps_t[k][:, 0:D], ACT.Copy).then_inc(columns, 1)
                else:
                    nc.scalar.activation(hs[:, k, :], m["cols"][:, bass.ds(c * P, P)], ACT.Relu,
                                         bias=m["shift"][:, 0:1], scale=m["gain"][:, 0:1]).then_inc(columns, 1)

            def step(c, i, j):
                if layer == 0:
                    normalise(c, i, j)
                    if not isinstance(c, int) or c >= 1:
                        columns_of(c - 1, (j - 1) % 2)
                else:
                    columns_of(c, j % 2)
            tile_steps(act, NT, step)
            if layer == 0:
                columns_of(NT - 1, 1)

        @block.tensor
        def _(pe):
            def turn(c, j):
                pe.wait_ge(normed, c + 1)
                wait_for(pe, columns, c - 1)
                nc.tensor.transpose(ps_t[j % 2][:, 0:D], xr[:, j // NB, j % NB, :], m["ident"][:, :]).then_inc(
                    turned, 1)

            def multiply(c, k):
                pe.wait_ge(columns, c + 1)
                wait_for(pe, scaled, c - 1)
                nc.tensor.matmul(ps_h[k][:, 0:D], hs[:, k, :], m["wc"][:, layer, :], start=True,
                                 stop=True).then_inc(multiplied, 1)

            def step(c, i, j):
                if layer == 0:
                    turn(c, j)
                    if not isinstance(c, int) or c >= 1:
                        multiply(c - 1, (j - 1) % 2)
                else:
                    multiply(c, j % 2)
            pe.wait_ge(m["loaded_conv"], 16 * 8)
            tile_steps(pe, NT, step)
            if layer == 0:
                multiply(NT - 1, 1)

        @block.vector
        def _(dve):
            def keep(b, h):
                nc.vector.tensor_copy(m["x2"][:, bass.ds(b * NB, NB), :], xr[:, h, :, :]).then_inc(kept, 1)

            def step(c, i, j):
                if j % NB == 0:
                    wait_for(dve, row_out[j // NB], i * 16)
                dve.wait_ge(multiplied, c + 1)
                nc.vector.tensor_scalar(out[:, j // NB, j % NB, :], ps_h[j % 2][:, 0:D], m["dinv"][:, bass.ds(c, 1)],
                                        None, ALU.mult).then_inc(scaled, 1)
                if layer == 0 and j % NB == NB - 1:
                    keep(i * 2 + j // NB, j // NB)
            tile_steps(dve, NT, step)

        @block.sync
        def _(sp):
            def step(b, i, h):
                sp.wait_ge(scaled, b * NB + NB)
                carry(sp, m["went"][2])
                sp.dma_start(m["conv_table"][layer][bass.ds(b * (NB * P), NB * P), :].rearrange(
                    "(c p) d -> p c d", p=P), out[:, h, :, :]).then_inc(row_out[h], 16)
            pair_steps(sp, NT // NB, step)
            for h in range(2):
                sp.wait_ge(row_out[h], 16 * (NT // (2 * NB)))
    return own


def batch_norm(nc, sh, a, m, layer):
    NT = sh.NT
    name = f"bn{layer}"
    with ExitStack() as ctx:
        def sb(n, shape, dt=F32):
            return ctx.enter_context(nc.sbuf_tensor(f"{name}_{n}", shape, dt))

        parts = [sb(f"part{p}", [P, 2, NB, D]) for p in range(3)]
        n_s = sh.N // sh.BN
        st = sb("st", [P, n_s, 6])
        mv = sb("mv", [P, 2])
        rs = sb("rs", [P, 2])
        ps_c = [ctx.enter_context(nc.psum_tensor(f"{name}_ps_c{k}", [P, 512], F32)) for k in range(2)]
        in0, in1, summed, scaled, turned, filled, chain, var_ok, rstd_ok = own = semaphores(nc, m, "bn", [
            "in0", "in1", "summed", "scaled", "turned", "filled", "chain", "var_ok", "rstd_ok"])
        loaded = [in0, in1]
        block = ctx.enter_context(nc.Block())

        @block.sync
        def _(sp):
            def step(b, i, h):
                wait_for(sp, turned, b * NB - NB)
                carry(sp, m["went"][2])
                for part, source in zip(parts, (*m["acc"][1 + layer], m["conv_table"][layer])):
                    sp.dma_start(part[:, h, :, :], source[bass.ds(b * (NB * P), NB * P), :].rearrange(
                        "(c p) d -> p c d", p=P)).then_inc(loaded[h], 16)
            pair_steps(sp, NT // NB, step)

        @block.tensor
        def _(pe):
            def step(c, i, j):
                if j % NB == 0:
                    pe.wait_ge(scaled, i * 2 + (j // NB + 1))
                wait_for(pe, filled, c - 1)
                nc.tensor.transpose(ps_c[j % 2][:, 0:P], parts[0][:, j // NB, j % NB, :], m["ident"][:, :]).then_inc(
                    turned, 1)
            tile_steps(pe, NT, step)

        @block.scalar
        def _(act):
            def step(c, i, j):
                act.wait_ge(turned, c + 1)
                nc.scalar.activation(m["cols"][:, bass.ds(c * P, P)], ps_c[j % 2][:, 0:P], ACT.Identity,
                                     bias=m["colc"][:, layer, 0:1]).then_inc(filled, 1)
            act.wait_ge(m["loaded_conv"], 16 * 8)
            tile_steps(act, NT, step)

        @block.gpsimd
        def _(pool):
            pool.wait_ge(var_ok, 1)
            nc.gpsimd.tensor_tensor(rs[:, 0:1], mv[:, 1:2], m["expo"][:, 0:1], ALU.pow).then_inc(rstd_ok, 1)

        @block.vector
        def _(dve):
            def step(b, i, h):
                dve.wait_ge(loaded[h], i * 48 + 48)
                t = parts[0][:, h, :, :]
                for n in (1, 2):
                    nc.vector.tensor_tensor(t, t, parts[n][:, h, :, :], ALU.add).then_inc(summed, 1)
                    dve.wait_ge(summed, b * 2 + n)
                nc.vector.tensor_tensor(t, t, m["dinv"][:, bass.ds(b * NB, NB)][:, :, None].broadcast_to([P, NB, D]),
                                        ALU.mult).then_inc(scaled, 1)
            pair_steps(dve, NT // NB, step)
            count = [0]

            def link(ins):
                count[0] += 1
                ins.then_inc(chain, 1)
                dve.wait_ge(chain, count[0])

            dve.wait_ge(filled, NT)
            for j in range(n_s):
                last = nc.vector.bn_stats(st[:, j, :], m["cols"][:, j * sh.BN:(j + 1) * sh.BN])
            link(last)
            link(nc.vector.bn_aggr(mv[:, :], st[:, :, :].rearrange("p j s -> p (j s)")))
            nc.vector.tensor_scalar(mv[:, 1:2], mv[:, 1:2], EPS, None, ALU.add).then_inc(var_ok, 1)
            dve.wait_ge(rstd_ok, 1)
            link(nc.vector.tensor_tensor(m["gain"][:, :], rs[:, 0:1], m["colc"][:, layer, 1:2], ALU.mult))
            link(nc.vector.tensor_tensor(rs[:, 1:2], mv[:, 0:1], m["gain"][:, :], ALU.mult))
            link(nc.vector.tensor_tensor(m["shift"][:, :], m["colc"][:, layer, 2:3], rs[:, 1:2], ALU.subtract))
    return own


def last_norm(nc, sh, a, m, out):
    NT = sh.NT
    full = sh.N // P
    rest = sh.N - full * P
    with ExitStack() as ctx:
        def sb(n, shape, dt=F32):
            return ctx.enter_context(nc.sbuf_tensor(f"fin_{n}", shape, dt))

        hs = sb("hs", [P, 2, P])
        st = sb("st", [P, NT, 6])
        mv = sb("mv", [P, 2, NT])
        rs = sb("rs", [P, NT])
        t1 = sb("t1", [P, NT])
        ps_y = [ctx.enter_context(nc.psum_tensor(f"fin_ps_y{k}", [P, 512], F32)) for k in range(2)]
        clipped, turned, joined, stats_ok, chain, var_ok, rstd_ok, ready, normed, out_ok = semaphores(nc, m, "fin", [
            "clipped", "turned", "joined", "stats", "chain", "var_ok", "rstd_ok", "ready", "normed", "out"])
        block = ctx.enter_context(nc.Block())
        n_b = NT // NB

        @block.scalar
        def _(act):
            def step(c, i, k):
                wait_for(act, turned, c - 1)
                nc.scalar.activation(hs[:, k, :], m["cols"][:, bass.ds(c * P, P)], ACT.Relu,
                                     bias=m["shift"][:, 0:1], scale=m["gain"][:, 0:1]).then_inc(clipped, 1)
            pair_steps(act, NT, step)
            act.wait_ge(ready, 1)
            for b in range(n_b):
                for c in range(b * NB, (b + 1) * NB):
                    last = nc.scalar.activation(m["x2"][:, c, :], m["x2"][:, c, :], ACT.Identity,
                                                bias=mv[:, 0, c:c + 1], scale=rs[:, c:c + 1])
                last.then_inc(normed, 1)

        @block.tensor
        def _(pe):
            def step(c, i, k):
                pe.wait_ge(clipped, c + 1)
                wait_for(pe, joined, c - 1)
                nc.tensor.transpose(ps_y[k][:, 0:D], hs[:, k, :], m["ident"][:, :]).then_inc(turned, 1)
            pair_steps(pe, NT, step)

        @block.gpsimd
        def _(pool):
            pool.wait_ge(var_ok, 1)
            nc.gpsimd.tensor_tensor(rs[:, :], mv[:, 1, :], m["expo"][:, 0:NT], ALU.pow).then_inc(rstd_ok, 1)

        @block.vector
        def _(dve):
            def step(c, i, k):
                dve.wait_ge(turned, c + 1)
                xc = m["x2"][:, bass.ds(c, 1), :].rearrange("p o d -> p (o d)")
                nc.vector.scalar_tensor_tensor(out=xc, in0=xc, scalar=2.0, in1=ps_y[k][:, 0:D], op0=ALU.mult,
                                               op1=ALU.add).then_inc(joined, 1)
                dve.wait_ge(joined, c + 1)
                nc.vector.bn_stats(st[:, bass.ds(c, 1), :].rearrange("p o d -> p (o d)"), xc).then_inc(stats_ok, 1)
            pair_steps(dve, NT, step)
            dve.wait_ge(stats_ok, NT)
            count = [0]

            def link(ins):
                count[0] += 1
                ins.then_inc(chain, 1)
                dve.wait_ge(chain, count[0])

            halves_to_mean_rstd(nc, dve, link, st, mv, t1)
            nc.vector.tensor_copy(mv[:, 0, :], mv[:, 0, :]).then_inc(var_ok, 1)
            dve.wait_ge(rstd_ok, 1)
            minus_mean_rstd(nc, mv, rs).then_inc(ready, 1)

        @block.sync
        def _(sp):
            stores = 0
            for b in range(n_b):
                sp.wait_ge(normed, b + 1)
                first, last = b * NB, min((b + 1) * NB, full)
                if last > first:
                    sp.dma_start(out[first * P:last * P, :].rearrange("(c p) d -> p c d", p=P),
                                 m["x2"][:, first:last, :]).then_inc(out_ok, 16)
                    stores += 1
            if rest:
                sp.dma_start(out[full * P:sh.N, :], m["x2"][0:rest, full, :]).then_inc(out_ok, 16)
                stores += 1
            sp.wait_ge(out_ok, 16 * stores)


def build(nc, a, out, n_nodes, n_groups):
    sh = Shape(n_nodes, n_groups)
    NT = sh.NT
    with ExitStack() as ctx:
        def sb(name, shape, dt=F32):
            return ctx.enter_context(nc.sbuf_tensor(name, shape, dt))

        def dram(name, shape, dt=F32):
            return nc.dram_tensor(name, shape, dt, kind="Internal").ap()

        m = {
            "sems": {}, "ident": sb("ident", [P, P]), "iota": sb("iota", [P, WIN]), "expo": sb("expo", [P, max(NT, TG)]),
            "w1c": sb("w1c", [P, H]), "wtab": sb("wtab", [P, TV]), "btab": sb("btab", [P, TV]),
            "wm": sb("wm", [P, QK, TV]), "w2u": sb("w2u", [P, 3, D]), "wu": sb("wu", [P, 2, D]),
            "wc": sb("wc", [P, 2, D]), "colc": sb("colc", [P, 2, 3]),
            "b1b": sb("b1b", [P, H]), "g1b": sb("g1b", [P, H]), "be1b": sb("be1b", [P, H]),
            "bub": sb("bub", [P, D]), "gub": sb("gub", [P, D]), "beub": sb("beub", [P, D]),
            "place_first": sb("place_first", [P, sh.G, TG]), "place": sb("place", [P, sh.G * TG]),
            "low_first": sb("low_first", [1, sh.G], I32), "low": sb("low", [1, sh.G], I32),
            "rounds": sb("rounds", [1, 1], I32), "deg": sb("deg", [P, NT]), "dinv": sb("dinv", [P, NT]),
            "zeros": sb("zeros", [P, 4 * HC]), "acc_zeroed_count": 0,
            "gain": sb("gain", [P, 1]), "shift": sb("shift", [P, 1]),
            "low_dram": dram("low_dram", [sh.G], I32), "need_dram": dram("need_dram", [sh.G], I32),
            "table": dram("table", [sh.NP, TR]),
            "conv_table": [dram(f"conv_table{j}", [sh.NP, D]) for j in range(2)],
            "acc": [[dram(f"acc{j}_{p}", [sh.ACC, HC if j == 0 else D]) for p in range(2)] for j in range(3)],
        }
        gathered = semaphores(nc, m, "all", [f"gathered{n}" for n in range(RING * TG)])
        m["went"] = semaphores(nc, m, "all", ["pool_went", "act_went", "sp_went"])
        m["gathered"] = [gathered[k * TG:(k + 1) * TG] for k in range(RING)]
        m["loaded_conv"], m["loaded_x"], m["acc_zeroed"], conv_zeroed = semaphores(nc, m, "all", [
            "loaded_conv", "loaded_x", "acc_zeroed", "conv_zeroed"])
        prepare(nc, sh, a, m)
        node_table(nc, sh, a, m)
        zeroings = 0
        with nc.Block() as block:
            @block.sync
            def _(sp):
                nonlocal zeroings
                for acc in (*m["acc"][1], *m["acc"][2]):
                    for b in range(NT // NB):
                        sp.dma_start(acc[b * NB * P:(b + 1) * NB * P, :].rearrange("(p k) c -> p (k c)", p=P),
                                     m["zeros"][:, 0:NB * D]).then_inc(conv_zeroed, 16)
                    sp.dma_start(acc[sh.NP:sh.ACC, :], m["zeros"][0:WIN, 0:D]).then_inc(conv_zeroed, 16)
                    zeroings += NT // NB + 1
        rounds_of(nc, sh, m, lambda: message_pass(nc, sh, a, m))
        m["x2"] = sb("x2", [P, NT, D])
        with ExitStack() as uctx:
            for n, shape in (("u", [P, NT, D]), ("u_st", [P, NT, 6]), ("u_mv", [P, 2, NT]), ("u_rs", [P, NT]),
                             ("u_t1", [P, NT])):
                m[n] = uctx.enter_context(nc.sbuf_tensor(n, shape, F32))
            node_update(nc, sh, a, m)
            clear(nc, conv_table(nc, sh, a, m, 0))
        with nc.Block() as block:
            @block.sync
            def _(sp):
                sp.wait_ge(conv_zeroed, 16 * zeroings)
        m["cols"] = sb("cols", [P, sh.NP])
        rounds_of(nc, sh, m, lambda: conv_pass(nc, sh, a, m, 0))
        clear(nc, batch_norm(nc, sh, a, m, 0))
        conv_table(nc, sh, a, m, 1)
        rounds_of(nc, sh, m, lambda: conv_pass(nc, sh, a, m, 1))
        batch_norm(nc, sh, a, m, 1)
        last_norm(nc, sh, a, m, out)


def lay_out(x, src, dst, edge_attr):
    import numpy as np
    n, e = x.shape[0], src.shape[0]
    nt = -(-n // P)
    g = RING * -(-e // (GE * RING))
    pad = g * GE - e
    src = np.concatenate([src, np.zeros(pad, src.dtype)])
    dst = np.concatenate([dst, np.full(pad, n, dst.dtype)])
    ea = np.concatenate([edge_attr, np.zeros((pad, ED), edge_attr.dtype)])
    xp = np.concatenate([x, np.zeros((nt * P - n, D), x.dtype)])
    c = np.ascontiguousarray
    return g, {
        "in_src": c(src.reshape(g * P, TG)),
        "in_dst_rows": c(dst.reshape(g // RING, RING, GE)),
        "in_dst_cols": c(dst.reshape(g, P, TG).transpose(1, 0, 2)),
        "in_ea_n": c(ea.reshape(g * P, TG * ED)),
        "in_ea_t": c(ea.reshape(g, P, TG // QK, QK, ED).transpose(0, 3, 4, 2, 1).reshape(g * P, TG // QK * P)),
        "in_xt": c(xp.T),
        "in_x_rows": c(xp.reshape(nt, P, D).transpose(1, 0, 2)),
    }


_WEIGHTS = ["L0_gnn_W1", "L0_gnn_b1", "L0_gnn_g1", "L0_gnn_be1", "L0_gnn_W2", "L0_gnn_b2", "L0_gnn_Wu", "L0_gnn_bu",
            "L0_gnn_gu", "L0_gnn_beu", "L1_gnn_W0", "L1_gnn_b0", "L1_gnn_g0", "L1_gnn_be0", "L1_gnn_W1", "L1_gnn_b1",
            "L1_gnn_g1", "L1_gnn_be1"]


def kernel(x, src, dst, edge_attr_32, **weights):
    import numpy as np
    import concourse.bacc as bacc
    from concourse.bass_utils import run_bass_kernel_spmd

    g, arrays = lay_out(np.asarray(x), np.asarray(src), np.asarray(dst), np.asarray(edge_attr_32))
    for w in _WEIGHTS:
        arrays[f"in_{w}"] = np.ascontiguousarray(np.asarray(weights[w]))
    nc = bacc.Bacc("TRN2", target_bir_lowering=False, num_devices=1)
    t = {n: nc.dram_tensor(n, v.shape, mybir.dt.from_np(v.dtype), kind="ExternalInput").ap()
         for n, v in arrays.items()}
    a = {k: t[f"in_{k}"] for k in ("src", "dst_rows", "dst_cols", "ea_n", "ea_t", "xt", "x_rows")}
    a.update({k: t[f"in_L0_gnn_{k}"] for k in ("W1", "b1", "g1", "be1", "W2", "b2", "Wu", "bu", "gu", "beu")})
    a["Wc"] = [t["in_L1_gnn_W0"], t["in_L1_gnn_W1"]]
    a["colc"] = [[t[f"in_L1_gnn_{r}{j}"] for r in ("b", "g", "be")] for j in range(2)]
    out = nc.dram_tensor("out", [x.shape[0], D], F32, kind="ExternalOutput").ap()
    build(nc, a, out, x.shape[0], g)
    r = run_bass_kernel_spmd(nc, [arrays], core_ids=[0])
    return r.results[0]["out"]
```

```python
import concourse.bass as bass
from concourse import mybir
from contextlib import ExitStack

F32 = mybir.dt.float32
I32 = mybir.dt.int32
ALU = mybir.AluOpType
ACT = mybir.ActivationFunctionType
AX = mybir.AxisListType

P = 128
TG = 8
GE = TG * P
WIN = 64
WIN_SHIFT = 6
RING = 4
CHUNK = 2
NC_CH = TG // CHUNK
DVE_CH = NC_CH // 2
D = 128
ED = 32
H = 256
TV = H + ED
TR = 320
HC = H + 1
QK = P // ED
EPS = 1e-5
NEWTON = 2 + 3 * 3
NB = 7


def wait_for(engine, sem, count):
    if isinstance(count, int) and count <= 0:
        return
    engine.wait_ge(sem, count)


def carry(engine, sem):
    engine.sem_inc(sem, 1)


def ring_steps(engine, n, step):
    for k in range(RING):
        step(k, 0, k)
    with engine.Fori(1, n // RING) as i:
        for k in range(RING):
            step(i * RING + k, i, k)


def pair_steps(engine, n, step):
    for k in range(2):
        step(k, 0, k)
    with engine.Fori(1, n // 2) as i:
        for k in range(2):
            step(i * 2 + k, i, k)


def tile_steps(engine, n, step):
    for j in range(2 * NB):
        step(j, 0, j)
    with engine.Fori(1, n // (2 * NB)) as i:
        for j in range(2 * NB):
            step(i * (2 * NB) + j, i, j)


class Shape:
    def __init__(self, n_nodes, n_groups):
        self.N = n_nodes
        self.NT = -(-n_nodes // P)
        self.NP = self.NT * P
        self.G = n_groups
        self.GP = n_groups // RING
        self.ACC = self.NP + WIN
        self.BN = max(d for d in range(1, 513) if n_nodes % d == 0)


def semaphores(nc, m, prefix, names):
    for n in names:
        if f"{prefix}_{n}" not in m["sems"]:
            m["sems"][f"{prefix}_{n}"] = nc.alloc_semaphore(name=f"{prefix}_{n}")
    return [m["sems"][f"{prefix}_{n}"] for n in names]


def clear(nc, sems):
    for s in sems:
        nc.sync.sem_clear(s)
    nc.all_engine_barrier()


def clear_all(nc, m, sems):
    nc.gpsimd.drain()
    gathered = [s for slot in m["gathered"] for s in slot]
    nums = [s.num for s in gathered]
    assert nums == list(range(nums[0], nums[-1] + 1))
    nc.gpsimd.dma_reset(range(nums[0], nums[-1] + 1))
    nc.all_engine_barrier()
    clear(nc, [*sems, *gathered])


def prepare(nc, sh, a, m):
    with ExitStack() as ctx:
        def sb(name, shape, dt=F32):
            return ctx.enter_context(nc.sbuf_tensor(name, shape, dt))

        w1x = sb("w1x", [P, H])
        w1e = sb("w1e", [P, H])
        b2b = sb("b2b", [P, D])
        w2 = sb("w2", [P, 2, D])
        mean = sb("prep_mean", [P, 3])
        wt = sb("prep_transposed", [P, 9, P])
        dst_rows = sb("dst_rows", [sh.GP, RING, GE], I32)
        dst_cols = sb("dst_cols", [P, sh.G, TG], I32)
        low = sb("group_low", [sh.GP, RING], I32)
        high = sb("group_high", [sh.GP, RING], I32)
        span = sb("group_span", [sh.GP, RING], I32)
        shifted = sb("group_shifted", [sh.GP, RING], I32)
        need = sb("group_rounds", [sh.GP, RING], I32)
        low_b = sb("low_b", [P, sh.G], I32)
        need_row = sb("need_row", [1, sh.G], I32)
        iota_i = sb("iota_i", [P, WIN], I32)
        zeros, zeroed = m["zeros"], m["acc_zeroed"]
        turned = ctx.enter_context(nc.psum_tensor("prep_turned", [P, 12, P], F32))
        prods = ctx.enter_context(nc.psum_tensor("prep_prods", [P, 512], F32))
        (loaded_w, loaded_dst, zero_set, cleared, made, centred, turned_ok, copied, prods_ok, folded,
         range_ok, chain, range_out, range_in) = semaphores(nc, m, "prep", [
            "loaded_w", "loaded_dst", "zero_set", "cleared", "made", "centred", "turned", "copied", "prods",
            "folded", "range", "chain", "range_out", "range_in"])
        block = ctx.enter_context(nc.Block())
        n_w = 1 + QK + 7 + 2

        @block.sync
        def _(sp):
            sp.dma_start(dst_rows[:, :, :], a["dst_rows"]).then_inc(loaded_dst, 16)
            sp.dma_start(dst_cols[:, :, :], a["dst_cols"]).then_inc(loaded_dst, 16)
            sp.dma_start(w1x[:, :], a["W1"][0:D, :]).then_inc(loaded_w, 16)
            for q in range(QK):
                sp.dma_start(w1e[q * ED:(q + 1) * ED, :], a["W1"][D:D + ED, :]).then_inc(loaded_w, 16)
            for dst, src in ((m["b1b"], a["b1"]), (m["g1b"], a["g1"]), (m["be1b"], a["be1"]), (b2b, a["b2"]),
                             (m["bub"], a["bu"]), (m["gub"], a["gu"]), (m["beub"], a["beu"])):
                sp.dma_start(dst[:, :], src.partition_broadcast(P)).then_inc(loaded_w, 16)
            sp.dma_start(w2[:, :, :], a["W2"].rearrange("(j p) d -> p j d", p=P)).then_inc(loaded_w, 16)
            sp.dma_start(m["wu"][:, :, :], a["Wu"].rearrange("(j p) d -> p j d", p=P)).then_inc(loaded_w, 16)
            for j in range(2):
                sp.dma_start(m["wc"][:, j, :], a["Wc"][j]).then_inc(m["loaded_conv"], 16)
                for r in range(3):
                    sp.dma_start(m["colc"][:, j, r:r + 1], a["colc"][j][r].rearrange("(p o) -> p o", o=1)).then_inc(
                        m["loaded_conv"], 16)
            sp.wait_ge(range_ok, 2)
            sp.dma_start(m["low_dram"].rearrange("(p j) -> p j", j=RING), low[:, :]).then_inc(range_out, 16)
            sp.dma_start(m["need_dram"].rearrange("(p j) -> p j", j=RING), need[:, :]).then_inc(range_out, 16)
            sp.wait_ge(range_out, 32)
            sp.dma_start(m["low_first"][:, :], m["low_dram"].rearrange("(o g) -> o g", o=1)).then_inc(range_in, 16)
            sp.dma_start(need_row[:, :], m["need_dram"].rearrange("(o g) -> o g", o=1)).then_inc(range_in, 16)
            sp.dma_start(low_b[:, :], m["low_dram"].partition_broadcast(P)).then_inc(range_in, 16)

        @block.scalar
        def _(act):
            act.wait_ge(zero_set, 1)
            acc, *conv_acc = m["acc"]
            for r in range(0, sh.NT, 4):
                k = min(4, sh.NT - r)
                act.dma_start(acc[r * P:(r + k) * P, :].rearrange("(p k) c -> p (k c)", p=P),
                              zeros[:, 0:k * HC]).then_inc(zeroed, 16)
            act.dma_start(acc[sh.NP:sh.ACC, :], zeros[0:WIN, 0:HC]).then_inc(zeroed, 16)
            for other in conv_acc:
                act.dma_start(other[sh.NP:sh.ACC, :], zeros[0:WIN, 0:D]).then_inc(zeroed, 16)

        @block.gpsimd
        def _(pool):
            nc.gpsimd.memset(zeros[:, :], 0.0).then_inc(zero_set, 1)
            nc.gpsimd.memset(m["ident"][:, :], 0.0).then_inc(cleared, 1)
            pool.wait_ge(cleared, 1)
            nc.gpsimd.affine_select(out=m["ident"][:, :], in_=m["ident"][:, :], compare_op=ALU.not_equal, fill=1.0,
                                    base=0, pattern=[[-1, P]], channel_multiplier=1).then_inc(made, 1)
            nc.gpsimd.iota(iota_i[:, :], pattern=[[1, WIN]], base=0, channel_multiplier=0).then_inc(made, 1)
            nc.gpsimd.memset(m["wm"][:, :, :], 0.0).then_inc(made, 1)

        @block.vector
        def _(dve):
            count = [0]

            def link(ins):
                count[0] += 1
                ins.then_inc(chain, 1)
                dve.wait_ge(chain, count[0])

            dve.wait_ge(loaded_dst, 32)
            nc.vector.tensor_reduce(high[:, :], dst_rows[:, :, :], AX.X, ALU.max).then_inc(chain, 1)
            count[0] += 1
            nc.vector.tensor_reduce(low[:, :], dst_rows[:, :, :], AX.X, ALU.min).then_inc(range_ok, 1)
            dve.wait_ge(range_ok, 1)
            dve.wait_ge(chain, count[0])
            link(nc.vector.tensor_tensor(span[:, :], high[:, :], low[:, :], ALU.subtract))
            link(nc.vector.tensor_scalar(shifted[:, :], span[:, :], WIN_SHIFT, None, ALU.logical_shift_right))
            nc.vector.tensor_scalar(need[:, :], shifted[:, :], 1, None, ALU.add).then_inc(range_ok, 1)
            dve.wait_ge(made, 3)
            link(nc.vector.tensor_copy(m["iota"][:, :], iota_i[:, :]))
            dve.wait_ge(loaded_w, 16 * n_w)
            for j, t in enumerate((w1x, w1e, m["b1b"])):
                link(nc.vector.tensor_reduce(mean[:, j:j + 1], t[:, :], AX.X, ALU.add))
            link(nc.vector.tensor_scalar(mean[:, :], mean[:, :], -1.0 / H, None, ALU.mult))
            for j, (t, o) in enumerate(((w1x, m["w1c"]), (w1e, w1e), (m["b1b"], m["b1b"]))):
                nc.vector.tensor_scalar(o[:, :], t[:, :], mean[:, j:j + 1], None, ALU.add).then_inc(centred, 1)
            dve.wait_ge(turned_ok, 1)
            for r in range(3):
                nc.vector.tensor_copy(wt[:, 3 * r:3 * r + 3, :], turned[:, 4 * r:4 * r + 3, :]).then_inc(copied, 1)
            dve.wait_ge(centred, 3)
            link(nc.vector.tensor_tensor(m["wtab"][:, 0:H], m["w1c"][:, :], m["g1b"][:, :], ALU.mult))
            link(nc.vector.tensor_tensor(m["btab"][:, 0:H], m["b1b"][:, :], m["g1b"][:, :], ALU.mult))
            for q in range(QK):
                r = slice(q * ED, (q + 1) * ED)
                link(nc.vector.tensor_tensor(m["wm"][r, q, 0:H], w1e[r, :], m["g1b"][r, :], ALU.mult))
            dve.wait_ge(prods_ok, 1)
            nc.vector.tensor_scalar(m["wtab"][:, H:TV], prods[:, 0:ED], 2.0 / H, None, ALU.mult).then_inc(folded, 1)
            nc.vector.tensor_scalar(m["btab"][:, H:TV], prods[:, ED:2 * ED], 2.0 / H, None, ALU.mult).then_inc(folded, 1)
            for q in range(QK):
                r = slice(q * ED, (q + 1) * ED)
                nc.vector.tensor_scalar(m["wm"][r, q, H:TV], prods[r, 2 * ED:3 * ED], 1.0 / H, None,
                                        ALU.mult).then_inc(folded, 1)
            nc.vector.tensor_copy(m["w2u"][:, :, :], prods[:, D:4 * D].rearrange("p (j d) -> p j d", j=3)).then_inc(
                folded, 1)
            dve.wait_ge(range_in, 48)
            link(nc.vector.tensor_reduce(m["rounds"][:, :], need_row[:, :], AX.X, ALU.max))
            link(nc.vector.tensor_tensor(m["place_first"][:, :, :], dst_cols[:, :, :],
                                         low_b[:, :, None].broadcast_to([P, sh.G, TG]), ALU.subtract))

        @block.tensor
        def _(pe):
            pe.wait_ge(centred, 3)
            pe.wait_ge(made, 3)
            parts = [m["w1c"][:, 0:P], m["w1c"][:, P:H], w1e[:, 0:P], w1e[:, P:H], m["b1b"][:, 0:P], m["b1b"][:, P:H],
                     w2[:, 0, :], w2[:, 1, :], b2b[:, :]]
            for n, t in enumerate(parts):
                last = nc.tensor.matmul(turned[:, 4 * (n // 3) + n % 3, :], t, m["ident"][:, :], start=True, stop=True)
            last.then_inc(turned_ok, 1)
            pe.wait_ge(copied, 3)
            for n, left in ((0, 0), (1, 4), (2, 2)):
                for j in range(2):
                    nc.tensor.matmul(prods[:, n * ED:(n + 1) * ED], wt[:, left + j, :], wt[:, 2 + j, 0:ED],
                                     start=(j == 0), stop=(j == 1))
            for n in range(3):
                last = nc.tensor.matmul(prods[:, (n + 1) * D:(n + 2) * D], wt[:, 6 + n, :], m["wu"][:, 1, :],
                                        start=True, stop=True)
            last.then_inc(prods_ok, 1)


def node_table(nc, sh, a, m):
    with ExitStack() as ctx:
        def sb(name, shape, dt=F32):
            return ctx.enter_context(nc.sbuf_tensor(name, shape, dt))

        xt = sb("tab_xt", [D, 2, NB, P])
        row = sb("tab_row", [P, 2, NB, TR])
        pc = sb("tab_pc", [P, 2, H])
        ps_row = [ctx.enter_context(nc.psum_tensor(f"tab_ps_row{k}", [P, 512], F32)) for k in range(2)]
        ps_pc = [ctx.enter_context(nc.psum_tensor(f"tab_ps_pc{k}", [P, 512], F32)) for k in range(2)]
        x_in0, x_in1, multiplied, biased, squared, out0, out1, padded = semaphores(nc, m, "tab", [
            "x_in0", "x_in1", "multiplied", "biased", "squared", "row_out0", "row_out1", "padded"])
        x_in, row_out = [x_in0, x_in1], [out0, out1]
        block = ctx.enter_context(nc.Block())

        @block.sync
        def _(sp):
            def step(b, i, h):
                wait_for(sp, multiplied, b * NB - NB)
                carry(sp, m["went"][2])
                sp.dma_start(xt[:, h, :, :], a["xt"][:, bass.ds(b * (NB * P), NB * P)].rearrange(
                    "p (c n) -> p c n", n=P)).then_inc(x_in[h], 16)
            pair_steps(sp, sh.NT // NB, step)
            sp.wait_ge(m["acc_zeroed"], 16 * (-(-sh.NT // 4) + 3))

        @block.gpsimd
        def _(pool):
            nc.gpsimd.memset(row[:, :, :, TV + 1:TR], 0.0).then_inc(padded, 1)

        @block.tensor
        def _(pe):
            def step(c, i, j):
                h, k = j // NB, j % 2
                if j % NB == 0:
                    pe.wait_ge(x_in[h], i * 16 + 16)
                wait_for(pe, biased, c - 1)
                x = xt[:, h, j % NB, :]
                nc.tensor.matmul(ps_row[k][:, 0:TV], x, m["wtab"][:, :], start=True, stop=True)
                nc.tensor.matmul(ps_pc[k][:, 0:H], x, m["w1c"][:, :], start=True, stop=True).then_inc(multiplied, 1)
            tile_steps(pe, sh.NT, step)

        @block.vector
        def _(dve):
            def step(c, i, j):
                h, k = j // NB, j % 2
                dve.wait_ge(multiplied, c + 1)
                if j % NB == 0:
                    wait_for(dve, row_out[h], i * 16)
                wait_for(dve, squared, c - 1)
                nc.vector.tensor_tensor(row[:, h, j % NB, 0:TV], ps_row[k][:, 0:TV], m["btab"][:, :], ALU.add)
                nc.vector.tensor_tensor(pc[:, k, :], ps_pc[k][:, 0:H], m["b1b"][:, :], ALU.add).then_inc(biased, 1)
            tile_steps(dve, sh.NT, step)

        @block.scalar
        def _(act):
            act.wait_ge(padded, 1)

            def step(c, i, j):
                h, k = j // NB, j % 2
                act.wait_ge(biased, c + 1)
                nc.scalar.activation(pc[:, k, :], pc[:, k, :], ACT.Square, scale=H ** -0.5,
                                     accum_out=row[:, h, j % NB, TV:TV + 1]).then_inc(squared, 1)
                if j % NB == NB - 1:
                    act.wait_ge(squared, c + 1)
                    act.dma_start(m["table"][bass.ds((c - (NB - 1)) * P, NB * P), :].rearrange(
                        "(c p) r -> p c r", p=P), row[:, h, :, :]).then_inc(row_out[h], 16)
            tile_steps(act, sh.NT, step)
            for h in range(2):
                act.wait_ge(row_out[h], 16 * (sh.NT // (2 * NB)))


def window_add(nc, ctx, sh, m, name, acc, width, summed, first, ps_sum):
    held = ctx.enter_context(nc.sbuf_tensor(f"{name}_window", [WIN, width], F32))
    win_in, win_out, added = semaphores(nc, m, "win", ["in", "out", "added"])

    def store(act, s):
        act.wait_ge(added, s + 1)
        carry(act, m["went"][1])
        low = nc.scalar.value_load(m["low"][0:1, bass.ds(s, 1)], min_val=0, max_val=sh.NP)
        act.dma_start(acc[bass.ds(low, WIN), :], held[:, :]).then_inc(win_out, 16)

    def load(act, s):
        wait_for(act, win_out, s * 16)
        carry(act, m["went"][1])
        low = nc.scalar.value_load(m["low"][0:1, bass.ds(s, 1)], min_val=0, max_val=sh.NP)
        act.dma_start(held[:, :], acc[bass.ds(low, WIN), :]).then_inc(win_in, 16)

    def add(dve, s, k):
        dve.wait_ge(summed, s + (first + 1))
        dve.wait_ge(win_in, s * 16 + 16)
        nc.vector.tensor_tensor(held[:, :], held[:, :], ps_sum[k % 2][0:WIN, 0:width], ALU.add).then_inc(added, 1)

    def stored(act):
        act.wait_ge(win_out, 16 * sh.G)

    return store, load, add, stored, added, [win_in, win_out, added]


def message_pass(nc, sh, a, m):
    with ExitStack() as ctx:
        def sb(name, shape, dt=F32):
            return ctx.enter_context(nc.sbuf_tensor(name, shape, dt))

        idx = sb("msg_idx", [P, RING * TG], I32)
        ea_t = sb("msg_ea_t", [P, RING, CHUNK, P])
        ea_n = sb("msg_ea_n", [P, RING, TG, ED])
        rows = sb("msg_rows", [P, RING, TG, TR])
        prod = sb("msg_prod", [P, TG, ED])
        dot = sb("msg_dot", [P, 2, TG])
        var = sb("msg_var", [P, 2, TG])
        half = sb("msg_half", [P, 2, TG])
        guess = sb("msg_guess", [P, 2, TG], I32)
        shifted = sb("msg_shifted", [P, 2, TG], I32)
        root = sb("msg_root", [P, 2, 2, TG])
        work = sb("msg_work", [P, 2, TG])
        rstd = sb("msg_rstd", [P, 2, TG])
        hid = sb("msg_hid", [P, RING, TG, HC])
        onehot = sb("msg_onehot", [P, RING, TG, WIN])
        ps_e = ctx.enter_context(nc.psum_tensor("msg_ps_e", [P, 2, CHUNK, 512], F32))
        ps_sum = [ctx.enter_context(nc.psum_tensor(f"msg_ps_sum{k}", [P, 512], F32)) for k in range(2)]
        edges_in = semaphores(nc, m, "msg", [f"edges_in{k}" for k in range(RING)])
        gathered = m["gathered"]
        (ea_done, joined, stat, var_ok, newton, multiplied, scaled, activated, placed, summed,
         ones_set) = own = semaphores(
            nc, m, "msg", ["ea_done", "joined", "stat", "var_ok", "newton", "multiplied", "scaled", "activated",
                           "placed", "summed", "ones_set"])
        store, load, add, stored, added, win_sems = window_add(nc, ctx, sh, m, "msg", m["acc"][0], HC, summed,
                                                               RING, ps_sum)
        block = ctx.enter_context(nc.Block())

        @block.sync
        def _(sp):
            def step(s, i, k):
                wait_for(sp, var_ok, s - (RING - 1))
                carry(sp, m["went"][2])
                sp.dma_start(idx[:, k * TG:(k + 1) * TG],
                             a["src"][bass.ds(s * P, P), :]).then_inc(edges_in[k], 16)
                sp.dma_start(ea_t[:, k, :, :], a["ea_t"][bass.ds(s * P, P), :].rearrange("p (c e) -> p c e", c=CHUNK)
                             ).then_inc(edges_in[k], 16)
                sp.dma_start(ea_n[:, k, :, :], a["ea_n"][bass.ds(s * P, P), :].rearrange("p (t d) -> p t d", t=TG)
                             ).then_inc(edges_in[k], 16)
            ring_steps(sp, sh.G, step)

        @block.gpsimd
        def _(pool):
            nc.gpsimd.memset(hid[:, :, :, H:HC], 1.0).then_inc(ones_set, 1)

            def step(s, i, k):
                pool.wait_ge(edges_in[k], i * 48 + 48)
                for t in range(TG):
                    if t in (0, TG // 2):
                        wait_for(pool, scaled, s * NC_CH - NC_CH * RING + (t // CHUNK + NC_CH // 2))
                        carry(pool, m["went"][0])
                    nc.gpsimd.indirect_dma_start(
                        rows[:, k, t, :], None, m["table"],
                        bass.IndirectOffsetOnAxis(idx[:, k * TG + t:k * TG + t + 1], axis=0)).then_inc(gathered[k][t], 16)
            ring_steps(pool, sh.G, step)

        @block.tensor
        def _(pe):
            def edge_part(s, i, k, chunks):
                pe.wait_ge(edges_in[k], i * 48 + 48)
                for c in chunks:
                    wait_for(pe, joined, s * NC_CH + (c - 1))
                    for j in range(CHUNK):
                        t = c * CHUNK + j
                        last = nc.tensor.matmul(ps_e[:, c % 2, j, 0:TV], ea_t[:, k, t // QK, :], m["wm"][:, t % QK, :],
                                                start=True, stop=True)
                    last.then_inc(ea_done, 1)

            def segment_sum(s, k, chunks):
                if chunks[0] == 0:
                    pe.wait_ge(placed, s + 1)
                    wait_for(pe, added, s - 1)
                for c in chunks:
                    pe.wait_ge(activated, s * NC_CH + (c + 1))
                    for t in range(c * CHUNK, (c + 1) * CHUNK):
                        ins = nc.tensor.matmul(ps_sum[k % 2][0:WIN, 0:HC], onehot[:, k, t, :], hid[:, k, t, :],
                                               start=(t == 0), stop=(t == TG - 1))
                if chunks[-1] == NC_CH - 1:
                    ins.then_inc(summed, 1)

            def step(s, i, k):
                edge_part(s, i, k, (0, 1))
                if not isinstance(s, int):
                    segment_sum(s - 4, k, (2, 3))
                edge_part(s, i, k, (2, 3))
                if not isinstance(s, int) or s >= 3:
                    segment_sum(s - 3, (k - 3) % RING, (0, 1))
            pe.sem_inc(summed, RING)
            ring_steps(pe, sh.G, step)
            segment_sum(sh.G - 4, 0, (2, 3))
            for g in (sh.G - 3, sh.G - 2, sh.G - 1):
                segment_sum(g, g % RING, range(NC_CH))

        @block.vector
        def _(dve):
            def join(s, i, k, c):
                for t in range(c * CHUNK, (c + 1) * CHUNK):
                    dve.wait_ge(gathered[k][t], i * 16 + 16)
                dve.wait_ge(ea_done, s * NC_CH + (c + 1))
                r = rows[:, k, c * CHUNK:(c + 1) * CHUNK, 0:TV]
                nc.vector.tensor_tensor(r, r, ps_e[:, c % 2, :, 0:TV], ALU.add).then_inc(joined, 1)

            def var_products(s, i, k):
                dve.wait_ge(edges_in[k], i * 48 + 48)
                dve.wait_ge(joined, s * NC_CH + NC_CH)
                nc.vector.tensor_tensor(prod[:, :, :], rows[:, k, :, H:TV], ea_n[:, k, :, :], ALU.mult).then_inc(stat, 1)

            def var_dot(s):
                dve.wait_ge(stat, s * 3 + 1)
                nc.vector.tensor_reduce(dot[:, 0, :], prod[:, :, :], AX.X, ALU.add).then_inc(stat, 1)

            def var_row(s, k):
                dve.wait_ge(stat, s * 3 + 2)
                nc.vector.tensor_tensor(dot[:, 1, :], dot[:, 0, :], rows[:, k, :, TV], ALU.add).then_inc(stat, 1)

            def var_eps(s, k):
                dve.wait_ge(stat, s * 3 + 3)
                nc.vector.tensor_scalar(var[:, k % 2, :], dot[:, 1, :], EPS, EPS, ALU.add, ALU.max).then_inc(var_ok, 1)

            def root_shift(pair):
                dve.wait_ge(var_ok, pair * 2 + 2)
                nc.vector.tensor_scalar(half[:, :, :], var[:, :, :], -0.5, None, ALU.mult)
                nc.vector.tensor_scalar(shifted[:, :, :], var[:, :, :].bitcast(I32), 1, None,
                                        ALU.logical_shift_right).then_inc(newton, 1)

            def root_guess(pair):
                dve.wait_ge(newton, pair * NEWTON + 1)
                nc.vector.tensor_scalar(guess[:, :, :], shifted[:, :, :], -1.0, float(0x5f3759df), ALU.mult,
                                        ALU.add).then_inc(newton, 1)

            roots = [guess[:, :, :].bitcast(F32), root[:, 0, :, :], root[:, 1, :, :], rstd[:, :, :]]

            def root_square(pair, r):
                dve.wait_ge(newton, pair * NEWTON + (2 + 3 * r))
                nc.vector.tensor_tensor(work[:, :, :], roots[r], roots[r], ALU.mult).then_inc(newton, 1)

            def root_times(pair, r):
                dve.wait_ge(newton, pair * NEWTON + (3 + 3 * r))
                nc.vector.tensor_tensor(work[:, :, :], work[:, :, :], half[:, :, :], ALU.mult).then_inc(newton, 1)

            def root_step(pair, r):
                dve.wait_ge(newton, pair * NEWTON + (4 + 3 * r))
                if r == 2:
                    wait_for(dve, scaled, pair * 2 * NC_CH)
                nc.vector.scalar_tensor_tensor(out=roots[r + 1], in0=work[:, :, :], scalar=1.5, in1=roots[r],
                                               op0=ALU.add, op1=ALU.mult).then_inc(newton, 1)

            def place(s, k):
                dve.wait_ge(summed, s + 1)
                nc.vector.tensor_tensor(onehot[:, k, :, :], m["iota"][:, None, :].broadcast_to([P, TG, WIN]),
                                        m["place"][:, bass.ds(s * TG, TG)][:, :, None].broadcast_to([P, TG, WIN]),
                                        ALU.is_equal).then_inc(placed, 1)

            def scale(s, k, pair, t):
                if t == 0:
                    dve.wait_ge(newton, pair * NEWTON + NEWTON)
                    dve.wait_ge(summed, s + 1)
                ins = nc.vector.scalar_tensor_tensor(
                    out=hid[:, k, t, 0:H], in0=rows[:, k, t, 0:H], scalar=rstd[:, k % 2, t:t + 1],
                    in1=m["be1b"][:, :], op0=ALU.mult, op1=ALU.add)
                if t % CHUNK == CHUNK - 1:
                    ins.then_inc(scaled, 1)

            def shift(s, k, c):
                dve.wait_ge(multiplied, s * (NC_CH - DVE_CH) + (c - DVE_CH + 1))
                h = hid[:, k, c * CHUNK:(c + 1) * CHUNK, 0:H]
                nc.vector.tensor_tensor(h, h, m["be1b"][:, None, :].broadcast_to([P, CHUNK, H]), ALU.add).then_inc(
                    scaled, 1)

            def even_step(s, i, k):
                pair = i * 2 + k // 2 - 1
                join(s, i, k, 0)
                root_shift(pair)
                join(s, i, k, 1)
                root_guess(pair)
                if not isinstance(s, int):
                    add(dve, s - 4, k)
                root_square(pair, 0)
                place(s - 2, (k - 2) % RING)
                root_times(pair, 0)
                join(s, i, k, 2)
                root_step(pair, 0)
                join(s, i, k, 3)
                root_square(pair, 1)
                var_products(s, i, k)
                root_times(pair, 1)
                var_dot(s)
                root_step(pair, 1)
                var_row(s, k)
                root_square(pair, 2)
                var_eps(s, k)
                root_times(pair, 2)
                root_step(pair, 2)
                for t in range(DVE_CH * CHUNK):
                    scale(s - 2, (k - 2) % RING, pair, t)
                for c in range(DVE_CH, NC_CH):
                    shift(s - 2, (k - 2) % RING, c)

            def odd_step(s, i, k):
                pair = i * 2 + k // 2 - 1
                kl = (k - 2) % RING
                join(s, i, k, 0)
                scale(s - 2, kl, pair, 0)
                join(s, i, k, 1)
                scale(s - 2, kl, pair, 1)
                if not isinstance(s, int):
                    add(dve, s - 4, k)
                place(s - 2, (k - 2) % RING)
                scale(s - 2, kl, pair, 2)
                join(s, i, k, 2)
                scale(s - 2, kl, pair, 3)
                join(s, i, k, 3)
                var_products(s, i, k)
                shift(s - 2, kl, 2)
                var_dot(s)
                shift(s - 2, kl, 3)
                var_row(s, k)
                var_eps(s, k)

            def step(s, i, k):
                if isinstance(s, int) and s < 2:
                    for c in range(NC_CH):
                        join(s, i, k, c)
                    var_products(s, i, k)
                    var_dot(s)
                    var_row(s, k)
                    var_eps(s, k)
                elif k % 2 == 0:
                    even_step(s, i, k)
                else:
                    odd_step(s, i, k)
            ring_steps(dve, sh.G, step)
            last_pair = sh.G // 2 - 1
            add(dve, sh.G - 4, 0)
            add(dve, sh.G - 3, 1)
            root_shift(last_pair)
            root_guess(last_pair)
            for r in range(3):
                root_square(last_pair, r)
                root_times(last_pair, r)
                root_step(last_pair, r)
            for g in (sh.G - 2, sh.G - 1):
                place(g, g % RING)
                for t in range(DVE_CH * CHUNK):
                    scale(g, g % RING, last_pair, t)
                for c in range(DVE_CH, NC_CH):
                    shift(g, g % RING, c)
            add(dve, sh.G - 2, 2)
            add(dve, sh.G - 1, 3)

        @block.scalar
        def _(act):
            def multiply(s, k, pair):
                act.wait_ge(newton, pair * NEWTON + NEWTON)
                act.wait_ge(summed, s + 1)
                for t in range(DVE_CH * CHUNK, TG):
                    ins = nc.scalar.activation(hid[:, k, t, 0:H], rows[:, k, t, 0:H], ACT.Identity,
                                               scale=rstd[:, k % 2, t:t + 1])
                    if t % CHUNK == CHUNK - 1:
                        ins.then_inc(multiplied, 1)

            def gelu(s, k):
                for c in range(NC_CH):
                    act.wait_ge(scaled, s * NC_CH + (c + 1))
                    h = hid[:, k, c * CHUNK:(c + 1) * CHUNK, 0:H]
                    nc.scalar.activation(h, h, ACT.Gelu).then_inc(activated, 1)

            act.wait_ge(ones_set, 1)

            def step(s, i, k):
                pair = i * 2 + k // 2 - 1
                if k % 2 and (not isinstance(s, int) or s >= 2):
                    multiply(s - 2, (k - 2) % RING, pair)
                if not isinstance(s, int):
                    store(act, s - 4)
                if k % 2 == 0 and (not isinstance(s, int) or s >= 2):
                    multiply(s - 2, (k - 2) % RING, pair)
                if not isinstance(s, int) or s >= 3:
                    load(act, s - 3)
                if not isinstance(s, int) or s >= 2:
                    gelu(s - 2, (k - 2) % RING)
            ring_steps(act, sh.G, step)
            store(act, sh.G - 4)
            load(act, sh.G - 3)
            store(act, sh.G - 3)
            load(act, sh.G - 2)
            for g in (sh.G - 2, sh.G - 1):
                multiply(g, g % RING, sh.G // 2 - 1)
                gelu(g, g % RING)
            store(act, sh.G - 2)
            load(act, sh.G - 1)
            store(act, sh.G - 1)
            stored(act)
    return [*edges_in, *own, *win_sems]


def conv_pass(nc, sh, a, m, layer):
    name = f"conv{layer}"
    with ExitStack() as ctx:
        idx = ctx.enter_context(nc.sbuf_tensor(f"{name}_idx", [P, RING * TG], I32))
        rows = ctx.enter_context(nc.sbuf_tensor(f"{name}_rows", [P, RING, TG, D], F32))
        onehot = ctx.enter_context(nc.sbuf_tensor(f"{name}_onehot", [P, 2, TG, WIN], F32))
        ps_sum = [ctx.enter_context(nc.psum_tensor(f"{name}_ps_sum{k}", [P, 512], F32)) for k in range(2)]
        idx_in = semaphores(nc, m, "conv", [f"idx_in{k}" for k in range(RING)])
        gathered = m["gathered"]
        placed, summed = own = semaphores(nc, m, "conv", ["placed", "summed"])
        store, load, add, stored, added, win_sems = window_add(nc, ctx, sh, m, name, m["acc"][1 + layer], D, summed, 0,
                                                               ps_sum)
        block = ctx.enter_context(nc.Block())

        @block.sync
        def _(sp):
            def step(s, i, k):
                for t in range(TG):
                    wait_for(sp, gathered[k][t], i * 16)
                carry(sp, m["went"][2])
                sp.dma_start(idx[:, k * TG:(k + 1) * TG], a["src"][bass.ds(s * P, P), :]).then_inc(idx_in[k], 16)
            ring_steps(sp, sh.G, step)

        @block.gpsimd
        def _(pool):
            def step(s, i, k):
                pool.wait_ge(idx_in[k], i * 16 + 16)
                wait_for(pool, summed, s - (RING - 1))
                carry(pool, m["went"][0])
                for t in range(TG):
                    nc.gpsimd.indirect_dma_start(
                        rows[:, k, t, :], None, m["conv_table"][layer],
                        bass.IndirectOffsetOnAxis(idx[:, k * TG + t:k * TG + t + 1], axis=0)).then_inc(gathered[k][t], 16)
            ring_steps(pool, sh.G, step)

        @block.tensor
        def _(pe):
            def step(s, i, k):
                pe.wait_ge(placed, s + 1)
                wait_for(pe, added, s - 1)
                for t in range(TG):
                    pe.wait_ge(gathered[k][t], i * 16 + 16)
                    last = nc.tensor.matmul(ps_sum[k % 2][0:WIN, 0:D], onehot[:, k % 2, t, :], rows[:, k, t, :],
                                            start=(t == 0), stop=(t == TG - 1))
                last.then_inc(summed, 1)
            ring_steps(pe, sh.G, step)

        @block.vector
        def _(dve):
            def step(s, i, k):
                if not isinstance(s, int) or s >= 2:
                    add(dve, s - 2, k)
                wait_for(dve, summed, s - 1)
                nc.vector.tensor_tensor(onehot[:, k % 2, :, :], m["iota"][:, None, :].broadcast_to([P, TG, WIN]),
                                        m["place"][:, bass.ds(s * TG, TG)][:, :, None].broadcast_to([P, TG, WIN]),
                                        ALU.is_equal).then_inc(placed, 1)
            ring_steps(dve, sh.G, step)
            add(dve, sh.G - 2, 2)
            add(dve, sh.G - 1, 3)

        @block.scalar
        def _(act):
            def step(s, i, k):
                if not isinstance(s, int) or s >= 2:
                    store(act, s - 2)
                if not isinstance(s, int) or s >= 1:
                    load(act, s - 1)
            ring_steps(act, sh.G, step)
            store(act, sh.G - 2)
            load(act, sh.G - 1)
            store(act, sh.G - 1)
            stored(act)
    return [*idx_in, *own, *win_sems]


def rounds_of(nc, sh, m, one_round):
    reset, moved = semaphores(nc, m, "rounds", ["reset", "moved"])
    with nc.Block() as block:
        @block.vector
        def _(dve):
            nc.vector.tensor_copy(m["place"][:, :], m["place_first"][:, :, :].rearrange("p g t -> p (g t)")).then_inc(
                reset, 1)
            nc.vector.tensor_copy(m["low"][:, :], m["low_first"][:, :]).then_inc(reset, 1)
            dve.wait_ge(reset, 2)
    rounds = nc.values_load(m["rounds"][0:1, 0:1], min_val=1, max_val=sh.NP // WIN + 1,
                            skip_runtime_bounds_check_because="a group's dst lie in the nodes, so the spans do")
    with nc.Fori(0, rounds):
        used = one_round()
        with nc.Block() as block:
            @block.vector
            def _(dve):
                nc.vector.tensor_scalar(m["place"][:, :], m["place"][:, :], -float(WIN), None, ALU.add).then_inc(
                    moved, 1)
                nc.vector.tensor_scalar(m["low"][:, :], m["low"][:, :], WIN, sh.NP, ALU.add, ALU.min).then_inc(
                    moved, 1)
                dve.wait_ge(moved, 2)
        clear_all(nc, m, [*used, moved])
    clear(nc, [reset])


def mean_and_variance(nc, link, st, mv, t1):
    link(nc.vector.tensor_tensor(mv[:, 0, :], st[:, :, 1], st[:, :, 4], ALU.add))
    link(nc.vector.tensor_scalar(mv[:, 0, :], mv[:, 0, :], 0.5, None, ALU.mult))
    link(nc.vector.tensor_tensor(t1[:, :], st[:, :, 1], mv[:, 0, :], ALU.subtract))
    link(nc.vector.tensor_tensor(t1[:, :], t1[:, :], t1[:, :], ALU.mult))
    link(nc.vector.tensor_tensor(mv[:, 1, :], st[:, :, 2], st[:, :, 5], ALU.add))
    link(nc.vector.tensor_scalar(mv[:, 1, :], mv[:, 1, :], 1.0 / D, EPS, ALU.mult, ALU.add))
    link(nc.vector.tensor_tensor(mv[:, 1, :], mv[:, 1, :], t1[:, :], ALU.add))


def inverse_root(nc, link, var, out, half, bits, work):
    nc.vector.tensor_scalar(half, var, -0.5, None, ALU.mult)
    link(nc.vector.tensor_scalar(bits, var.bitcast(I32), 1, None, ALU.logical_shift_right))
    link(nc.vector.tensor_scalar(bits, bits, -1.0, float(0x5f3759df), ALU.mult, ALU.add))
    y = bits.bitcast(F32)
    for r in range(3):
        link(nc.vector.tensor_tensor(work, y, y, ALU.mult))
        link(nc.vector.tensor_tensor(work, work, half, ALU.mult))
        link(nc.vector.scalar_tensor_tensor(out=out if r == 2 else y, in0=work, scalar=1.5, in1=y, op0=ALU.add,
                                            op1=ALU.mult))


def mean_rstd(nc, link, st, mv, rs, tmp):
    mean_and_variance(nc, link, st, mv, rs)
    inverse_root(nc, link, mv[:, 1, :], rs, tmp[:, 0, :], tmp[:, 1, :].bitcast(I32), tmp[:, 2, :])
    return nc.vector.scalar_tensor_tensor(out=mv[:, 0, :], in0=mv[:, 0, :], scalar=-1.0, in1=rs, op0=ALU.mult,
                                          op1=ALU.mult)


def flat(t):
    return t.rearrange("p t d -> p (t d)")


def across(v, width=D):
    return v[:, :, None].broadcast_to([P, v.shape[1], width])


def node_update(nc, sh, a, m):
    NT = sh.NT
    n_b = NT // NB
    u, st, mv, rs, tmp = m["u"], m["u_st"], m["u_mv"], m["u_rs"], m["u_tmp"]
    parts = (range(0, 4), range(4, NB))
    with ExitStack() as c2:
        def sb2(name, shape, dt=F32):
            return c2.enter_context(nc.sbuf_tensor(name, shape, dt))

        sums = sb2("upd_sums", [P, 2, NB, HC])
        xt = sb2("upd_xt", [D, 2, NB, P])
        s_cols = sb2("upd_cols", [P, NB, 2, P])
        bias = sb2("upd_bias", [P, NB, D])
        ps_t = c2.enter_context(nc.psum_tensor("upd_ps_t", [P, 8, 2 * P], F32))
        ps_u = c2.enter_context(nc.psum_tensor("upd_ps_u", [P, 2, 8, D], F32))
        sums0, sums1, xt0, xt1, turned, copied, multiplied, based, made_u, stats_ok = semaphores(nc, m, "upd", [
            "sums_in0", "sums_in1", "xt_in0", "xt_in1", "turned", "copied", "multiplied", "based", "made_u", "stats"])
        sums_in, xt_in = [sums0, sums1], [xt0, xt1]
        block = c2.enter_context(nc.Block())

        @block.sync
        def _(sp):
            def step(b, i, h):
                wait_for(sp, turned, b * 2 - 2)
                carry(sp, m["went"][2])
                wait_for(sp, based, b - 1)
                carry(sp, m["went"][2])
                sp.dma_start(sums[:, h, :, :], m["acc"][0][bass.ds(b * (NB * P), NB * P), :].rearrange(
                    "(c p) r -> p c r", p=P)).then_inc(sums_in[h], 16)
                wait_for(sp, made_u, b - 1)
                carry(sp, m["went"][2])
                sp.dma_start(xt[:, h, :, :], a["xt"][:, bass.ds(b * (NB * P), NB * P)].rearrange(
                    "p (c n) -> p c n", n=P)).then_inc(xt_in[h], 16)
            pair_steps(sp, n_b, step)
            sp.dma_start(m["x2"][:, :, :], a["x_rows"]).then_inc(m["loaded_x"], 16)

        @block.vector
        def _(dve):
            def base(b, i, h):
                dve.wait_ge(sums_in[h], i * 16 + 16)
                wait_for(dve, made_u, b)
                nc.vector.tensor_copy(m["deg"][:, bass.ds(b * NB, NB)], sums[:, h, :, H])
                for c in range(NB):
                    last = nc.vector.scalar_tensor_tensor(out=bias[:, c, :], in0=m["w2u"][:, 2, :],
                                                          scalar=sums[:, h, c, H:HC], in1=m["bub"][:, :],
                                                          op0=ALU.mult, op1=ALU.add)
                last.then_inc(based, 1)

            def collect(b, h):
                dve.wait_ge(multiplied, b * 2 + 2)
                dve.wait_ge(based, b + 1)
                nc.vector.tensor_tensor(u[:, bass.ds(b * NB, NB), :], ps_u[:, h, 0:NB, :], bias[:, :, :],
                                        ALU.add).then_inc(made_u, 1)

            def spread(b):
                dve.wait_ge(made_u, b + 1)
                for c in range(NB):
                    last = nc.vector.bn_stats(flat(st[:, bass.ds(b * NB + c, 1), :]),
                                              flat(u[:, bass.ds(b * NB + c, 1), :]))
                last.then_inc(stats_ok, 1)

            def step(b, i, h):
                base(b, i, h)
                if not isinstance(b, int) or b >= 1:
                    spread(b - 1)
                collect(b, h)
            pair_steps(dve, n_b, step)
            spread(n_b - 1)
            dve.wait_ge(stats_ok, n_b)

        @block.tensor
        def _(pe):
            def turn(b, i, h, part):
                pe.wait_ge(sums_in[h], i * 16 + 16)
                wait_for(pe, copied, b * 2 + (part - 1))
                for c in parts[part]:
                    for r in range(2):
                        last = nc.tensor.transpose(ps_t[:, c, r * P:(r + 1) * P],
                                                   sums[:, h, c, r * P:(r + 1) * P], m["ident"][:, :])
                last.then_inc(turned, 1)

            def multiply(b, i, h, part):
                pe.wait_ge(copied, b * 2 + (part + 1))
                if part == 0:
                    pe.wait_ge(xt_in[h], i * 16 + 16)
                    wait_for(pe, made_u, b - 1)
                for c in parts[part]:
                    nc.tensor.matmul(ps_u[:, h, c, :], xt[:, h, c, :], m["wu"][:, 0, :], start=True, stop=False)
                    for r in range(2):
                        last = nc.tensor.matmul(ps_u[:, h, c, :], s_cols[:, c, r, :], m["w2u"][:, r, :],
                                                start=False, stop=(r == 1))
                last.then_inc(multiplied, 1)

            def step(b, i, h):
                turn(b, i, h, 0)
                if not isinstance(b, int) or b >= 1:
                    multiply(b - 1, i, 1 - h, 1)
                turn(b, i, h, 1)
                multiply(b, i, h, 0)
            pair_steps(pe, n_b, step)
            multiply(n_b - 1, n_b // 2 - 1, 1, 1)

        @block.scalar
        def _(act):
            def step(b, i, h):
                for part, tiles in enumerate(parts):
                    act.wait_ge(turned, b * 2 + (part + 1))
                    wait_for(act, multiplied, b * 2 + (part - 1))
                    r = slice(tiles[0], tiles[-1] + 1)
                    nc.scalar.activation(s_cols[:, r, :, :].rearrange("p c r d -> p (c r d)"), flat(ps_t[:, r, :]),
                                         ACT.Copy).then_inc(copied, 1)
            pair_steps(act, n_b, step)

    chain, ready, normed, shifted, gelu_ok = semaphores(nc, m, "ln", [
        "chain", "ready", "normed", "shifted", "gelu"])
    with nc.Block() as block:
        @block.scalar
        def _(act):
            def normalise(b):
                for c in range(b * NB, (b + 1) * NB):
                    last = nc.scalar.activation(u[:, c, :], u[:, c, :], ACT.Identity, bias=mv[:, 0, c:c + 1],
                                                scale=rs[:, c:c + 1])
                last.then_inc(normed, 1)

            def gelu(b):
                act.wait_ge(shifted, b + 1)
                t = u[:, b * NB:(b + 1) * NB, :]
                nc.scalar.activation(t, t, ACT.Gelu).then_inc(gelu_ok, 1)

            act.wait_ge(ready, 1)
            for b in range(n_b):
                normalise(b)
                if b >= 1:
                    gelu(b - 1)
            gelu(n_b - 1)

        @block.vector
        def _(dve):
            count = [0]

            def link(ins):
                count[0] += 1
                ins.then_inc(chain, 1)
                dve.wait_ge(chain, count[0])

            mean_rstd(nc, link, st, mv, rs[:, :], tmp).then_inc(ready, 1)

            def for_all(v):
                return v[:, None, :].broadcast_to([P, NB, D])

            def affine(b):
                dve.wait_ge(normed, b + 1)
                t = u[:, b * NB:(b + 1) * NB, :]
                link(nc.vector.tensor_tensor(t, t, for_all(m["gub"]), ALU.mult))
                nc.vector.tensor_tensor(t, t, for_all(m["beub"]), ALU.add).then_inc(shifted, 1)

            def plus_2x(b):
                dve.wait_ge(gelu_ok, b + 1)
                r = slice(b * NB, (b + 1) * NB)
                link(nc.vector.scalar_tensor_tensor(out=flat(u[:, r, :]), in0=flat(m["x2"][:, r, :]), scalar=2.0,
                                                    in1=flat(u[:, r, :]), op0=ALU.mult, op1=ALU.add))
                for c in range(b * NB, (b + 1) * NB):
                    last = nc.vector.bn_stats(st[:, c, :], u[:, c, :])
                if b == n_b - 1:
                    link(last)

            link(nc.vector.tensor_scalar(m["deg"][:, :], m["deg"][:, :], 1.0, None, ALU.add))
            inverse_root(nc, link, m["deg"][:, :], m["dinv"][:, :], tmp[:, 0, :], tmp[:, 1, :].bitcast(I32),
                         tmp[:, 2, :])
            dve.wait_ge(m["loaded_x"], 16)
            for b in range(n_b):
                affine(b)
                if b >= 2:
                    plus_2x(b - 2)
            plus_2x(n_b - 2)
            plus_2x(n_b - 1)
            link(mean_rstd(nc, link, st, mv, rs[:, :], tmp))


def conv_table(nc, sh, m, layer):
    name = f"ctab{layer}"
    n_b = sh.NT // NB
    with ExitStack() as ctx:
        def sb(n, shape, dt=F32):
            return ctx.enter_context(nc.sbuf_tensor(f"{name}_{n}", shape, dt))

        xr = sb("xr", [P, 2, NB, D])
        hs = sb("hs", [P, 2, NB, D])
        out = sb("out", [P, 2, NB, D])
        ps_t = ctx.enter_context(nc.psum_tensor(f"{name}_ps_t", [P, 2, 8, D], F32))
        ps_h = ctx.enter_context(nc.psum_tensor(f"{name}_ps_h", [P, 2, 8, D], F32))
        scaled_x, normed, kept, turned, columns, multiplied, scaled, out0, out1 = own = semaphores(nc, m, "ctab", [
            "scaled_x", "normed", "kept", "turned", "columns", "multiplied", "scaled", "out0", "out1"])
        row_out = [out0, out1]
        block = ctx.enter_context(nc.Block())

        @block.scalar
        def _(act):
            def step(b, i, h):
                wait_for(act, multiplied, b - 1)
                if layer == 0:
                    act.wait_ge(normed, b + 1)
                    nc.scalar.activation(m["x2"][:, bass.ds(b * NB, NB), :], xr[:, h, :, :], ACT.Copy).then_inc(kept, 1)
                    act.wait_ge(turned, b + 1)
                    nc.scalar.activation(flat(hs[:, h, :, :]), flat(ps_t[:, h, 0:NB, :]), ACT.Copy).then_inc(columns, 1)
                else:
                    nc.scalar.activation(flat(hs[:, h, :, :]), m["cols"][:, bass.ds(b * (NB * P), NB * P)], ACT.Relu,
                                         bias=m["shift"][:, 0:1], scale=m["gain"][:, 0:1]).then_inc(columns, 1)
            pair_steps(act, n_b, step)

        @block.tensor
        def _(pe):
            def turn(b, h):
                pe.wait_ge(normed, b + 1)
                wait_for(pe, columns, b - 1)
                for c in range(NB):
                    last = nc.tensor.transpose(ps_t[:, h, c, :], xr[:, h, c, :], m["ident"][:, :])
                last.then_inc(turned, 1)

            def multiply(b, h):
                pe.wait_ge(columns, b + 1)
                wait_for(pe, scaled, b - 1)
                for c in range(NB):
                    last = nc.tensor.matmul(ps_h[:, h, c, :], hs[:, h, c, :], m["wc"][:, layer, :], start=True,
                                            stop=True)
                last.then_inc(multiplied, 1)

            def step(b, i, h):
                if layer == 0:
                    turn(b, h)
                    if not isinstance(b, int) or b >= 1:
                        multiply(b - 1, 1 - h)
                else:
                    multiply(b, h)
            pe.wait_ge(m["loaded_conv"], 16 * 8)
            pair_steps(pe, n_b, step)
            if layer == 0:
                multiply(n_b - 1, 1)

        @block.vector
        def _(dve):
            def batch_of(t, b):
                return t[:, bass.ds(b * NB, NB)]

            def normalise(b, h):
                u = m["u"][:, bass.ds(b * NB, NB), :]
                nc.vector.tensor_tensor(u, u, across(batch_of(m["u_rs"], b)), ALU.mult).then_inc(scaled_x, 1)
                dve.wait_ge(scaled_x, b + 1)
                wait_for(dve, turned, b - 1)
                wait_for(dve, kept, b - 1)
                nc.vector.tensor_tensor(xr[:, h, :, :], u, across(m["u_mv"][:, 0, bass.ds(b * NB, NB)]),
                                        ALU.add).then_inc(normed, 1)

            def times_dinv(b, i, h):
                dve.wait_ge(row_out[h], i * 32 + 32)
                dve.wait_ge(multiplied, b + 1)
                nc.vector.tensor_tensor(out[:, h, :, :], ps_h[:, h, 0:NB, :], across(batch_of(m["dinv"], b)),
                                        ALU.mult).then_inc(scaled, 1)

            def step(b, i, h):
                if layer == 0:
                    normalise(b, h)
                    if not isinstance(b, int) or b >= 2:
                        times_dinv(b - 2, i - 1, h)
                else:
                    times_dinv(b, i, h)
            pair_steps(dve, n_b, step)
            if layer == 0:
                times_dinv(n_b - 2, n_b // 2 - 1, 0)
                times_dinv(n_b - 1, n_b // 2 - 1, 1)

        @block.sync
        def _(sp):
            def step(b, i, h):
                sp.wait_ge(scaled, b + 1)
                carry(sp, m["went"][2])
                for target in (m["conv_table"][layer], m["acc"][1 + layer]):
                    sp.dma_start(target[bass.ds(b * (NB * P), NB * P), :].rearrange("(c p) d -> p c d", p=P),
                                 out[:, h, :, :]).then_inc(row_out[h], 16)
            for h in range(2):
                sp.sem_inc(row_out[h], 32)
            pair_steps(sp, n_b, step)
            for h in range(2):
                sp.wait_ge(row_out[h], 32 * (n_b // 2) + 32)
    return own


def batch_norm(nc, sh, m, layer):
    name = f"bn{layer}"
    n_b = sh.NT // NB
    with ExitStack() as ctx:
        def sb(n, shape, dt=F32):
            return ctx.enter_context(nc.sbuf_tensor(f"{name}_{n}", shape, dt))

        sums = sb("sums", [P, 2, NB, D])
        n_s = sh.N // sh.BN
        st = sb("st", [P, n_s, 6])
        mv = sb("mv", [P, 2])
        rs = sb("rs", [P, 2])
        tmp = sb("tmp", [P, 3])
        ps_c = ctx.enter_context(nc.psum_tensor(f"{name}_ps_c", [P, 2, 8, P], F32))
        in0, in1, scaled, turned, filled, chain = own = semaphores(nc, m, "bn", [
            "in0", "in1", "scaled", "turned", "filled", "chain"])
        loaded = [in0, in1]
        block = ctx.enter_context(nc.Block())

        @block.sync
        def _(sp):
            def step(b, i, h):
                wait_for(sp, turned, b - 1)
                carry(sp, m["went"][2])
                sp.dma_start(sums[:, h, :, :], m["acc"][1 + layer][bass.ds(b * (NB * P), NB * P), :].rearrange(
                    "(c p) d -> p c d", p=P)).then_inc(loaded[h], 16)
            pair_steps(sp, n_b, step)

        @block.tensor
        def _(pe):
            def step(b, i, h):
                pe.wait_ge(scaled, b + 1)
                wait_for(pe, filled, b - 1)
                for c in range(NB):
                    last = nc.tensor.transpose(ps_c[:, h, c, :], sums[:, h, c, :], m["ident"][:, :])
                last.then_inc(turned, 1)
            pair_steps(pe, n_b, step)

        @block.scalar
        def _(act):
            def step(b, i, h):
                act.wait_ge(turned, b + 1)
                nc.scalar.activation(m["cols"][:, bass.ds(b * (NB * P), NB * P)], flat(ps_c[:, h, 0:NB, :]),
                                     ACT.Identity, bias=m["colc"][:, layer, 0:1]).then_inc(filled, 1)
            act.wait_ge(m["loaded_conv"], 16 * 8)
            pair_steps(act, n_b, step)

        @block.vector
        def _(dve):
            def step(b, i, h):
                dve.wait_ge(loaded[h], i * 16 + 16)
                nc.vector.tensor_tensor(sums[:, h, :, :], sums[:, h, :, :], across(m["dinv"][:, bass.ds(b * NB, NB)]),
                                        ALU.mult).then_inc(scaled, 1)
            pair_steps(dve, n_b, step)
            count = [0]

            def link(ins):
                count[0] += 1
                ins.then_inc(chain, 1)
                dve.wait_ge(chain, count[0])

            dve.wait_ge(filled, n_b)
            for j in range(n_s):
                last = nc.vector.bn_stats(st[:, j, :], m["cols"][:, j * sh.BN:(j + 1) * sh.BN])
            link(last)
            link(nc.vector.bn_aggr(mv[:, :], st[:, :, :].rearrange("p j s -> p (j s)")))
            link(nc.vector.tensor_scalar(mv[:, 1:2], mv[:, 1:2], EPS, None, ALU.add))
            inverse_root(nc, link, mv[:, 1:2], rs[:, 0:1], tmp[:, 0:1], tmp[:, 1:2].bitcast(I32), tmp[:, 2:3])
            link(nc.vector.tensor_tensor(m["gain"][:, :], rs[:, 0:1], m["colc"][:, layer, 1:2], ALU.mult))
            link(nc.vector.tensor_tensor(rs[:, 1:2], mv[:, 0:1], m["gain"][:, :], ALU.mult))
            link(nc.vector.tensor_tensor(m["shift"][:, :], m["colc"][:, layer, 2:3], rs[:, 1:2], ALU.subtract))
    return own


def last_norm(nc, sh, m, out):
    NT = sh.NT
    full = sh.N // P
    rest = sh.N - full * P
    with ExitStack() as ctx:
        def sb(n, shape, dt=F32):
            return ctx.enter_context(nc.sbuf_tensor(f"fin_{n}", shape, dt))

        hs = sb("hs", [P, 2, NB, P])
        st = sb("st", [P, NT, 6])
        mv = sb("mv", [P, 2, NT])
        rs = sb("rs", [P, NT])
        tmp = sb("tmp", [P, 3, NT])
        ps_y = ctx.enter_context(nc.psum_tensor("fin_ps_y", [P, 2, 8, P], F32))
        clipped, turned, joined, stats_ok, chain, ready, scaled, normed_act, normed_dve, out_ok = semaphores(
            nc, m, "fin", ["clipped", "turned", "joined", "stats", "chain", "ready", "scaled", "normed_act",
                           "normed_dve", "out"])
        block = ctx.enter_context(nc.Block())
        n_b = NT // NB
        for_dve, for_act = range(0, n_b, 2), range(1, n_b, 2)

        @block.scalar
        def _(act):
            def step(b, i, h):
                wait_for(act, turned, b - 1)
                nc.scalar.activation(flat(hs[:, h, :, :]), m["cols"][:, bass.ds(b * (NB * P), NB * P)], ACT.Relu,
                                     bias=m["shift"][:, 0:1], scale=m["gain"][:, 0:1]).then_inc(clipped, 1)
            pair_steps(act, n_b, step)
            act.wait_ge(ready, 1)
            for b in for_act:
                for c in range(b * NB, (b + 1) * NB):
                    last = nc.scalar.activation(m["x2"][:, c, :], m["x2"][:, c, :], ACT.Identity,
                                                bias=mv[:, 0, c:c + 1], scale=rs[:, c:c + 1])
                last.then_inc(normed_act, 1)

        @block.tensor
        def _(pe):
            def step(b, i, h):
                pe.wait_ge(clipped, b + 1)
                wait_for(pe, joined, b - 1)
                for c in range(NB):
                    last = nc.tensor.transpose(ps_y[:, h, c, :], hs[:, h, c, :], m["ident"][:, :])
                last.then_inc(turned, 1)
            pair_steps(pe, n_b, step)

        @block.vector
        def _(dve):
            def join(b, h):
                dve.wait_ge(turned, b + 1)
                xb = flat(m["x2"][:, bass.ds(b * NB, NB), :])
                nc.vector.scalar_tensor_tensor(out=xb, in0=xb, scalar=2.0, in1=flat(ps_y[:, h, 0:NB, :]),
                                               op0=ALU.mult, op1=ALU.add).then_inc(joined, 1)

            def spread(b):
                dve.wait_ge(joined, b + 1)
                for c in range(NB):
                    last = nc.vector.bn_stats(flat(st[:, bass.ds(b * NB + c, 1), :]),
                                              flat(m["x2"][:, bass.ds(b * NB + c, 1), :]))
                last.then_inc(stats_ok, 1)

            def step(b, i, h):
                join(b, h)
                spread(b)
            pair_steps(dve, n_b, step)
            dve.wait_ge(stats_ok, n_b)
            count = [0]

            def link(ins):
                count[0] += 1
                ins.then_inc(chain, 1)
                dve.wait_ge(chain, count[0])

            mean_rstd(nc, link, st, mv, rs[:, :], tmp).then_inc(ready, 1)
            dve.wait_ge(ready, 1)
            for n, b in enumerate(for_dve):
                r = slice(b * NB, (b + 1) * NB)
                nc.vector.tensor_tensor(m["x2"][:, r, :], m["x2"][:, r, :], across(rs[:, r]), ALU.mult).then_inc(
                    scaled, 1)
                dve.wait_ge(scaled, n + 1)
                nc.vector.tensor_tensor(m["x2"][:, r, :], m["x2"][:, r, :], across(mv[:, 0, r]), ALU.add).then_inc(
                    normed_dve, 1)

        @block.sync
        def _(sp):
            stores = 0
            for b in range(n_b):
                if b in for_dve:
                    sp.wait_ge(normed_dve, b // 2 + 1)
                else:
                    sp.wait_ge(normed_act, b // 2 + 1)
                first, last = b * NB, min((b + 1) * NB, full)
                if last > first:
                    sp.dma_start(out[first * P:last * P, :].rearrange("(c p) d -> p c d", p=P),
                                 m["x2"][:, first:last, :]).then_inc(out_ok, 16)
                    stores += 1
            if rest:
                sp.dma_start(out[full * P:sh.N, :], m["x2"][0:rest, full, :]).then_inc(out_ok, 16)
                stores += 1
            sp.wait_ge(out_ok, 16 * stores)


def build(nc, a, out, n_nodes, n_groups):
    sh = Shape(n_nodes, n_groups)
    NT = sh.NT
    with ExitStack() as ctx:
        def sb(name, shape, dt=F32):
            return ctx.enter_context(nc.sbuf_tensor(name, shape, dt))

        def dram(name, shape, dt=F32):
            return nc.dram_tensor(name, shape, dt, kind="Internal").ap()

        m = {
            "sems": {}, "ident": sb("ident", [P, P]), "iota": sb("iota", [P, WIN]),
            "w1c": sb("w1c", [P, H]), "wtab": sb("wtab", [P, TV]), "btab": sb("btab", [P, TV]),
            "wm": sb("wm", [P, QK, TV]), "w2u": sb("w2u", [P, 3, D]), "wu": sb("wu", [P, 2, D]),
            "wc": sb("wc", [P, 2, D]), "colc": sb("colc", [P, 2, 3]),
            "b1b": sb("b1b", [P, H]), "g1b": sb("g1b", [P, H]), "be1b": sb("be1b", [P, H]),
            "bub": sb("bub", [P, D]), "gub": sb("gub", [P, D]), "beub": sb("beub", [P, D]),
            "place_first": sb("place_first", [P, sh.G, TG]), "place": sb("place", [P, sh.G * TG]),
            "low_first": sb("low_first", [1, sh.G], I32), "low": sb("low", [1, sh.G], I32),
            "rounds": sb("rounds", [1, 1], I32), "deg": sb("deg", [P, NT]), "dinv": sb("dinv", [P, NT]),
            "zeros": sb("zeros", [P, 4 * HC]),
            "gain": sb("gain", [P, 1]), "shift": sb("shift", [P, 1]),
            "low_dram": dram("low_dram", [sh.G], I32), "need_dram": dram("need_dram", [sh.G], I32),
            "table": dram("table", [sh.NP, TR]),
            "conv_table": [dram(f"conv_table{j}", [sh.NP, D]) for j in range(2)],
            "acc": [dram(f"acc{j}", [sh.ACC, HC if j == 0 else D]) for j in range(3)],
        }
        gathered = semaphores(nc, m, "all", [f"gathered{n}" for n in range(RING * TG)])
        m["went"] = semaphores(nc, m, "all", ["pool_went", "act_went", "sp_went"])
        m["gathered"] = [gathered[k * TG:(k + 1) * TG] for k in range(RING)]
        m["loaded_conv"], m["loaded_x"], m["acc_zeroed"] = semaphores(nc, m, "all", [
            "loaded_conv", "loaded_x", "acc_zeroed"])
        prepare(nc, sh, a, m)
        node_table(nc, sh, a, m)
        rounds_of(nc, sh, m, lambda: message_pass(nc, sh, a, m))
        m["x2"] = sb("x2", [P, NT, D])
        with ExitStack() as uctx:
            for n, shape in (("u", [P, NT, D]), ("u_st", [P, NT, 6]), ("u_mv", [P, 2, NT]), ("u_rs", [P, NT]),
                             ("u_tmp", [P, 3, NT])):
                m[n] = uctx.enter_context(nc.sbuf_tensor(n, shape, F32))
            node_update(nc, sh, a, m)
            clear(nc, conv_table(nc, sh, m, 0))
        m["cols"] = sb("cols", [P, sh.NP])
        rounds_of(nc, sh, m, lambda: conv_pass(nc, sh, a, m, 0))
        clear(nc, batch_norm(nc, sh, m, 0))
        conv_table(nc, sh, m, 1)
        rounds_of(nc, sh, m, lambda: conv_pass(nc, sh, a, m, 1))
        batch_norm(nc, sh, m, 1)
        last_norm(nc, sh, m, out)


def lay_out(x, src, dst, edge_attr):
    import numpy as np
    n, e = x.shape[0], src.shape[0]
    nt = -(-n // P)
    g = RING * -(-e // (GE * RING))
    pad = g * GE - e
    src = np.concatenate([src, np.zeros(pad, src.dtype)])
    dst = np.concatenate([dst, np.full(pad, n, dst.dtype)])
    ea = np.concatenate([edge_attr, np.zeros((pad, ED), edge_attr.dtype)])
    xp = np.concatenate([x, np.zeros((nt * P - n, D), x.dtype)])
    c = np.ascontiguousarray
    return g, {
        "in_src": c(src.reshape(g * P, TG)),
        "in_dst_rows": c(dst.reshape(g // RING, RING, GE)),
        "in_dst_cols": c(dst.reshape(g, P, TG).transpose(1, 0, 2)),
        "in_ea_n": c(ea.reshape(g * P, TG * ED)),
        "in_ea_t": c(ea.reshape(g, P, TG // QK, QK, ED).transpose(0, 3, 4, 2, 1).reshape(g * P, TG // QK * P)),
        "in_xt": c(xp.T),
        "in_x_rows": c(xp.reshape(nt, P, D).transpose(1, 0, 2)),
    }


_WEIGHTS = ["L0_gnn_W1", "L0_gnn_b1", "L0_gnn_g1", "L0_gnn_be1", "L0_gnn_W2", "L0_gnn_b2", "L0_gnn_Wu", "L0_gnn_bu",
            "L0_gnn_gu", "L0_gnn_beu", "L1_gnn_W0", "L1_gnn_b0", "L1_gnn_g0", "L1_gnn_be0", "L1_gnn_W1", "L1_gnn_b1",
            "L1_gnn_g1", "L1_gnn_be1"]


def kernel(x, src, dst, edge_attr_32, **weights):
    import numpy as np
    import concourse.bacc as bacc
    from concourse.bass_utils import run_bass_kernel_spmd

    g, arrays = lay_out(np.asarray(x), np.asarray(src), np.asarray(dst), np.asarray(edge_attr_32))
    for w in _WEIGHTS:
        arrays[f"in_{w}"] = np.ascontiguousarray(np.asarray(weights[w]))
    nc = bacc.Bacc("TRN2", target_bir_lowering=False, num_devices=1)
    t = {n: nc.dram_tensor(n, v.shape, mybir.dt.from_np(v.dtype), kind="ExternalInput").ap()
         for n, v in arrays.items()}
    a = {k: t[f"in_{k}"] for k in ("src", "dst_rows", "dst_cols", "ea_n", "ea_t", "xt", "x_rows")}
    a.update({k: t[f"in_L0_gnn_{k}"] for k in ("W1", "b1", "g1", "be1", "W2", "b2", "Wu", "bu", "gu", "beu")})
    a["Wc"] = [t["in_L1_gnn_W0"], t["in_L1_gnn_W1"]]
    a["colc"] = [[t[f"in_L1_gnn_{r}{j}"] for r in ("b", "g", "be")] for j in range(2)]
    out = nc.dram_tensor("out", [x.shape[0], D], F32, kind="ExternalOutput").ap()
    build(nc, a, out, x.shape[0], g)
    r = run_bass_kernel_spmd(nc, [arrays], core_ids=[0])
    return r.results[0]["out"]
```
